# Optimizing a Trainium2 kernel written in Bass

```python
import numpy as np
import jax
import jax.numpy as jnp

def _softmax(x, axis=-1):
    return jax.nn.softmax(x, axis=axis)

def _gelu(x):
    return jax.nn.gelu(x, approximate=True)

def _silu(x):
    return jax.nn.silu(x)

def _sigmoid(x):
    return jax.nn.sigmoid(x)

def _layernorm(x, axis=-1, eps=1e-05):
    m = jnp.mean(x, axis=axis, keepdims=True)
    v = jnp.var(x, axis=axis, keepdims=True)
    return (x - m) / jnp.sqrt(v + eps)

def _scatter_add(tgt, idx, src, axis=0):
    return tgt.at[idx].add(src)

def _segment_sum(src, seg, n):
    return jax.ops.segment_sum(src, seg, n)
kernel_name = 'mk_adaln_d2_jaxref_r8_28c836'

def setup_inputs(seed: int=0):
    np.random.seed(seed)
    _w = jnp.asarray

    def _L0_attn_setup():
        import jax, jax.numpy as jnp
        import numpy as np
        B, T, C = (2, 256, 128)
        NHEADS = 16
        HEAD_DIM = C // NHEADS
        THETA = 10000.0
        SCALE_BASE = 512.0
        GN_EPS = 1e-05

        def _rotate_half(x):
            x1 = x[..., 0::2]
            x2 = x[..., 1::2]
            return jnp.stack([-x2, x1], axis=-1).reshape(x.shape)

        def _rope_xpos(q, k, T):
            d = q.shape[-1]
            half = jnp.arange(0, d, 2, dtype=jnp.float32)
            inv_freq = 1.0 / THETA ** (half / d)
            t = jnp.arange(T, dtype=jnp.float32)
            freqs = t[:, None] * inv_freq[None, :]
            freqs = jnp.repeat(freqs, 2, axis=-1)
            scale_vec = (half + 0.4 * d) / (1.4 * d)
            power = (t - T // 2) / SCALE_BASE
            scale = scale_vec[None, :] ** power[:, None]
            scale = jnp.repeat(scale, 2, axis=-1)
            cos, sin = (jnp.cos(freqs), jnp.sin(freqs))
            q = q * (cos * scale) + _rotate_half(q) * (sin * scale)
            k = k * (cos / scale) + _rotate_half(k) * (sin / scale)
            return (q, k)

        def _decay_mask(T):
            gamma = 1.0 - 2.0 ** (-5.0 - jnp.arange(NHEADS, dtype=jnp.float32))
            idx = jnp.arange(T)
            diff = idx[:, None] - idx[None, :]
            causal = diff >= 0
            expn = jnp.where(causal, diff, 0).astype(jnp.float32)
            return jnp.where(causal[None], gamma[:, None, None] ** expn[None], 0.0)
        key = jax.random.key(seed)
        ks = jax.random.split(key, 4)
        s = 0.02
        return {'x': jax.random.normal(ks[0], (B, T, C), jnp.float32), 'w_qkv': jax.random.normal(ks[1], (3 * C, C), jnp.float32) * s, 'w_gated': jax.random.normal(ks[2], (C, C), jnp.float32) * s, 'w_proj': jax.random.normal(ks[3], (C, C), jnp.float32) * s, 'gn_weight': jnp.ones((C,), jnp.float32), 'gn_bias': jnp.zeros((C,), jnp.float32)}
    _L0_attn_in = _L0_attn_setup()

    def _L0_ffn_setup():
        import jax, jax.numpy as jnp
        import numpy as np
        D_MODEL, D_FF, N_EXPERTS, TOP_K = (128, 512, 8, 2)
        key = jax.random.key(seed)
        k0, k1, k2, k3 = jax.random.split(key, 4)
        x = jax.random.normal(k0, (2, 256, D_MODEL), dtype=jnp.float32)
        Wg = jax.random.normal(k1, (D_MODEL, N_EXPERTS), dtype=jnp.float32) * 0.02
        W1 = jax.random.normal(k2, (N_EXPERTS, D_MODEL, D_FF), dtype=jnp.float32) * 0.02
        b1 = jnp.zeros((N_EXPERTS, D_FF), dtype=jnp.float32)
        W2 = jax.random.normal(k3, (N_EXPERTS, D_FF, D_MODEL), dtype=jnp.float32) * 0.02
        b2 = jnp.zeros((N_EXPERTS, D_MODEL), dtype=jnp.float32)
        return {'x': x, 'Wg': Wg, 'W1': W1, 'b1': b1, 'W2': W2, 'b2': b2}
    _L0_ffn_in = _L0_ffn_setup()
    _L0_c = _w((lambda *s: np.random.randn(*s).astype(np.float32) * 0.05)(8, 128))
    _L0_wmod = _w((lambda *s: np.random.randn(*s).astype(np.float32) * 0.05)(128, 6 * 128) * 128 ** (-0.5))

    def _L1_attn_setup():
        import jax, jax.numpy as jnp
        import numpy as np
        D_MODEL = 128
        NUM_HEADS = 16
        HEAD_DIM = D_MODEL // NUM_HEADS
        CHUNK = 256
        BATCH = 1
        SEQ = 1024
        key = jax.random.key(seed)
        ks = jax.random.split(key, 5)
        hidden_states = jax.random.normal(ks[0], (BATCH, SEQ, D_MODEL), dtype=jnp.float32)
        scale = 0.02
        Wq = jax.random.normal(ks[1], (D_MODEL, D_MODEL), dtype=jnp.float32) * scale
        Wk = jax.random.normal(ks[2], (D_MODEL, D_MODEL), dtype=jnp.float32) * scale
        Wv = jax.random.normal(ks[3], (D_MODEL, D_MODEL), dtype=jnp.float32) * scale
        Wo = jax.random.normal(ks[4], (D_MODEL, D_MODEL), dtype=jnp.float32) * scale
        return {'hidden_states': hidden_states, 'Wq': Wq, 'Wk': Wk, 'Wv': Wv, 'Wo': Wo}
    _L1_attn_in = _L1_attn_setup()

    def _L1_ffn_setup():
        import jax, jax.numpy as jnp
        import numpy as np
        TOP_K = 2
        NUM_EXPERTS = 8
        B, T, H, F = (4, 256, 128, 512)
        key = jax.random.key(seed)
        ks = jax.random.split(key, 6)
        s_in = 1.0 / np.sqrt(H)
        s_ff = 1.0 / np.sqrt(F)
        return {'x': jax.random.normal(ks[0], (B, T, H), dtype=jnp.float32), 'router_w': jax.random.normal(ks[1], (NUM_EXPERTS, H), dtype=jnp.float32) * s_in, 'router_b': jax.random.normal(ks[2], (NUM_EXPERTS,), dtype=jnp.float32) * 0.01, 'gate_w': jax.random.normal(ks[3], (NUM_EXPERTS, F, H), dtype=jnp.float32) * s_in, 'up_w': jax.random.normal(ks[4], (NUM_EXPERTS, F, H), dtype=jnp.float32) * s_in, 'down_w': jax.random.normal(ks[5], (NUM_EXPERTS, H, F), dtype=jnp.float32) * s_ff}
    _L1_ffn_in = _L1_ffn_setup()
    _L1_c = _w((lambda *s: np.random.randn(*s).astype(np.float32) * 0.05)(8, 128))
    _L1_wmod = _w((lambda *s: np.random.randn(*s).astype(np.float32) * 0.05)(128, 6 * 128) * 128 ** (-0.5))
    _d = {'L0_attn_x': _L0_attn_in['x'], 'L0_attn_w_qkv': _L0_attn_in['w_qkv'], 'L0_attn_w_gated': _L0_attn_in['w_gated'], 'L0_attn_w_proj': _L0_attn_in['w_proj'], 'L0_attn_gn_weight': _L0_attn_in['gn_weight'], 'L0_attn_gn_bias': _L0_attn_in['gn_bias'], 'L0_ffn_Wg': _L0_ffn_in['Wg'], 'L0_ffn_W1': _L0_ffn_in['W1'], 'L0_ffn_b1': _L0_ffn_in['b1'], 'L0_ffn_W2': _L0_ffn_in['W2'], 'L0_ffn_b2': _L0_ffn_in['b2'], 'L0_c': _L0_c, 'L0_wmod': _L0_wmod, 'L1_attn_Wq': _L1_attn_in['Wq'], 'L1_attn_Wk': _L1_attn_in['Wk'], 'L1_attn_Wv': _L1_attn_in['Wv'], 'L1_attn_Wo': _L1_attn_in['Wo'], 'L1_ffn_router_w': _L1_ffn_in['router_w'], 'L1_ffn_router_b': _L1_ffn_in['router_b'], 'L1_ffn_gate_w': _L1_ffn_in['gate_w'], 'L1_ffn_up_w': _L1_ffn_in['up_w'], 'L1_ffn_down_w': _L1_ffn_in['down_w'], 'L1_c': _L1_c, 'L1_wmod': _L1_wmod}
    _x0 = _d['L0_attn_x']
    _d['L0_attn_x'] = jax.random.normal(jax.random.fold_in(jax.random.key(seed), 1), (8, 256, 128), dtype=_x0.dtype)
    del _x0
    return _d

def reference(L0_attn_x, L0_attn_w_qkv, L0_attn_w_gated, L0_attn_w_proj, L0_attn_gn_weight, L0_attn_gn_bias, L0_ffn_Wg, L0_ffn_W1, L0_ffn_b1, L0_ffn_W2, L0_ffn_b2, L0_c, L0_wmod, L1_attn_Wq, L1_attn_Wk, L1_attn_Wv, L1_attn_Wo, L1_ffn_router_w, L1_ffn_router_b, L1_ffn_gate_w, L1_ffn_up_w, L1_ffn_down_w, L1_c, L1_wmod):

    def _L0_attn_ref(x, w_qkv, w_gated, w_proj, gn_weight, gn_bias):
        import jax, jax.numpy as jnp
        import numpy as np
        B, T, C = (2, 256, 128)
        NHEADS = 16
        HEAD_DIM = C // NHEADS
        THETA = 10000.0
        SCALE_BASE = 512.0
        GN_EPS = 1e-05

        def _rotate_half(x):
            x1 = x[..., 0::2]
            x2 = x[..., 1::2]
            return jnp.stack([-x2, x1], axis=-1).reshape(x.shape)

        def _rope_xpos(q, k, T):
            d = q.shape[-1]
            half = jnp.arange(0, d, 2, dtype=jnp.float32)
            inv_freq = 1.0 / THETA ** (half / d)
            t = jnp.arange(T, dtype=jnp.float32)
            freqs = t[:, None] * inv_freq[None, :]
            freqs = jnp.repeat(freqs, 2, axis=-1)
            scale_vec = (half + 0.4 * d) / (1.4 * d)
            power = (t - T // 2) / SCALE_BASE
            scale = scale_vec[None, :] ** power[:, None]
            scale = jnp.repeat(scale, 2, axis=-1)
            cos, sin = (jnp.cos(freqs), jnp.sin(freqs))
            q = q * (cos * scale) + _rotate_half(q) * (sin * scale)
            k = k * (cos / scale) + _rotate_half(k) * (sin / scale)
            return (q, k)

        def _decay_mask(T):
            gamma = 1.0 - 2.0 ** (-5.0 - jnp.arange(NHEADS, dtype=jnp.float32))
            idx = jnp.arange(T)
            diff = idx[:, None] - idx[None, :]
            causal = diff >= 0
            expn = jnp.where(causal, diff, 0).astype(jnp.float32)
            return jnp.where(causal[None], gamma[:, None, None] ** expn[None], 0.0)
        Bx, Tx, Cx = x.shape
        qkv = x @ w_qkv.T
        q, k, v = jnp.split(qkv, 3, axis=-1)

        def to_heads(u):
            return u.reshape(Bx, Tx, NHEADS, HEAD_DIM).transpose(0, 2, 1, 3)
        q, k, v = (to_heads(q), to_heads(k), to_heads(v))
        q, k = _rope_xpos(q, k, Tx)
        mask = _decay_mask(Tx)
        scores = jnp.einsum('bhtd,bhsd->bhts', q, k) * HEAD_DIM ** (-0.5)
        scores = scores * mask[None]
        y = jnp.einsum('bhts,bhsd->bhtd', scores, v)
        y = y.transpose(0, 2, 1, 3).reshape(Bx, Tx, Cx)
        yt = y.transpose(0, 2, 1).reshape(Bx, NHEADS, HEAD_DIM, Tx)
        mean = yt.mean(axis=(2, 3), keepdims=True)
        var = yt.var(axis=(2, 3), keepdims=True)
        yn = (yt - mean) / jnp.sqrt(var + GN_EPS)
        yn = yn.reshape(Bx, Cx, Tx)
        yn = yn * gn_weight[None, :, None] + gn_bias[None, :, None]
        yn = yn.transpose(0, 2, 1)
        out = jax.nn.silu(x @ w_gated.T) * yn
        return out @ w_proj.T

    def _L0_ffn_ref(x, Wg, W1, b1, W2, b2):
        import jax, jax.numpy as jnp
        import numpy as np
        D_MODEL, D_FF, N_EXPERTS, TOP_K = (128, 512, 8, 2)
        B = x.shape[:-1]
        xs = x.reshape(-1, x.shape[-1])
        T = xs.shape[0]
        gate_logits = xs @ Wg
        weights, sel = jax.lax.top_k(gate_logits, TOP_K)
        weights = jax.nn.softmax(weights.astype(jnp.float32), axis=1).astype(x.dtype)
        h = jax.nn.relu(jnp.einsum('td,edf->etf', xs, W1) + b1[:, None, :])
        out_e = jnp.einsum('etf,efd->etd', h, W2) + b2[:, None, :]
        tok = jnp.arange(T)
        picked = out_e[sel, tok[:, None]]
        out = jnp.einsum('tk,tkd->td', weights, picked)
        return out.reshape(*B, x.shape[-1])

    def _L1_attn_ref(hidden_states, Wq, Wk, Wv, Wo):
        import jax, jax.numpy as jnp
        import numpy as np
        D_MODEL = 128
        NUM_HEADS = 16
        HEAD_DIM = D_MODEL // NUM_HEADS
        CHUNK = 256
        BATCH = 1
        SEQ = 1024
        B, S, D = hidden_states.shape
        H, hd, C = (NUM_HEADS, HEAD_DIM, CHUNK)
        Nc = S // C

        def split_heads(x):
            return x.reshape(B, S, H, hd).transpose(0, 2, 1, 3).reshape(B, H, Nc, C, hd)
        q = split_heads(hidden_states @ Wq.T)
        k = split_heads(hidden_states @ Wk.T)
        v = split_heads(hidden_states @ Wv.T)
        scores = jnp.einsum('bhnqd,bhnkd->bhnqk', q, k) / np.sqrt(hd).astype(jnp.float32)
        causal = jnp.tril(jnp.ones((C, C), dtype=bool))
        scores = jnp.where(causal, scores, -jnp.inf)
        attn = jax.nn.softmax(scores, axis=-1)
        out = jnp.einsum('bhnqk,bhnkd->bhnqd', attn, v)
        out = out.reshape(B, H, S, hd).transpose(0, 2, 1, 3).reshape(B, S, D)
        return out @ Wo.T

    def _L1_ffn_ref(x, router_w, router_b, gate_w, up_w, down_w):
        import jax, jax.numpy as jnp
        import numpy as np
        TOP_K = 2
        NUM_EXPERTS = 8
        B, T, H, F = (4, 256, 128, 512)
        logits = jnp.einsum('bth,eh->bte', x, router_w) + router_b
        topv, topi = jax.lax.top_k(logits, TOP_K)
        gates = jax.nn.softmax(topv, axis=-1)

        def body(acc, inputs):
            e, gw, uw, dw = inputs
            w = jnp.sum(gates * (topi == e), axis=-1)
            h = jax.nn.silu(jnp.einsum('bth,fh->btf', x, gw)) * jnp.einsum('bth,fh->btf', x, uw)
            y = jnp.einsum('btf,hf->bth', h, dw)
            return (acc + y * w[..., None], None)
        init = jnp.zeros_like(x)
        xs = (jnp.arange(NUM_EXPERTS), gate_w, up_w, down_w)
        out, _ = jax.lax.scan(body, init, xs)
        return out
    x = L0_attn_x
    mod = (_silu(L0_c) @ L0_wmod).reshape(L0_c.shape[0], 6, 1, -1)
    sa, ca, ga, sb, cb, gb = (mod[:, 0], mod[:, 1], mod[:, 2], mod[:, 3], mod[:, 4], mod[:, 5])
    ga = (2 * (ga >= 0) - 1) * jnp.maximum(jnp.abs(ga), 0.25)
    gb = (2 * (gb >= 0) - 1) * jnp.maximum(jnp.abs(gb), 0.25)
    h = _layernorm(x, axis=-1) * (1 + ca) + sa
    x = x + ga * _L0_attn_ref(h, L0_attn_w_qkv, L0_attn_w_gated, L0_attn_w_proj, L0_attn_gn_weight, L0_attn_gn_bias)
    h = _layernorm(x, axis=-1) * (1 + cb) + sb
    x = x + gb * _L0_ffn_ref(h, L0_ffn_Wg, L0_ffn_W1, L0_ffn_b1, L0_ffn_W2, L0_ffn_b2)
    mod = (_silu(L1_c) @ L1_wmod).reshape(L1_c.shape[0], 6, 1, -1)
    sa, ca, ga, sb, cb, gb = (mod[:, 0], mod[:, 1], mod[:, 2], mod[:, 3], mod[:, 4], mod[:, 5])
    ga = (2 * (ga >= 0) - 1) * jnp.maximum(jnp.abs(ga), 0.25)
    gb = (2 * (gb >= 0) - 1) * jnp.maximum(jnp.abs(gb), 0.25)
    h = _layernorm(x, axis=-1) * (1 + ca) + sa
    x = x + ga * _L1_attn_ref(h, L1_attn_Wq, L1_attn_Wk, L1_attn_Wv, L1_attn_Wo)
    h = _layernorm(x, axis=-1) * (1 + cb) + sb
    x = x + gb * _L1_ffn_ref(h, L1_ffn_router_w, L1_ffn_router_b, L1_ffn_gate_w, L1_ffn_up_w, L1_ffn_down_w)
    return x

_drawn_inputs = setup_inputs


def setup_inputs(seed=0):
    import zlib

    import numpy as np

    out = dict(_drawn_inputs(seed))
    spreads = {'L0_attn_gn_weight': (1.0, 0.6),
     'L0_attn_gn_bias': (0.0, 0.8),
     'L0_ffn_b1': (0.0, 0.8),
     'L0_ffn_b2': (0.0, 0.388)}
    factors = {'L0_attn_w_qkv': 6.275,
     'L0_attn_w_gated': 6.124,
     'L0_attn_w_proj': 5.859,
     'L0_ffn_W1': 4.225,
     'L0_ffn_W2': 3.42,
     'L1_attn_Wq': 8.0,
     'L1_attn_Wk': 8.0,
     'L1_attn_Wv': 8.0,
     'L1_attn_Wo': 8.0,
     'L1_ffn_router_b': 27.988}
    for name, (base, spread) in spreads.items():
        noise = np.random.default_rng([zlib.crc32(name.encode()), seed]).standard_normal(out[name].shape)
        drawn = base * np.exp(spread * noise) if base else spread * noise
        out[name] = jnp.asarray(drawn.astype(out[name].dtype))
    for name, factor in factors.items():
        out[name] = (out[name] * factor).astype(out[name].dtype)
    return out
```

```python
from contextlib import ExitStack

import numpy as np

import concourse.bass as bass
from concourse import mybir

F32 = mybir.dt.float32
BF16 = mybir.dt.bfloat16
I32 = mybir.dt.int32
U32 = mybir.dt.uint32
ALU = mybir.AluOpType
ACT = mybir.ActivationFunctionType
AX_X = mybir.AxisListType.X

P = 128
NB, T, C = 8, 256, 128
H, HD = 16, 8
E, F = 8, 512
TOK = NB * T
NT = TOK // P
KT = T // P
FK = F // P
CHOICES = 2
TILES = (CHOICES * TOK + E * (P - 1)) // P
RING = 4
PEEL = TILES % RING + RING
TURNS = (TILES - PEEL) // RING - 1
EPS = 1e-5
FLOOR = 0.25
BIG = 3.0e38
PARTS = 3
MAX_ROW = 96
STACKS = 4

CONST_COLS = [("ident", P), ("causal", P), ("same_head", P),
              ("head_avg", P), ("before", P), ("iota", P), ("expert_id", P), ("restart", P),
              ("steps128", 16), ("trash", TILES), ("tile_id", 32), ("pid1", 1)]
CONST_AT, _o = {}, 0
for _n, _w in CONST_COLS:
    CONST_AT[_n] = (_o, _o + _w)
    _o += _w
CONST_N = _o
D_MAJOR = np.arange(C).reshape(H, HD).T.reshape(-1)


def shape_constants():
    out = np.zeros((P, CONST_N), np.float64)
    rotary = np.zeros((2, P, 2 * T), np.float64)

    def put(name, value):
        a, b = CONST_AT[name]
        out[:, a:b] = value

    p = np.arange(P)
    d, h = p // H, p % H
    half = np.arange(0, HD, 2)
    inv_freq = 1.0 / 10000.0 ** (half / HD)
    t = np.arange(T)
    angle = t[None, :] * inv_freq[d // 2][:, None]
    scale = ((half + 0.4 * HD) / (1.4 * HD))[d // 2][:, None] ** ((t - T // 2) / 512.0)[None, :]
    gamma = (1.0 - 2.0 ** (-5.0 - h))[:, None]
    q_side = scale * gamma ** (t - P)[None, :] * HD ** -0.5
    k_side = gamma ** (P - t)[None, :] / scale
    sign = np.where(d % 2 == 0, -1.0, 1.0)[:, None]
    rotary[0] = np.concatenate([np.cos(angle) * q_side, np.cos(angle) * k_side], 1)
    rotary[1] = np.concatenate([sign * np.sin(angle) * q_side, sign * np.sin(angle) * k_side], 1)
    put("ident", np.eye(P))
    put("causal", p[:, None] <= p[None, :])
    put("same_head", h[:, None] == h[None, :])
    put("head_avg", (h[:, None] == h[None, :]) / HD)
    put("before", p[:, None] < p[None, :])
    put("iota", p[None, :])
    put("expert_id", (p // NT)[None, :])
    put("restart", (p % NT != 0)[None, :])
    put("steps128", (P * np.arange(16))[None, :])
    put("trash", CHOICES * TOK + 1 + P * np.arange(TILES)[None, :] + p[:, None])
    put("tile_id", np.arange(2 * NT)[None, :])
    put("pid1", (p + 1)[:, None])
    return out.astype(np.float32), rotary.astype(np.float32)


LAYER0_TOTAL = {
    **dict.fromkeys(("x_t_ps", "h_t", "v_ps", "x_mid", "out_ps", "mod_ps", "mod_bc", "mod_bc_half", "w_out", "o_t", "h_mul",
                     "h2_ps", "h2_t", "logits_ps", "logits", "qk_ps", "part1_", "rest1_", "part2_", "part3_", "var", "rstd",
                     "mix3_", "mixed_x"), NB),
    **dict.fromkeys(("stats", "mv", "xh", "h_tok", "y_pad", "mix1_", "mixed"), 2 * NB),
    **dict.fromkeys(("x_t", "x_t_e_ps", "hidden_ps", "w_now", "hid_t", "y_ps", "y_rows"), TILES),
    **{f"{way}{r}": 16 * ((TILES - r + RING - 1) // RING) for way in ("gathered", "scattered") for r in range(RING)},
    **dict.fromkeys(("ranks_ps", "counts_ps", "total_b", "picked_b", "tiles_before_b", "src_row", "dst_row", "tile_exp",
                     "gap", "gap_exp", "weights"), 1),
    "slot_ps": CHOICES * NT, "hot_lane": CHOICES * NT, "hot_vals": 2, "diag": 4 * NB,
    "h_stored": 16 * NB // 2, "parts_out": 96 * NB // 2, "stacked": 96 * NB // 2, "pair_in": 32 * NB // 2,
    "y_out": 128 * NB // 2, "y_in": 16 * NB // 2,
}


def exists(n):
    return not isinstance(n, int) or 0 <= n < TILES


def all_tiles(eng, step):
    for n in range(PEEL):
        step(n, n % RING, n // RING)
    with eng.Fori(0, TURNS) as i:
        for u in range(PEEL, PEEL + RING):
            step(i * RING + u, u % RING, i + u // RING)
    for n in range(TILES - RING, TILES):
        step(n, n % RING, n // RING)


def split_layer(name):
    for at in (-1, -3):
        for base in (name[:at], name[:at - 1]):
            if base in LAYER0_TOTAL and name[at] in "01":
                return base, int(name[at]), name[at:][1:]
    return name, 0, ""


class Named(dict):

    def __init__(self, make):
        super().__init__()
        self.make = make

    def __missing__(self, name):
        self[name] = self.make(name)
        return self[name]


def at_least(eng, sem, count, base=0):
    if not isinstance(count, int) or count > 0:
        eng.wait_ge(sem, count + base)


def cnt(b):
    return max(0, min(b + 1, NB))


def adaln_layers(nc, ins, out):
    ctx = ExitStack()
    with ctx:
        def sb(name, shape, dt=F32):
            return ctx.enter_context(nc.sbuf_tensor(name, [P] + shape, dt))

        def dram(name, shape, dt=F32):
            return nc.dram_tensor(name, shape, dt, kind="Internal").ap()

        handle = Named(lambda name: ctx.enter_context(nc.semaphore(name)))
        sem = Named(lambda name: handle["%s%s" % split_layer(name)[::2]])
        base = Named(lambda name: LAYER0_TOTAL[split_layer(name)[0]] * split_layer(name)[1]
                     if split_layer(name)[0] in LAYER0_TOTAL else 0)

        X = sb("X", [NT, C])
        consts = sb("consts", [CONST_N])
        c_t = sb("c_t", [2, NB])
        sc_t = sb("sc_t", [2, NB])
        mod_t = sb("mod_t", [2, 6, NB])
        ones = sb("ones", [P])
        ones_b = sb("ones_b", [P], BF16)
        before_b = sb("before_b", [P], BF16)
        iota_b = sb("iota_b", [P], BF16)
        ident_b = sb("ident_b", [P], BF16)
        half_neg = sb("half_neg", [2])
        w_qk = sb("w_qk", [2 * C])
        w_v = sb("w_v", [C])
        w_proj = sb("w_proj", [C])
        gn = sb("gn", [2])
        router_w = sb("router_w", [2, E])
        router_b = sb("router_b", [E])
        W1 = sb("W1", [E, F])
        W_up = sb("W_up", [E, F])
        B1 = sb("B1", [E, FK])
        b_now = sb("b_now", [2, FK])
        W2 = sb("W2", [E, FK, C])

        stats = sb("stats", [2, KT, 6])
        mv = sb("mv", [2, KT, 2])
        var_eps = sb("var_eps", [2, KT])
        rstd = sb("rstd", [2, KT])
        xh = sb("xh", [2, 2, KT, C])
        h_t = sb("h_t", [2, T])
        h_tok = sb("h_tok", [2, KT, C])
        h2_t = sb("h2_t", [T])
        rot = sb("rot", [2, 2 * T])
        qk = sb("qk", [3, 2 * T])
        rest = sb("rest", [2, 2 * T])
        parts = sb("parts", [2, PARTS, 2 * T], BF16)
        stack_q = sb("stack_q", [STACKS, H * T], BF16)
        stack_k = sb("stack_k", [STACKS, H * T], BF16)
        V = sb("V", [4, KT, H * 9 + 24])
        probs = sb("probs", [4, 512])
        y_pad = sb("y_pad", [2, 4 * T])
        y_t = sb("y_t", [3, T])
        gn_stats = sb("gn_stats", [6])
        gn_mv = sb("gn_mv", [2])
        gn_avg = sb("gn_avg", [2])
        gn_ve = sb("gn_ve", [2])
        gn_rstd = sb("gn_rstd", [1])
        gn_ab = sb("gn_ab", [2])
        y_n = sb("y_n", [T])
        o_t = sb("o_t", [2, T])
        diag = sb("diag", [4, C])
        mod_bc = sb("mod_bc", [4, 3 * C])
        gb_bc = sb("gb_bc", [NB, C])
        w_out = sb("w_out", [2, C])
        row_max = sb("row_max", [KT, H])
        max_parts = sb("max_parts", [2, KT, 2 * H], BF16)
        den = sb("den", [2, 2 * H])
        den_inv = sb("den_inv", [2, 2 * H])

        logits = sb("logits", [E, NT])
        r_max = sb("r_max", [NT])
        r_min = sb("r_min", [NT])
        r_max2 = sb("r_max2", [NT])
        gap = sb("gap", [NT])
        gap_exp = sb("gap_exp", [NT])
        gap_den = sb("gap_den", [NT])
        weight = sb("weight", [CHOICES, NT])
        picked_b = sb("picked_b", [E, NT], BF16)
        tiles_before_b = sb("tiles_before_b", [E, NT], BF16)
        total_b = sb("total_b", [E], BF16)
        over = sb("over", [E, 16])
        n_tiles = sb("n_tiles", [E])
        tile_end = sb("tile_end", [E])
        tile_start = sb("tile_start", [E])
        slot = sb("slot", [CHOICES * NT])
        slot_i = sb("slot_i", [CHOICES * NT], I32)
        tile_i = sb("tile_i", [CHOICES * NT], I32)
        lane_i = sb("lane_i", [CHOICES * NT], I32)
        slot_tile = sb("slot_tile", [CHOICES * NT])
        slot_lane = sb("slot_lane", [CHOICES * NT])
        tile_exp_f = sb("tile_exp_f", [TILES])
        tile_exp = sb("tile_exp", [TILES], I32)
        ident_lo = sb("ident_lo", [TILES])
        ident_all = sb("ident_all", [TILES])
        empty = sb("empty", [TILES])
        empty_at = sb("empty_at", [TILES])
        wrap = sb("wrap", [TILES])
        src_f = sb("src_f", [TILES])
        src_row = sb("src_row", [TILES], U32)
        dst_row = sb("dst_row", [TILES], U32)

        h_tmp = sb("h_tmp", [KT, C])
        gate_tmp = sb("gate_tmp", [2 * CHOICES, 3, NB])
        neg_mask = sb("neg_mask", [P], BF16)

        def guests(host, host_dt, layout):
            axes = "abcd"[:len(host.shape) - 1]
            flat = host[(slice(None),) * len(host.shape)]
            if len(axes) > 1:
                flat = flat.rearrange(f"p {' '.join(axes)} -> p ({' '.join(axes)})")
            if host_dt == BF16:
                flat = flat.bitcast(F32)
            views, at = [], 0
            for shape, dt in layout:
                words = int(np.prod(shape)) // (2 if dt == BF16 else 1)
                v = flat[:, at:at + words]
                at += words
                v = v.bitcast(dt) if dt != F32 else v
                if len(shape) > 1:
                    names = [f"n{i}" for i in range(len(shape))]
                    v = v.rearrange(f"p ({' '.join(names)}) -> p {' '.join(names)}", **dict(zip(names, shape)))
                views.append(v)
            return views

        (mod_w,) = guests(stack_q[:, STACKS - 1, :], BF16, [([2, 6 * C], F32)])
        sgate, y_state = guests(stack_q[:, STACKS - 1, :], BF16, [([6, T], F32), ([3, P], F32)])
        (w_now,) = guests(stack_q[:, STACKS - 1, :], BF16, [([2, 2, F], F32)])
        hid_t, hid_g = guests(stack_k[:, STACKS - 1, :], BF16, [([2, F], F32)] * 2)
        rotary, w_qks, w_gate, state, k_tok = guests(
            stack_k[:, STACKS - 1, :], BF16, [([2, 2 * T], F32), ([2 * C], F32), ([C], F32), ([C], F32), ([C], F32)])
        y_mix, y_mix2, y_mix3, den_bc, max_t = guests(
            qk, F32, [([KT, C], F32)] * 3 + [([2, T], F32), ([2, T], BF16)])
        (y_pair,) = guests(rot, F32, [([2, CHOICES, KT, C], F32)])
        hot_vals, hot_lane = guests(parts, BF16, [([CHOICES * NT, 2, TILES], BF16), ([4, P], BF16)])
        hot_tile, ended = guests(rest, F32, [([CHOICES * NT, TILES], BF16), ([TILES, E], F32)])
        x_rows, y_rows, x_t, r_eq, r_idx, second, picked, upto = guests(
            probs, F32, [([RING, C], F32), ([RING, C], F32), ([2, P], F32)] + [([E, NT], F32)] * 5)
        B2, pick, place, place_c = guests(y_pad, F32, [([E, C], F32), ([CHOICES, E, NT], F32)] + [([E, NT], F32)] * 2)

        bank = [ctx.enter_context(nc.psum_tensor(f"bank{i}", [P, 512], F32)) for i in range(4)]
        pair = [ctx.enter_context(nc.psum_tensor(f"pair{i}", [P, 1024], F32)) for i in range(2)]
        P0, P1, P2, Y0 = bank
        HIDDEN = P1[:, :], P2[:, :]
        UP = Y0[:, :], pair[0][:, 0:512]
        Y_ROWS = pair[0][:, 512:512 + C], pair[1][:, 0:C]

        parts_d = dram("parts_d", [2, 2, 2, PARTS * HD, H * T], BF16)
        y_d = dram("y_d", [2, 2, HD + 1, H, T])
        den_d = dram("den_d", [2, H, T])
        max_d = dram("max_d", [2, 2 * H, T], BF16)
        h_d = [dram(f"h_d{l}", [TOK, C]) for l in range(2)]
        ye_d = [dram(f"ye_d{l}", [CHOICES * TOK + TILES * P, C]) for l in range(2)]

        def const(name):
            a, b = CONST_AT[name]
            return consts[:, a:b]

        block = ctx.enter_context(nc.Block())

        def exp_cells(g):
            gp, i6 = g // 6, g % 6
            if i6 < 4:
                return [(8 * gp + 2 * i6 + n, 0, 0, T) for n in range(2)]
            return [(8 * gp + 4 * (i6 - 4) + n, P, P, P) for n in range(4)]

        def half_bank(g):
            return pair[1][:, (g % 2) * 512:(g % 2 + 1) * 512]

        LAG = {0: dict(scores=2, back=4, route=5, last=6), 1: dict(scores=1, probs=3, dens=4, back=5, route=6, last=7)}

        def stages(l, s):
            got = {"front": s, "next": s + 1} | {k: s - v for k, v in LAG[l].items()}
            got["logits"] = s - LAG[l]["route"] - 1
            return {k: (b if 0 <= b < NB else None) for k, b in got.items()}

        STEPS = {l: range(-1, NB + LAG[l]["last"]) for l in range(2)}

        @block.sync
        def _(sp):
            xv = ins["x"].rearrange("b (k p) c -> p (b k) c", p=P)
            sp.dma_start(X[:, 0:KT, :], xv[:, 0:KT, :]).then_inc(sem["x_in0"], 16)
            sp.dma_start(consts[:, :], ins["consts"]).then_inc(sem["consts_in"], 16)
            for l in range(2):
                sp.dma_start(c_t[:, l, :], ins[f"c_t{l}"]).then_inc(sem["mod_in"], 16)
                sp.dma_start(mod_w[:, l, :], ins[f"wmod{l}"]).then_inc(sem["mod_in"], 16)
            sp.dma_start(w_qk[:, :], ins["w_qk0"]).then_inc(sem["attn_in"], 16)
            sp.dma_start(w_qks[:, :], ins["w_qks"]).then_inc(sem["attn_in"], 16)
            sp.dma_start(w_v[:, :], ins["w_v0"]).then_inc(sem["attn_in"], 16)
            sp.dma_start(w_gate[:, :], ins["w_gate"]).then_inc(sem["attn_in"], 16)
            sp.dma_start(rotary[:, :, :], ins["rotary"].rearrange("a p t -> p a t")).then_inc(sem["rotary_in"], 16)
            sp.dma_start(X[:, KT:NT, :], xv[:, KT:NT, :]).then_inc(sem["x_in1"], 16)
            sp.dma_start(w_proj[:, :], ins["w_proj0"]).then_inc(sem["late_in"], 16)
            sp.dma_start(gn[:, :], ins["gn"]).then_inc(sem["late_in"], 16)
            sp.dma_start(router_w[:, 0, :], ins["router_w0"]).then_inc(sem["late_in"], 16)
            sp.dma_start(router_w[:, 1, :], ins["router_w1"]).then_inc(sem["late_in"], 16)
            sp.dma_start(router_b[:, :], ins["router_b"].rearrange("(a e) -> a e", a=1).broadcast_to((P, E)))\
              .then_inc(sem["late_in"], 16)
            def store_h(l, b):
                sp.wait_ge(sem[f"h_tok{l}"], base[f"h_tok{l}"] + 2 * (b + 1))
                sp.dma_start(h_d[l][b * T:(b + 1) * T, :].rearrange("(k p) c -> p k c", p=P), h_tok[:, b % 2])\
                  .then_inc(sem[f"h_stored{l}_{b % 2}"], 16)

            def stack_parts(l, b):
                sp.wait_ge(sem[f"part3_{l}"], base[f"part3_{l}"] + b + 1)
                d = parts_d[l, b % 2]
                at_least(sp, sem[f"stacked{l}_{b % 2}"], 96 * (b // 2), base[f"stacked{l}_{b % 2}"])
                for part in range(PARTS):
                    for side in range(2):
                        sp.dma_start(d[side, part * HD:(part + 1) * HD, :].rearrange("d (h t) -> (d h) t", t=T),
                                     parts[:, b % 2, part, side * T:(side + 1) * T])\
                          .then_inc(sem[f"parts_out{l}_{b % 2}"], 16)
                sp.wait_ge(sem[f"parts_out{l}_{b % 2}"], base[f"parts_out{l}_{b % 2}"] + 96 * (b // 2 + 1))
                if l == 0 and b == 0:
                    sp.wait_ge(sem["stack_rows"], 6)
                if l == 1 and b == STACKS - 1:
                    sp.wait_ge(sem["pool_rows"], STACKS + 2)
                if l == 0:
                    at_least(sp, sem["scores0"], 4 * cnt(b - 3))
                else:
                    at_least(sp, sem["scores_exp"], 12 * cnt(b - STACKS))
                r = b % (3 if l == 0 else STACKS)
                row = 0
                for k_part, n in ((0, 3), (1, 2), (2, 1)):
                    sp.dma_start(stack_q[row:row + n * HD, r, :], d[0, 0:n * HD, :]).then_inc(sem[f"stacked{l}_{b % 2}"], 16)
                    k_src = d[1:2, k_part * HD:(k_part + 1) * HD, :]
                    if n > 1:
                        k_src = k_src.broadcast_to((n, HD, H * T))
                    sp.dma_start(stack_k[row:row + n * HD, r, :], k_src if n > 1 else k_src[0])\
                      .then_inc(sem[f"stacked{l}_{b % 2}"], 16)
                    row += n * HD

            def unpad_y(l, b):
                sp.wait_ge(sem[f"y_pad{l}"], base[f"y_pad{l}"] + 2 * (b + 1))
                rows = HD + (l == 1)
                if l == 0:
                    at_least(sp, sem[f"y_in0_{b % 2}"], 16 * (b // 2))
                else:
                    at_least(sp, sem[f"y_in1_{b % 2}"], 32 * (b // 2), base[f"y_in1_{b % 2}"])
                for j in range(4):
                    dst = y_d[l, b % 2, 0:rows].rearrange("d (g j) t -> j d g t", j=4)[j]
                    src = y_pad[32 * j:32 * j + rows, b % 2, :]
                    if l == 0:
                        for ch in range(KT):
                            sp.dma_start(dst[:, :, ch * P:(ch + 1) * P],
                                         src[:, ch * 512:(ch + 1) * 512].rearrange("d (g t) -> d g t", g=4))\
                              .then_inc(sem[f"y_out{l}_{b % 2}"], 16)
                    else:
                        sp.dma_start(dst, src.rearrange("d (g t) -> d g t", g=4)).then_inc(sem[f"y_out{l}_{b % 2}"], 16)
                sp.wait_ge(sem[f"y_out{l}_{b % 2}"], base[f"y_out{l}_{b % 2}"] + (128 if l == 0 else 64) * (b // 2 + 1))
                at_least(sp, sem[f"o_t{l}"], cnt(b - 3), base[f"o_t{l}"])
                sp.dma_start(y_t[:, b % 3, :], y_d[l, b % 2, 0:HD].rearrange("d h t -> (d h) t"))\
                  .then_inc(sem[f"y_in{l}_{b % 2}"], 16)
                if l == 1:
                    at_least(sp, sem["den_inv"], cnt(b - 2))
                    sp.dma_start(den[:, b % 2, :], y_d[l, b % 2, HD].rearrange("h (a t) -> (h a) t", t=2 * H))\
                      .then_inc(sem[f"y_in1_{b % 2}"], 16)

            def spread_den(b):
                sp.wait_ge(sem["den_inv"], b + 1)
                at_least(sp, sem[f"den_in{b % 2}"], 16 * (b // 2))
                sp.dma_start(den_d[b % 2].rearrange("h (a t) -> (h a) t", t=2 * H), den_inv[:, b % 2, :])\
                  .then_inc(sem[f"den_out{b % 2}"], 16)
                sp.wait_ge(sem[f"den_out{b % 2}"], 16 * (b // 2 + 1))
                at_least(sp, sem["o_t1"], cnt(b - 2), base["o_t1"])
                sp.dma_start(den_bc[:, b % 2, :], den_d[b % 2:b % 2 + 1].broadcast_to((HD, H, T)))\
                  .then_inc(sem[f"den_in{b % 2}"], 16)

            def stack_max(b):
                sp.wait_ge(sem["max_t"], b + 1)
                at_least(sp, sem[f"max_in{b % 2}"], 16 * (b // 2))
                sp.dma_start(max_d[b % 2], max_t[0:2 * H, b % 2, :]).then_inc(sem[f"max_out{b % 2}"], 16)
                sp.wait_ge(sem[f"max_out{b % 2}"], 16 * (b // 2 + 1))
                sp.dma_start(stack_q[MAX_ROW:MAX_ROW + 2, b % STACKS, :], max_d[b % 2].rearrange("(r h) t -> r (h t)", r=2))\
                  .then_inc(sem[f"max_in{b % 2}"], 16)

            def load_pair(l, b):
                if b == 0:
                    for r in range(RING):
                        sp.wait_ge(sem[f"scattered{r}_{l}"],
                                   base[f"scattered{r}_{l}"] + LAYER0_TOTAL[f"scattered{r}"])
                at_least(sp, sem[f"mixed{l}"], 2 * cnt(b - 2), base[f"mixed{l}"])
                src = ye_d[l][0:CHOICES * TOK, :].rearrange("(a b k p) c -> b p a k c", a=CHOICES, k=KT, p=P)[b]
                for a in range(CHOICES):
                    sp.dma_start(y_pair[:, b % 2, a], src[:, a]).then_inc(sem[f"pair_in{l}_{b % 2}"], 16)

            for s in STEPS[0]:
                b = stages(0, s)
                if b["route"] is not None:
                    store_h(0, b["route"])
                if b["front"] is not None:
                    stack_parts(0, b["front"])
                if b["scores"] is not None:
                    unpad_y(0, b["scores"])

            sp.wait_ge(sem["v_ps0"], NB)
            sp.dma_start(w_qk[:, :], ins["w_qk1"]).then_inc(sem["w1_in"], 16)
            sp.dma_start(w_v[:, :], ins["w_v1"]).then_inc(sem["w1_in"], 16)
            sp.wait_ge(sem["w_out0"], NB)
            sp.dma_start(w_proj[:, :], ins["w_proj1"]).then_inc(sem["w1_in"], 16)

            for s in STEPS[1]:
                b = stages(1, s)
                if s == -1:
                    load_pair(0, 0)
                    load_pair(0, 1)
                elif s + 2 < NB:
                    load_pair(0, s + 2)
                if b["route"] is not None:
                    store_h(1, b["route"])
                if s - 2 >= 0 and s - 2 < NB:
                    stack_max(s - 2)
                if b["front"] is not None:
                    stack_parts(1, b["front"])
                if b["dens"] is not None:
                    spread_den(b["dens"])
                if b["probs"] is not None:
                    unpad_y(1, b["probs"])

            ov = out.rearrange("b (k p) c -> p b k c", p=P)
            for b in range(NB):
                load_pair(1, b)
                if b >= 1:
                    sp.wait_ge(sem["mixed_x1"], base["mixed_x1"] + b)
                    sp.dma_start(ov[:, b - 1], X[:, (b - 1) * KT:b * KT, :]).then_inc(sem["stored"], 16)
            sp.wait_ge(sem["mixed_x1"], base["mixed_x1"] + NB)
            sp.dma_start(ov[:, NB - 1], X[:, (NB - 1) * KT:, :]).then_inc(sem["stored"], 16)
            sp.wait_ge(sem["stored"], 16 * NB)

        @block.tensor
        def _(pe):
            def transpose_x(l, b):
                pe.wait_ge(sem[f"xh{l}_0"], base[f"xh{l}_0"] + 2 * (b + 1))
                if b == 0 and l == 0:
                    pe.wait_ge(sem["consts_in"], 16)
                for k in range(KT):
                    i = pe.transpose(P0[:, k * P:(k + 1) * P], xh[:, 0, b % 2, k], const("ident"))
                i.then_inc(sem[f"x_t_ps{l}"], 1)

            def project_qk(l, b):
                pe.wait_ge(sem[f"h_t{l}"], base[f"h_t{l}"] + b + 1)
                if b == 0:
                    pe.wait_ge(sem["w1_in" if l else "attn_in"], 16 * (3 if l else 4))
                for side in range(2):
                    i = pe.matmul(P0[:, side * T:(side + 1) * T], w_qk[:, side * C:(side + 1) * C], h_t[:, b % 2],
                                  start=True, stop=True)
                i.then_inc(sem[f"qk_ps{l}"], 1)

            def project_qks(b):
                at_least(pe, sem["gn_avg"], cnt(b - 4))
                for side in range(2):
                    i = pe.matmul(P1[:, side * T:(side + 1) * T], w_qks[:, side * C:(side + 1) * C], h_t[:, b % 2],
                                  start=True, stop=True)
                i.then_inc(sem["qks_ps"], 1)

            def project_v(l, b, ps):
                for k in range(KT):
                    i = pe.matmul(ps[:, k * P:(k + 1) * P], h_t[:, b % 2, k * P:(k + 1) * P], w_v[:, :],
                                  start=True, stop=True)
                if l == 0:
                    i = pe.matmul(ps[:, T:2 * T], w_gate[:, :], h_t[:, b % 2], start=True, stop=True)
                i.then_inc(sem[f"v_ps{l}"], 1)

            def retention_scores(b, g):
                if g == 0:
                    pe.wait_ge(sem[f"stacked0_{b % 2}"], 96 * (b // 2 + 1))
                    if b == 0:
                        pe.wait_ge(sem["stack_rows"], 6)
                at_least(pe, sem["masked"], 4 * b + g - 1)
                r, ch = b % 3, g // 2
                for n in range(8):
                    at = (8 * (g % 2) + n) * T + ch * P
                    i = pe.matmul(pair[g % 2][:, n * P:(n + 1) * P], stack_k[:, r, at:at + P], stack_q[:, r, at:at + P],
                                  start=True, stop=True)
                i.then_inc(sem["scores0"], 1)

            def retention_pv(b, g):
                pe.wait_ge(sem["masked"], 4 * b + g + 1)
                ch = g // 2
                if g == 0:
                    pe.wait_ge(sem["v0"], b + 1)
                if g % 2 == 0:
                    at_least(pe, sem["y_pad0"], 2 * b + ch)
                for n in range(8):
                    h = 8 * (g % 2) + n
                    j, gg = h % 4, h // 4
                    i = pe.matmul(Y0[32 * j:32 * j + 32, gg * P:(gg + 1) * P], V[:, b % 4, ch, h * HD:h * HD + 32],
                                  probs[:, 2 * (g % 2) + n // 4, (n % 4) * P:(n % 4 + 1) * P], start=True, stop=True)
                i.then_inc(sem["pv0"], 1)

            def keys_to_tokens(b):
                at_least(pe, sem["logits0"], cnt(b + 2 - 6))
                pe.wait_ge(sem["qk0"], b + 1)
                pe.transpose(P1[:, 0:P], qk[:, b % 3, T:T + P], const("ident")).then_inc(sem["k_tok_ps"], 1)

            def key_value_state(b):
                pe.wait_ge(sem["k_tok"], b + 1)
                at_least(pe, sem["rot_a"], cnt(b + 2))
                v = V[:, b % 4, 0, 0:C].rearrange("p (h d) -> p d h", d=HD)
                pe.matmul(P0[:, 0:C], k_tok[:, :], v, start=True, stop=True).then_inc(sem["state_ps"], 1)

            def state_to_y(b):
                pe.wait_ge(sem["state"], b + 1)
                at_least(pe, sem["gated0"], cnt(b + 2))
                pe.matmul(P2[:, 0:P], state[:, :], qk[:, b % 3, P:T], start=True, stop=True).then_inc(sem["y_state_ps"], 1)

            def average_heads(b):
                pe.wait_ge(sem["gn_sq"], b + 1)
                at_least(pe, sem["k_tok"], cnt(b + 2))
                pe.matmul(P1[:, 0:2], const("head_avg"), gn_mv[:, :], start=True, stop=True).then_inc(sem["gn_avg_ps"], 1)

            def broadcast_mod(l, b, ps):
                pe.wait_ge(sem[f"diag{l}"], base[f"diag{l}"] + 4 * (b + 1))
                if l == 0 and b == 0:
                    pe.wait_ge(sem["ones"], 1)
                pe.matmul(ps[:, :], ones[:, :], diag[:, :, :].rearrange("p a c -> p (a c)"), start=True, stop=True)\
                  .then_inc(sem[f"mod_ps{l}"], 1)

            def project_out(l, b):
                pe.wait_ge(sem[f"o_t{l}"], base[f"o_t{l}"] + b + 1)
                pe.wait_ge(sem[f"w_out{l}"], base[f"w_out{l}"] + b + 1)
                for k in range(KT):
                    i = pe.matmul(P1[:, k * P:(k + 1) * P], o_t[:, b % 2, k * P:(k + 1) * P], w_out[:, b % 2, :],
                                  start=True, stop=True)
                i.then_inc(sem[f"out_ps{l}"], 1)

            def transpose_h2(l, b):
                pe.wait_ge(sem[f"h_tok{l}"], base[f"h_tok{l}"] + 2 * (b + 1))
                for k in range(KT):
                    i = pe.transpose(P0[:, k * P:(k + 1) * P], h_tok[:, b % 2, k], const("ident"))
                i.then_inc(sem[f"h2_ps{l}"], 1)

            def route_logits(l, b):
                pe.wait_ge(sem[f"h2_t{l}"], base[f"h2_t{l}"] + b + 1)
                if b == 0 and l == 0:
                    pe.wait_ge(sem["late_in"], 16 * 5)
                for k in range(KT):
                    i = pe.matmul(P1[:, k * E:(k + 1) * E], h2_t[:, k * P:(k + 1) * P], router_w[:, l, :],
                                  start=True, stop=True)
                i.then_inc(sem[f"logits_ps{l}"], 1)

            pe.wait_ge(sem["silu_c"], 1)
            for l in range(2):
                for k in range(6):
                    i = pe.matmul(P2[:, (6 * l + k) * NB:(6 * l + k + 1) * NB], mod_w[:, l, k * C:(k + 1) * C],
                                  sc_t[:, l, :], start=True, stop=True)
            i.then_inc(sem["mod_t_ps"], 1)

            for s in STEPS[0]:
                b = stages(0, s)
                a, m, z, y = b["front"], b["scores"], b["back"], b["route"]
                if m is not None:
                    retention_scores(m, 0)
                    retention_scores(m, 1)
                if a is not None:
                    at_least(pe, sem["h2_t0"], cnt(s - 6))
                    transpose_x(0, a)
                if m is not None:
                    keys_to_tokens(m)
                    at_least(pe, sem["y_state"], cnt(m - 1))
                    at_least(pe, sem["gated0"], cnt(s - 1))
                    broadcast_mod(0, m, P2)
                    retention_pv(m, 0)
                    retention_scores(m, 2)
                if z is not None:
                    at_least(pe, sem["logits0"], cnt(s - 6))
                    average_heads(z)
                if a is not None:
                    project_qk(0, a)
                    if a >= 2:
                        pe.wait_ge(sem["k_tok"], cnt(m))
                    project_qks(a)
                if m is not None:
                    retention_pv(m, 1)
                    retention_scores(m, 3)
                if a is not None:
                    at_least(pe, sem["mod_bc0"], cnt(m if m is not None else -1))
                    if a == 0:
                        pe.wait_ge(sem["mod_shift"], 8)
                        pe.wait_ge(sem["mod_t_gate"], 4)
                    else:
                        at_least(pe, sem["gated0"], cnt(a - 1))
                    project_v(0, a, P2)
                if m is not None:
                    at_least(pe, sem["h2_t0"], cnt(s - 6))
                    key_value_state(m)
                    retention_pv(m, 2)
                if z is not None:
                    at_least(pe, sem["rot_b"], cnt(s))
                    at_least(pe, sem["k_tok"], cnt(s - 2))
                    project_out(0, z)
                if m is not None:
                    at_least(pe, sem["mod_bc0"], cnt(m))
                    state_to_y(m)
                    retention_pv(m, 3)
                if y is not None:
                    at_least(pe, sem["state"], cnt(s - 2))
                    at_least(pe, sem["h2_t0"], cnt(s - 6))
                    transpose_h2(0, y)
                    at_least(pe, sem["x_mid0"], cnt(s - 4))
                    at_least(pe, sem["logits0"], cnt(s - 6))
                    route_logits(0, y)

            def routing(l):
                pe.wait_ge(sem[f"picked_b{l}"], base[f"picked_b{l}"] + 1)
                pe.wait_ge(sem[f"tiles_before_b{l}"], base[f"tiles_before_b{l}"] + 1)
                if l == 0:
                    pe.wait_ge(sem["bf16_consts"], 4)
                flat = lambda t: t[:, :, :].rearrange("p e i -> p (e i)")
                pe.matmul(P0[:, 0:P], before_b[:, :], flat(picked_b), start=True, stop=False)
                pe.matmul(P0[:, 0:P], ones_b[:, :], flat(tiles_before_b), start=False, stop=True)\
                  .then_inc(sem[f"ranks_ps{l}"], 1)
                pe.wait_ge(sem[f"total_b{l}"], base[f"total_b{l}"] + 1)
                pe.matmul(P1[:, 0:E], ones_b[:, :], total_b[:, :], start=True, stop=True).then_inc(sem[f"counts_ps{l}"], 1)
                pe.wait_ge(sem[f"hot_vals{l}"], base[f"hot_vals{l}"] + 2)
                for n in range(CHOICES * NT):
                    pe.wait_ge(sem[f"hot_lane{l}"], base[f"hot_lane{l}"] + n + 1)
                    pe.matmul(P2[:, 0:2 * TILES], hot_lane[:, n % 4, :], hot_vals[:, n].rearrange("p a j -> p (a j)"),
                              start=(n == 0), stop=(n == CHOICES * NT - 1)).then_inc(sem[f"slot_ps{l}"], 1)

            def expert_tiles(l):
                def transpose_rows(n, r, uses):
                    pe.wait_ge(sem[f"gathered{r}_{l}"], base[f"gathered{r}_{l}"] + 16 * (uses + 1))
                    pe.transpose(P0[:, 0:P], x_rows[:, r, :], const("ident")).then_inc(sem[f"x_t_e_ps{l}"], 1)

                def first(n, r):
                    pe.wait_ge(sem[f"x_t{l}"], base[f"x_t{l}"] + n + 1)
                    pe.wait_ge(sem[f"w_now{l}"], base[f"w_now{l}"] + n + 1)
                    at_least(pe, sem[f"hid_t{l}"], n - 1, base[f"hid_t{l}"])
                    for which, (banks, done) in enumerate(((HIDDEN, f"hidden_ps{l}"), (UP, "up_ps"))[:l + 1]):
                        for k in range(FK):
                            i = pe.matmul(banks[r % 2][:, k * P:(k + 1) * P], w_now[:, r % 2, which, k * P:(k + 1) * P],
                                          x_t[:, r % 2, :], start=True, stop=True)
                        i.then_inc(sem[done], 1)

                def second(n, r):
                    expert = pe.value_load(tile_exp[0:1, bass.ds(n, 1)], min_val=0, max_val=E - 1)
                    at_least(pe, sem[f"y_rows{l}"], n - 1, base[f"y_rows{l}"])
                    pe.wait_ge(sem[f"hid_t{l}"], base[f"hid_t{l}"] + n + 1)
                    for k in range(FK):
                        i = pe.matmul(Y_ROWS[r % 2], hid_t[:, r % 2, k * P:(k + 1) * P], W2[:, bass.ds(expert, 1), k, :],
                                      start=(k == 0), stop=(k == FK - 1))
                    i.then_inc(sem[f"y_ps{l}"], 1)

                def step(n, r, uses):
                    first(n, r)
                    if exists(n + 1):
                        transpose_rows(n + 1, (r + 1) % RING, uses + (r + 1) // RING)
                    if exists(n - 1):
                        second(n - 1, (r - 1) % RING)

                pe.wait_ge(sem[f"tile_exp{l}"], base[f"tile_exp{l}"] + 1)
                pe.wait_ge(sem[f"experts{l}_in"], 64 if l == 0 else 32)
                transpose_rows(0, 0, 0)
                all_tiles(pe, step)
                second(TILES - 1, (TILES - 1) % RING)

            routing(0)
            expert_tiles(0)

            half = [[pair[i][:, k * 512:(k + 1) * 512] for k in range(2)] for i in range(2)]

            def max_scores(b, g):
                ps = half[0][g % 2]
                if g == 0:
                    pe.wait_ge(sem[f"stacked1_{b % 2}"], base[f"stacked1_{b % 2}"] + 96 * (b // 2 + 1))
                at_least(pe, sem["maxed"], 12 * b + g - 1)
                r = b % STACKS
                if g < 4:
                    cells = [(4 * g + n, 0, P) for n in range(4)]
                else:
                    cells = [(2 * (g - 4) + n, P, T) for n in range(2)]
                for n, (h, t0, keys) in enumerate(cells):
                    i = pe.matmul(ps[:, n * keys:(n + 1) * keys], stack_q[0:MAX_ROW, r, h * T + t0:h * T + t0 + P],
                                  stack_k[0:MAX_ROW, r, h * T:h * T + keys], start=(n == 0), stop=False,
                                  skip_group_check=True)
                diag_blocks = [n * keys + keys - P for n in range(len(cells))]
                for n, at in enumerate(diag_blocks):
                    i = pe.matmul(ps[:, at:at + P], ident_b[:, :], neg_mask[:, :], start=False, stop=(n == len(cells) - 1),
                                  skip_group_check=True)
                i.then_inc(sem["scores_max"], 1)

            def exp_scores(b, g):
                gp, i6 = g // 6, g % 6
                ps = half[1][g % 2]
                if g == 0:
                    pe.wait_ge(sem[f"max_in{b % 2}"], 16 * (b // 2 + 1))
                at_least(pe, sem["exped"], 12 * b + g - 1)
                r = b % STACKS
                for n, (h, s0, t0, cols) in enumerate(exp_cells(g)):
                    i = pe.matmul(ps[:, n * cols:(n + 1) * cols], stack_k[:, r, h * T + s0:h * T + s0 + P],
                                  stack_q[:, r, h * T + t0:h * T + t0 + cols], start=True, stop=True)
                i.then_inc(sem["scores_exp"], 1)

            def softmax_pv(b, g):
                gp, i6 = g // 6, g % 6
                ps = (Y0, P2)[gp]
                pe.wait_ge(sem["probs_causal"], 12 * b + g + 1)
                if i6 == 0:
                    at_least(pe, sem["y_pad1"], 2 * b + gp - 1, base["y_pad1"])
                if g == 0:
                    pe.wait_ge(sem["v1"], b + 1)
                for n, (h, s0, t0, cols) in enumerate(exp_cells(g)):
                    j, gg = h % 4, (h // 4) % 2
                    i = pe.matmul(ps[32 * j:32 * j + 32, gg * T + t0:gg * T + t0 + cols],
                                  V[:, b % 4, s0 // P, h * 9:h * 9 + 32], probs[:, g % 4, n * cols:(n + 1) * cols],
                                  start=(i6 < 2 and gg == 0), stop=(i6 >= 4), skip_group_check=True)
                i.then_inc(sem["pv1"], 1)

            def max_to_rows(b):
                pe.wait_ge(sem["max_parts"], 2 * (b + 1))
                for k in range(KT):
                    i = pe.transpose(P1[0:2 * H, k * 64:(k + 1) * 64].bitcast(BF16), max_parts[:, b % 2, k], ident_b[:, :])
                i.then_inc(sem["max_t_ps"], 1)

            for s in STEPS[1]:
                b = stages(1, s)
                a, m, w, z, y = b["front"], b["scores"], b["probs"], b["back"], b["route"]
                if a is not None:
                    at_least(pe, sem["h2_t1"], cnt(s - 7), base["h2_t1"])
                    at_least(pe, sem["part1_1"], cnt(s - 1), base["part1_1"])
                    at_least(pe, sem["rest1_1"], cnt(s - 1), base["rest1_1"])
                    transpose_x(1, a)
                at_least(pe, sem["v1"], cnt(s - 1))
                at_least(pe, sem["mod_bc1"], cnt(s - 6), base["mod_bc1"])
                at_least(pe, sem["x_mid1"], cnt(s - 6), base["x_mid1"])
                at_least(pe, sem["logits1"], cnt(s - 7), base["logits1"])
                if 0 <= s - 2 < NB:
                    max_to_rows(s - 2)
                if w is not None:
                    exp_scores(w, 0)
                if m is not None:
                    max_scores(m, 0)
                if a is not None:
                    project_qk(1, a)
                if z is not None:
                    at_least(pe, sem["max_t"], cnt(s - 2))
                    broadcast_mod(1, z, P1)
                if a is not None:
                    at_least(pe, sem["mod_bc1"], cnt(s - 5), base["mod_bc1"])
                    at_least(pe, sem["max_t"], cnt(s - 2))
                    project_v(1, a, P1)
                for g in range(12):
                    if w is not None and g + 1 < 12:
                        exp_scores(w, g + 1)
                    if m is not None and g + 1 < 12:
                        max_scores(m, g + 1)
                    if w is not None:
                        softmax_pv(w, g)
                    if g == 5 and z is not None:
                        at_least(pe, sem["v1"], cnt(s))
                        at_least(pe, sem["mod_bc1"], cnt(z), base["mod_bc1"])
                        project_out(1, z)
                    if g == 7 and y is not None:
                        at_least(pe, sem["part1_1"], cnt(s), base["part1_1"])
                        at_least(pe, sem["rest1_1"], cnt(s), base["rest1_1"])
                        at_least(pe, sem["h2_t1"], cnt(s - 7), base["h2_t1"])
                        transpose_h2(1, y)
                    if g == 9 and y is not None:
                        at_least(pe, sem["x_mid1"], cnt(s - 5), base["x_mid1"])
                        at_least(pe, sem["max_t"], cnt(s - 2))
                        at_least(pe, sem["v1"], cnt(s))
                        route_logits(1, y)

            routing(1)
            expert_tiles(1)

        @block.vector
        def _(ve):
            def norm_stats(l, which, b):
                tag = f"{l}_{which}"
                for k in range(KT):
                    ve.bn_stats(stats[:, which, k], X[:, b * KT + k, :]).then_inc(sem[f"stats{tag}"], 1)
                ve.wait_ge(sem[f"stats{tag}"], base[f"stats{tag}"] + 2 * (b + 1))
                for k in range(KT):
                    ve.bn_aggr(mv[:, which, k], stats[:, which, k]).then_inc(sem[f"mv{tag}"], 1)
                ve.wait_ge(sem[f"mv{tag}"], base[f"mv{tag}"] + 2 * (b + 1))
                ve.tensor_scalar(var_eps[:, which, :], mv[:, which, :, 1], EPS, None, ALU.add).then_inc(sem[f"var{tag}"], 1)

            def norm_apply(l, which, b):
                tag = f"{l}_{which}"
                ve.wait_ge(sem[f"rstd{tag}"], base[f"rstd{tag}"] + b + 1)
                if which == 0:
                    at_least(ve, sem[f"x_t_ps{l}"], cnt(b - 2), base[f"x_t_ps{l}"])
                else:
                    at_least(ve, sem[f"h_mul{l}"], cnt(b - 2), base[f"h_mul{l}"])
                for k in range(KT):
                    ve.tensor_scalar(xh[:, which, b % 2, k], X[:, b * KT + k, :], mv[:, which, k, 0:1], rstd[:, which, k:k + 1],
                                     ALU.subtract, ALU.mult).then_inc(sem[f"xh{tag}"], 1)

            def read_logits(l, b):
                ve.wait_ge(sem[f"logits_ps{l}"], base[f"logits_ps{l}"] + b + 1)
                dst = logits[:, :, b * KT:(b + 1) * KT].rearrange("p e k -> p k e")
                src = P1[:, 0:KT * E].rearrange("p (k e) -> p k e", e=E)
                if l == 0:
                    ve.tensor_copy(dst, src).then_inc(sem[f"logits{l}"], 1)
                else:
                    ve.tensor_tensor(dst, src, router_b[:, :].unsqueeze(1).broadcast_to((P, KT, E)), ALU.add)\
                      .then_inc(sem[f"logits{l}"], 1)

            def add_to_x(l, b):
                ve.wait_ge(sem[f"out_ps{l}"], base[f"out_ps{l}"] + b + 1)
                xs = X[:, b * KT:(b + 1) * KT, :]
                ve.tensor_tensor(xs, P1[:, 0:T].rearrange("p (k c) -> p k c", k=KT), xs, ALU.add)\
                  .then_inc(sem[f"x_mid{l}"], 1)

            def mask_scores(b, g):
                ve.wait_ge(sem["scores0"], 4 * b + g + 1)
                at_least(ve, sem["pv0"], 4 * b + g - 1)
                if b == 0 and g == 0:
                    ve.wait_ge(sem["consts_in"], 16)
                ve.tensor_tensor(probs[:, 2 * (g % 2):2 * (g % 2) + 2, :].rearrange("p a (n t) -> p (a n) t", t=P),
                                 pair[g % 2][:, :].rearrange("p (n t) -> p n t", t=P),
                                 const("causal").unsqueeze(1).broadcast_to((P, 8, P)), ALU.mult).then_inc(sem["masked"], 1)

            def group_stats(b):
                ve.wait_ge(sem[f"y_in0_{b % 2}"], 16 * (b // 2 + 1))
                ve.wait_ge(sem["y_state"], b + 1)
                y = y_t[:, b % 3, :]
                ve.tensor_tensor(y[:, P:T], y[:, P:T], y_state[:, b % 3, :], ALU.add).then_inc(sem["y_sum"], 1)
                ve.wait_ge(sem["y_sum"], b + 1)
                ve.bn_stats(gn_stats[:, :], y).then_inc(sem["gn_stats"], 1)
                ve.wait_ge(sem["gn_stats"], b + 1)
                at_least(ve, sem["gn_avg_ps"], b)
                ve.bn_aggr(gn_mv[:, :], gn_stats[:, :]).then_inc(sem["gn_mv"], 1)
                ve.wait_ge(sem["gn_mv"], b + 1)
                ve.scalar_tensor_tensor(out=gn_mv[:, 1:2], in0=gn_mv[:, 0:1], scalar=gn_mv[:, 0:1], in1=gn_mv[:, 1:2],
                                        op0=ALU.mult, op1=ALU.add).then_inc(sem["gn_sq"], 1)

            def group_var(b):
                ve.wait_ge(sem["gn_avg"], b + 1)
                ve.scalar_tensor_tensor(out=gn_ve[:, 0:1], in0=gn_avg[:, 0:1], scalar=gn_avg[:, 0:1], in1=gn_avg[:, 1:2],
                                        op0=ALU.mult, op1=ALU.subtract).then_inc(sem["gn_neg"], 1)
                ve.wait_ge(sem["gn_neg"], b + 1)
                ve.tensor_scalar(gn_ve[:, 1:2], gn_ve[:, 0:1], -1.0, EPS, ALU.mult, ALU.add).then_inc(sem["gn_var"], 1)

            def group_apply(b):
                ve.wait_ge(sem["gn_rstd"], b + 1)
                if b == 0:
                    ve.wait_ge(sem["late_in"], 16 * 5)
                ve.tensor_tensor(gn_ab[:, 0:1], gn_rstd[:, :], gn[:, 0:1], ALU.mult).then_inc(sem["gn_a"], 1)
                ve.wait_ge(sem["gn_a"], b + 1)
                ve.scalar_tensor_tensor(out=gn_ab[:, 1:2], in0=gn_avg[:, 0:1], scalar=gn_ab[:, 0:1], in1=gn[:, 1:2],
                                        op0=ALU.mult, op1=ALU.subtract).then_inc(sem["gn_b"], 1)
                ve.wait_ge(sem["gn_b"], b + 1)
                at_least(ve, sem["o_t0"], b)
                ve.tensor_scalar(y_n[:, :], y_t[:, b % 3, :], gn_ab[:, 0:1], gn_ab[:, 1:2], ALU.mult, ALU.subtract)\
                  .then_inc(sem["y_n"], 1)

            def rotate(b):
                ve.wait_ge(sem["qk_ps0"], b + 1)
                at_least(ve, sem["qk0"], b)
                if b == 0:
                    ve.wait_ge(sem["rotary_in"], 16)
                ve.tensor_tensor(rot[:, 0], P0[:, :], rotary[:, 0], ALU.mult).then_inc(sem["rot_a"], 1)
                ve.wait_ge(sem["qks_ps"], b + 1)
                ve.tensor_tensor(rot[:, 1], P1[:, :], rotary[:, 1], ALU.mult).then_inc(sem["rot_b"], 1)

            def mask_state(b):
                ve.wait_ge(sem["state_ps"], b + 1)
                at_least(ve, sem["y_state_ps"], b)
                ve.tensor_tensor(state[:, :], P0[:, 0:C], const("same_head"), ALU.mult).then_inc(sem["state"], 1)

            ve.memset(ones[:, :], 1.0).then_inc(sem["ones"], 1)
            ve.memset(half_neg[:, :], -0.5).then_inc(sem["half_neg"], 1)
            for r in range(3):
                ve.memset(stack_q[:, r, :].bitcast(F32), 0.0).then_inc(sem["stack_rows"], 1)
                if r == 0:
                    ve.wait_ge(sem["x_in0"], 16)
                    norm_stats(0, 0, 0)
                    norm_apply(0, 0, 0)
                    ve.wait_ge(sem["mod_t_ps"], 1)
                    for l in range(2):
                        for k in (0, 3):
                            at = (6 * l + k) * NB
                            ve.tensor_copy(mod_t[:, l, k, :], P2[:, at:at + NB]).then_inc(sem["mod_shift"], 1)
                        for k in (1, 4):
                            at = (6 * l + k) * NB
                            ve.tensor_scalar(mod_t[:, l, k, :], P2[:, at:at + NB], 1.0, None, ALU.add).then_inc(sem["mod_shift"], 1)
                    for l in range(2):
                        for n, k in enumerate((2, 5)):
                            at, done = (6 * l + k) * NB, 3 * (2 * l + n)
                            raw, low, up = P2[:, at:at + NB], gate_tmp[:, 2 * l + n, 0, :], gate_tmp[:, 2 * l + n, 1, :]
                            ve.tensor_scalar(low, raw, -FLOOR, None, ALU.min).then_inc(sem["gate_steps"], 1)
                            ve.tensor_scalar(up, raw, FLOOR, None, ALU.max).then_inc(sem["gate_steps"], 1)
                            ve.wait_ge(sem["gate_steps"], done + 2)
                            ve.tensor_tensor(up, up, low, ALU.subtract).then_inc(sem["gate_steps"], 1)
                            ve.wait_ge(sem["gate_steps"], done + 3)
                            ve.scalar_tensor_tensor(out=gate_tmp[:, 2 * l + n, 2, :], in0=raw, scalar=0.0, in1=up, op0=ALU.is_ge, op1=ALU.mult)\
                              .then_inc(sem["gate_pos"], 1)
                            ve.wait_ge(sem["gate_pos"], 2 * l + n + 1)
                            ve.tensor_tensor(mod_t[:, l, k, :], gate_tmp[:, 2 * l + n, 2, :], low, ALU.add).then_inc(sem["mod_t_gate"], 1)
            ve.memset(V[:, :, :, :], 0.0).then_inc(sem["v_clear"], 1)
            ve.wait_ge(sem["v_clear"], 1)
            ve.wait_ge(sem["pool_rows"], STACKS - 1)
            ve.memset(stack_k[MAX_ROW:MAX_ROW + 2, 0:STACKS - 1, :], 1.0).then_inc(sem["stack_rows"], 3)

            for s in STEPS[0]:
                b = stages(0, s)
                a, m, z, y = b["front"], b["scores"], b["back"], b["route"]
                if b["logits"] is not None:
                    read_logits(0, b["logits"])
                if m is not None:
                    mask_scores(m, 0)
                    mask_scores(m, 1)
                if z is not None:
                    group_stats(z)
                if a is not None:
                    rotate(a)
                if z is not None:
                    group_var(z)
                if m is not None:
                    mask_scores(m, 2)
                if z is not None:
                    group_apply(z)
                if m is not None:
                    mask_state(m)
                    mask_scores(m, 3)
                if z is not None:
                    add_to_x(0, z)
                    ve.wait_ge(sem["x_mid0"], z + 1)
                    norm_stats(0, 1, z)
                n = b["next"]
                if n is not None and n > 0:
                    if n == 1:
                        ve.wait_ge(sem["x_in1"], 16)
                    norm_stats(0, 0, n)
                if z is not None:
                    norm_apply(0, 1, z)
                if n is not None and n > 0:
                    norm_apply(0, 0, n)

            routing_steps = [0]

            def routing(l):
                steps = routing_steps

                def done(i):
                    i.then_inc(sem["routing"], 1)
                    steps[0] += 1
                    ve.wait_ge(sem["routing"], steps[0])

                by_tile = lambda t: t.rearrange("p e i -> p i e")
                over_e = lambda t: t.unsqueeze(1).broadcast_to((P, E, NT))
                L = logits[:, :, :]
                ve.wait_ge(sem[f"logits{l}"], base[f"logits{l}"] + NB)
                if l == 0:
                    ve.wait_ge(sem["bf16_consts"], 4)
                ids = const("expert_id").rearrange("p (e i) -> p e i", e=E)
                for choice, (src, top) in enumerate(((L, r_max), (second[:, :, :], r_max2))):
                    if choice == 1:
                        done(ve.scalar_tensor_tensor(out=second[:, :, :], in0=pick[:, 0], scalar=-BIG, in1=L,
                                                     op0=ALU.mult, op1=ALU.add))
                    done(ve.tensor_reduce(top[:, :], by_tile(src), AX_X, ALU.max))
                    done(ve.tensor_tensor(r_eq[:, :, :], src, over_e(top[:, :]), ALU.is_equal))
                    done(ve.scalar_tensor_tensor(out=r_idx[:, :, :], in0=r_eq[:, :, :], scalar=-64.0, in1=ids,
                                                 op0=ALU.mult, op1=ALU.add))
                    done(ve.tensor_reduce(r_min[:, :], by_tile(r_idx[:, :, :]), AX_X, ALU.min))
                    done(ve.tensor_tensor(pick[:, choice], r_idx[:, :, :], over_e(r_min[:, :]), ALU.is_equal))
                ve.tensor_tensor(gap[:, :], r_max2[:, :], r_max[:, :], ALU.subtract).then_inc(sem[f"gap{l}"], 1)
                done(ve.tensor_tensor(picked[:, :, :], pick[:, 0], pick[:, 1], ALU.add))
                ve.tensor_copy(picked_b[:, :, :], picked[:, :, :]).then_inc(sem[f"picked_b{l}"], 1)
                flat = lambda t: t[:, :, :].rearrange("p e i -> p (e i)")
                done(ve.tensor_tensor_scan(flat(upto), const("restart"), flat(picked), 0.0, ALU.mult, ALU.add))
                ve.tensor_tensor(tiles_before_b[:, :, :], upto[:, :, :], picked[:, :, :], ALU.subtract)\
                  .then_inc(sem[f"tiles_before_b{l}"], 1)
                ve.tensor_copy(total_b[:, :], upto[:, :, NT - 1]).then_inc(sem[f"total_b{l}"], 1)
                ve.wait_ge(sem[f"counts_ps{l}"], base[f"counts_ps{l}"] + 1)
                done(ve.tensor_tensor(over[:, :, :], P1[:, 0:E].unsqueeze(2).broadcast_to((P, E, 16)),
                                      const("steps128").unsqueeze(1).broadcast_to((P, E, 16)), ALU.is_gt))
                done(ve.tensor_reduce(n_tiles[:, :], over[:, :, :], AX_X, ALU.add))
                done(ve.tensor_tensor_scan(tile_end[:, :], ones[:, 0:E], n_tiles[:, :], 0.0, ALU.mult, ALU.add))
                done(ve.tensor_tensor(tile_start[:, :], tile_end[:, :], n_tiles[:, :], ALU.subtract))
                ve.wait_ge(sem[f"ranks_ps{l}"], base[f"ranks_ps{l}"] + 1)
                done(ve.scalar_tensor_tensor(out=place[:, :, :], in0=tile_start[:, :].unsqueeze(2).broadcast_to((P, E, NT)),
                                             scalar=float(P), in1=P0[:, 0:P].rearrange("p (e i) -> p e i", e=E),
                                             op0=ALU.mult, op1=ALU.add))
                for choice in range(CHOICES):
                    done(ve.tensor_tensor(place_c[:, :, :], pick[:, choice], place[:, :, :], ALU.mult))
                    done(ve.tensor_reduce(slot[:, choice * NT:(choice + 1) * NT], by_tile(place_c[:, :, :]), AX_X, ALU.add))
                done(ve.tensor_copy(slot_i[:, :], slot[:, :]))
                done(ve.tensor_scalar(tile_i[:, :], slot_i[:, :], 7, None, ALU.logical_shift_right))
                done(ve.tensor_scalar(lane_i[:, :], slot_i[:, :], P - 1, None, ALU.bitwise_and))
                done(ve.tensor_copy(slot_tile[:, :], tile_i[:, :]))
                done(ve.tensor_copy(slot_lane[:, :], lane_i[:, :]))
                done(ve.tensor_tensor(hot_tile[:, :, :], slot_tile[:, :].unsqueeze(2).broadcast_to((P, CHOICES * NT, TILES)),
                                      const("iota")[:, 0:TILES].unsqueeze(1).broadcast_to((P, CHOICES * NT, TILES)),
                                      ALU.is_equal))
                ve.tensor_scalar(hot_vals[:, :, 0, :], hot_tile[:, :, :], const("pid1"), None, ALU.mult)\
                  .then_inc(sem[f"hot_vals{l}"], 1)
                ve.tensor_tensor(hot_vals[:, :, 1, :], hot_tile[:, :, :],
                                 const("tile_id").unsqueeze(2).broadcast_to((P, CHOICES * NT, TILES)), ALU.mult)\
                  .then_inc(sem[f"hot_vals{l}"], 1)
                for n in range(CHOICES * NT):
                    at_least(ve, sem[f"slot_ps{l}"], n - 3, base[f"slot_ps{l}"])
                    ve.tensor_scalar(hot_lane[:, n % 4, :], iota_b[:, :], slot_lane[:, n:n + 1], None, ALU.is_equal)\
                      .then_inc(sem[f"hot_lane{l}"], 1)
                done(ve.tensor_tensor(ended[:, :, :], tile_end[:, :].unsqueeze(1).broadcast_to((P, TILES, E)),
                                      const("iota")[:, 0:TILES].unsqueeze(2).broadcast_to((P, TILES, E)), ALU.is_le))
                done(ve.tensor_reduce(tile_exp_f[:, :], ended[:, :, :], AX_X, ALU.add))
                ve.tensor_scalar(tile_exp[:, :], tile_exp_f[:, :], float(E - 1), None, ALU.min).then_inc(sem[f"tile_exp{l}"], 1)
                ve.wait_ge(sem[f"slot_ps{l}"], base[f"slot_ps{l}"] + CHOICES * NT)
                done(ve.tensor_copy(ident_lo[:, :], P2[:, 0:TILES]))
                done(ve.scalar_tensor_tensor(out=ident_all[:, :], in0=P2[:, TILES:2 * TILES], scalar=float(P), in1=ident_lo[:, :],
                                             op0=ALU.mult, op1=ALU.add))
                done(ve.tensor_scalar(wrap[:, :], ident_all[:, :], TOK + 0.5, -float(TOK), ALU.is_gt, ALU.mult))
                done(ve.scalar_tensor_tensor(out=src_f[:, :], in0=wrap[:, :], scalar=-1.0, in1=ident_all[:, :],
                                             op0=ALU.add, op1=ALU.add))
                ve.tensor_scalar(src_row[:, :], src_f[:, :], 0.0, None, ALU.max).then_inc(sem[f"src_row{l}"], 1)
                done(ve.tensor_scalar(empty[:, :], ident_all[:, :], 0.5, None, ALU.is_lt))
                done(ve.tensor_tensor(empty_at[:, :], empty[:, :], const("trash"), ALU.mult))
                ve.scalar_tensor_tensor(out=dst_row[:, :], in0=empty_at[:, :], scalar=-1.0, in1=ident_all[:, :],
                                        op0=ALU.add, op1=ALU.add).then_inc(sem[f"dst_row{l}"], 1)
                ve.wait_ge(sem[f"gap_exp{l}"], base[f"gap_exp{l}"] + 1)
                done(ve.tensor_scalar(gap_den[:, :], gap_exp[:, :], 1.0, None, ALU.add))
                done(ve.reciprocal(weight[:, 0, :], gap_den[:, :]))
                ve.tensor_tensor(weight[:, 1, :], gap_exp[:, :], weight[:, 0, :], ALU.mult).then_inc(sem[f"weights{l}"], 1)

            def expert_tiles(l):
                def expert_of(n):
                    return ve.value_load(tile_exp[0:1, bass.ds(n, 1)], min_val=0, max_val=E - 1)

                def copy_weights(n, r):
                    e = expert_of(n)
                    if l == 0:
                        ve.tensor_copy(b_now[:, r % 2, :], B1[:, bass.ds(e, 1), :]).then_inc(sem["b_now"], 1)
                        ve.tensor_copy(w_now[:, r % 2, 0, :], W1[:, bass.ds(e, 1), :]).then_inc(sem["w_now0"], 1)
                    else:
                        ve.tensor_copy(w_now[:, r % 2, 0, :], W1[:, bass.ds(e, 1), :]).then_inc(sem["gate_now"], 1)
                        ve.tensor_copy(w_now[:, r % 2, 1, :], W_up[:, bass.ds(e, 1), :]).then_inc(sem["w_now1"], 1)

                def keep_rows(n, r, uses):
                    if l == 0:
                        e = expert_of(n)
                    ve.wait_ge(sem[f"y_ps{l}"], base[f"y_ps{l}"] + n + 1)
                    at_least(ve, sem[f"scattered{r}_{l}"], 16 * uses, base[f"scattered{r}_{l}"])
                    if l == 0:
                        ve.tensor_tensor(y_rows[:, r, :], Y_ROWS[r % 2], B2[:, bass.ds(e, 1), :], ALU.add)\
                          .then_inc(sem["y_rows0"], 1)
                    else:
                        ve.tensor_copy(y_rows[:, r, :], Y_ROWS[r % 2]).then_inc(sem["y_rows1"], 1)

                def step(n, r, uses):
                    at_least(ve, sem[f"y_ps{l}"], n - 1, base[f"y_ps{l}"])
                    if l == 0:
                        ve.wait_ge(sem["hidden_ps0"], n + 1)
                        ve.wait_ge(sem["b_now"], n + 1)
                        for k in range(FK):
                            i = ve.tensor_scalar(hid_t[:, r % 2, k * P:(k + 1) * P], HIDDEN[r % 2][:, k * P:(k + 1) * P],
                                                 b_now[:, r % 2, k:k + 1], 0.0, ALU.add, ALU.max)
                        i.then_inc(sem["hid_t0"], 1)
                    else:
                        ve.wait_ge(sem["up_ps"], n + 1)
                        ve.wait_ge(sem["hid_g"], n + 1)
                        ve.tensor_tensor(hid_t[:, r % 2, :], UP[r % 2], hid_g[:, r % 2, :], ALU.mult).then_inc(sem["hid_t1"], 1)
                    if exists(n - 1):
                        keep_rows(n - 1, (r - 1) % RING, uses - (r == 0))
                    if l == 0:
                        ve.wait_ge(sem["hid_t0"], n + 1)
                    if exists(n + 2):
                        copy_weights(n + 2, r)

                ve.wait_ge(sem[f"tile_exp{l}"], base[f"tile_exp{l}"] + 1)
                ve.wait_ge(sem[f"experts{l}_in"], 64 if l == 0 else 32)
                if l == 1:
                    ve.wait_ge(sem["up_in"], 16)
                copy_weights(0, 0)
                copy_weights(1, 1)
                all_tiles(ve, step)
                keep_rows(TILES - 1, (TILES - 1) % RING, (TILES - 1) // RING)

            def mix(l, b):
                for k in range(KT):
                    ve.wait_ge(sem[f"mix1_{l}"], base[f"mix1_{l}"] + 2 * b + k + 1)
                    at_least(ve, sem[f"mix3_{l}"], b, base[f"mix3_{l}"])
                    ve.scalar_tensor_tensor(out=y_mix2[:, k, :], in0=y_pair[:, b % 2, 1, k],
                                            scalar=weight[:, 1, b * KT + k:b * KT + k + 1], in1=y_mix[:, k, :],
                                            op0=ALU.mult, op1=ALU.add).then_inc(sem[f"mixed{l}"], 1)

            def mix_into_x(l, b):
                ve.wait_ge(sem[f"mix3_{l}"], base[f"mix3_{l}"] + b + 1)
                xs = X[:, b * KT:(b + 1) * KT, :]
                ve.tensor_tensor(xs, xs, y_mix3[:, :, :], ALU.add).then_inc(sem[f"mixed_x{l}"], 1)

            routing(0)
            expert_tiles(0)

            def max_of(b, g):
                ve.wait_ge(sem["scores_max"], 12 * b + g + 1)
                if g == 0:
                    at_least(ve, sem["max_parts"], 2 * b)
                ps = pair[0][:, (g % 2) * 512:(g % 2 + 1) * 512]
                if g < 4:
                    ve.tensor_reduce(row_max[:, 0, 4 * g:4 * g + 4], ps.rearrange("p (h s) -> p h s", h=4), AX_X, ALU.max)\
                      .then_inc(sem["maxed"], 1)
                else:
                    ve.tensor_reduce(row_max[:, 1, 2 * (g - 4):2 * (g - 4) + 2], ps.rearrange("p (h s) -> p h s", h=2), AX_X,
                                     ALU.max).then_inc(sem["maxed"], 1)

            def split_max(b):
                ve.wait_ge(sem["maxed"], 12 * (b + 1))
                at_least(ve, sem["max_t_ps"], cnt(b - 2))
                hi, lo = max_parts[:, b % 2, :, 0:H], max_parts[:, b % 2, :, H:2 * H]
                ve.tensor_scalar(hi, row_max[:, :, :], -1.0, None, ALU.mult).then_inc(sem["max_hi"], 1)
                ve.wait_ge(sem["max_hi"], b + 1)
                ve.scalar_tensor_tensor(out=lo, in0=row_max[:, :, :], scalar=-1.0, in1=hi, op0=ALU.mult, op1=ALU.subtract)\
                  .then_inc(sem["max_parts"], 2)

            def rest_of_qk(b):
                ve.wait_ge(sem["part1_1"], base["part1_1"] + b + 1)
                at_least(ve, sem["part3_1"], cnt(b - 2), base["part3_1"])
                ve.tensor_tensor(rest[:, b % 2, :], P0[:, :], parts[:, b % 2, 0, :], ALU.subtract).then_inc(sem["rest1_1"], 1)

            for s in STEPS[1]:
                b = stages(1, s)
                a, m, v, z = b["front"], b["scores"], b["dens"], b["back"]
                if b["logits"] is not None:
                    read_logits(1, b["logits"])
                if m is not None:
                    max_of(m, 0)
                if a is not None:
                    rest_of_qk(a)
                if v is not None:
                    ve.wait_ge(sem[f"y_in1_{v % 2}"], base[f"y_in1_{v % 2}"] + 32 * (v // 2 + 1))
                    at_least(ve, sem[f"den_out{v % 2}"], 16 * (v // 2))
                    ve.reciprocal(den_inv[:, v % 2, :], den[:, v % 2, :]).then_inc(sem["den_inv"], 1)
                for g in range(1, 12):
                    if m is not None:
                        max_of(m, g)
                    if g == 8 and z is not None:
                        add_to_x(1, z)
                        ve.wait_ge(sem["x_mid1"], base["x_mid1"] + z + 1)
                        norm_stats(1, 1, z)
                    if g == 10 and z is not None:
                        norm_apply(1, 1, z)
                if m is not None:
                    split_max(m)
                if s == -1:
                    mix(0, 0)
                    mix_into_x(0, 0)
                    ve.wait_ge(sem["mixed_x0"], 1)
                    norm_stats(1, 0, 0)
                    mix(0, 1)
                    norm_apply(1, 0, 0)
                    mix_into_x(0, 1)
                n = b["next"]
                if n is not None and n > 0:
                    if n + 1 < NB:
                        mix(0, n + 1)
                    ve.wait_ge(sem["mixed_x0"], n + 1)
                    norm_stats(1, 0, n)
                    if n + 1 < NB:
                        mix_into_x(0, n + 1)
                    norm_apply(1, 0, n)

            routing(1)
            expert_tiles(1)
            for b in range(NB + 1):
                if b < NB:
                    mix(1, b)
                if b >= 1:
                    mix_into_x(1, b - 1)

        @block.scalar
        def _(act):
            def modulate(l, b):
                act.wait_ge(sem[f"x_t_ps{l}"], base[f"x_t_ps{l}"] + b + 1)
                at_least(act, sem[f"v_ps{l}"], cnt(b - 2), base[f"v_ps{l}"])
                if b == 0 and l == 0:
                    act.wait_ge(sem["mod_shift"], 8)
                    act.wait_ge(sem["mod_t_gate"], 4)
                act.activation(h_t[:, b % 2], P0[:, 0:T], ACT.Identity, bias=mod_t[:, l, 0, b:b + 1],
                               scale=mod_t[:, l, 1, b:b + 1]).then_inc(sem[f"h_t{l}"], 1)

            def make_diag(l, b):
                at_least(act, sem[f"mod_ps{l}"], b, base[f"mod_ps{l}"])
                for n, k in enumerate((2, 3, 4, 5)):
                    act.activation(diag[:, n, :], const("ident"), ACT.Copy, scale=mod_t[:, l, k, b:b + 1]).then_inc(sem[f"diag{l}"], 1)

            def keep_mod(l, b, ps):
                act.wait_ge(sem[f"mod_ps{l}"], base[f"mod_ps{l}"] + b + 1)
                at_least(act, sem[f"h_tok{l}"], 2 * cnt(b - 4), base[f"h_tok{l}"])
                act.copy(mod_bc[:, b % 4, :], ps[:, 0:3 * C]).then_inc(sem[f"mod_bc_half{l}"], 1)
                if l == 1:
                    act.wait_ge(sem["mix3_0"], b + 1)
                act.copy(gb_bc[:, b, :], ps[:, 3 * C:4 * C]).then_inc(sem[f"mod_bc{l}"], 1)

            def first_part(l, b):
                at_least(act, sem[f"parts_out{l}_{b % 2}"], 96 * (b // 2), base[f"parts_out{l}_{b % 2}"])
                if l == 0:
                    act.wait_ge(sem["qk0"], b + 1)
                    act.copy(parts[:, b % 2, 0, :], qk[:, b % 3, :]).then_inc(sem["part1_0"], 1)
                else:
                    act.wait_ge(sem["qk_ps1"], base["qk_ps1"] + b + 1)
                    act.copy(parts[:, b % 2, 0, :], P0[:, :]).then_inc(sem["part1_1"], 1)

            def second_part(l, b):
                act.wait_ge(sem[f"rest1_{l}"], base[f"rest1_{l}"] + b + 1)
                act.copy(parts[:, b % 2, 1, :], rest[:, b % 2, :]).then_inc(sem[f"part2_{l}"], 1)

            def keep_h2(l, b):
                act.wait_ge(sem[f"h2_ps{l}"], base[f"h2_ps{l}"] + b + 1)
                at_least(act, sem[f"logits_ps{l}"], b, base[f"logits_ps{l}"])
                act.copy(h2_t[:, :], P0[:, 0:T]).then_inc(sem[f"h2_t{l}"], 1)

            act.wait_ge(sem["mod_in"], 64)
            act.activation(sc_t[:, :, :], c_t[:, :, :], ACT.Silu).then_inc(sem["silu_c"], 1)

            act.dma_start(W1[:, :, :], ins["w1"].rearrange("e c f -> c e f")).then_inc(sem["experts0_in"], 16)
            act.dma_start(W2[:, :, :, :], ins["w2"].rearrange("e (k p) c -> p e k c", p=P)).then_inc(sem["experts0_in"], 16)
            act.dma_start(B1[:, :, :], ins["b1"]).then_inc(sem["experts0_in"], 16)
            act.dma_start(W_up[:, :, :], ins["up_w"].rearrange("e c f -> c e f")).then_inc(sem["up_in"], 16)

            for s in STEPS[0]:
                b = stages(0, s)
                a, m, z, y = b["front"], b["scores"], b["back"], b["route"]
                if a is not None:
                    modulate(0, a)
                if m is not None:
                    act.wait_ge(sem["k_tok_ps"], m + 1)
                    at_least(act, sem["state_ps"], m)
                    act.copy(k_tok[:, :], P1[:, 0:P]).then_inc(sem["k_tok"], 1)
                    keep_mod(0, m, P2)
                if z is not None:
                    act.wait_ge(sem["gn_avg_ps"], z + 1)
                    at_least(act, sem["gn_b"], z)
                    act.copy(gn_avg[:, :], P1[:, 0:2]).then_inc(sem["gn_avg"], 1)
                if m is not None:
                    act.wait_ge(sem["pv0"], 4 * m + 2)
                    at_least(act, sem[f"y_out0_{m % 2}"], 128 * (m // 2))
                    act.copy(y_pad[:, m % 2, 0:512], Y0[:, :]).then_inc(sem["y_pad0"], 1)
                if a is not None:
                    act.wait_ge(sem["v_ps0"], a + 1)
                    if a == 0:
                        act.wait_ge(sem["v_clear"], 1)
                    at_least(act, sem["pv0"], 4 * cnt(a - 4))
                    act.copy(V[:, a % 4, :, 0:C], P2[:, 0:T].rearrange("p (k c) -> p k c", k=KT)).then_inc(sem["v0"], 1)
                    at_least(act, sem["o_t0"], cnt(a - 6))
                    act.activation(sgate[:, a % 6, :], P2[:, T:2 * T], ACT.Silu).then_inc(sem["gated0"], 1)
                    first_part(0, a)
                if m is not None:
                    act.wait_ge(sem["y_state_ps"], m + 1)
                    at_least(act, sem["y_sum"], cnt(m - 3))
                    act.copy(y_state[:, m % 3, :], P2[:, 0:P]).then_inc(sem["y_state"], 1)
                if a is not None:
                    second_part(0, a)
                if m is not None:
                    act.wait_ge(sem["pv0"], 4 * m + 4)
                    act.copy(y_pad[:, m % 2, 512:1024], Y0[:, :]).then_inc(sem["y_pad0"], 1)
                if y is not None:
                    keep_h2(0, y)
                if s == 1:
                    make_diag(0, 0)
                elif m is not None and m + 1 < NB:
                    make_diag(0, m + 1)

            def expert_tiles(l):
                def keep_x_t(n, r):
                    act.wait_ge(sem[f"x_t_e_ps{l}"], base[f"x_t_e_ps{l}"] + n + 1)
                    if l == 0:
                        at_least(act, sem["hidden_ps0"], n - 1)
                    else:
                        at_least(act, sem["up_ps"], n - 1)
                    act.copy(x_t[:, r % 2, :], P0[:, 0:P]).then_inc(sem[f"x_t{l}"], 1)

                def step(n, r, uses):
                    if exists(n + 1):
                        keep_x_t(n + 1, r + 1)
                    if l == 1:
                        act.wait_ge(sem["hidden_ps1"], base["hidden_ps1"] + n + 1)
                        at_least(act, sem["hid_t1"], n - 1, base["hid_t1"])
                        act.activation(hid_g[:, r % 2, :], HIDDEN[r % 2], ACT.Silu).then_inc(sem["hid_g"], 1)

                keep_x_t(0, 0)
                all_tiles(act, step)

            def gap_exp_of(l):
                act.wait_ge(sem[f"gap{l}"], base[f"gap{l}"] + 1)
                act.activation(gap_exp[:, :], gap[:, :], ACT.Exp).then_inc(sem[f"gap_exp{l}"], 1)

            def mix1(l, b):
                act.wait_ge(sem[f"pair_in{l}_{b % 2}"], base[f"pair_in{l}_{b % 2}"] + 32 * (b // 2 + 1))
                act.wait_ge(sem[f"weights{l}"], base[f"weights{l}"] + 1)
                for k in range(KT):
                    at_least(act, sem[f"mixed{l}"], 2 * (b - 1) + k + 1, base[f"mixed{l}"])
                    act.activation(y_mix[:, k, :], y_pair[:, b % 2, 0, k], ACT.Copy, scale=weight[:, 0, b * KT + k:b * KT + k + 1])\
                       .then_inc(sem[f"mix1_{l}"], 1)

            for r in range(2):
                act.wait_ge(sem[f"y_out0_{r}"], 128 * (NB // 2))
            b2 = ins["b2"].rearrange("(a e) c -> a (e c)", a=1)
            act.dma_start(B2[:, :, :].rearrange("p e c -> p (e c)"), b2.broadcast_to((P, E * C))).then_inc(sem["experts0_in"], 16)
            gap_exp_of(0)
            expert_tiles(0)
            act.wait_ge(sem["y_ps0"], TILES)
            act.wait_ge(sem["w_now0"], TILES)
            act.dma_start(W1[:, :, :], ins["gate_w"].rearrange("e c f -> c e f")).then_inc(sem["experts1_in"], 16)
            act.dma_start(W2[:, :, :, :], ins["down_w"].rearrange("e (k p) c -> p e k c", p=P)).then_inc(sem["experts1_in"], 16)

            for s in STEPS[1]:
                b = stages(1, s)
                a, m, w, z, y = b["front"], b["scores"], b["probs"], b["back"], b["route"]
                if a is not None:
                    modulate(1, a)
                if 0 <= s - 2 < NB:
                    act.wait_ge(sem["max_t_ps"], s - 1)
                    at_least(act, sem[f"max_out{s % 2}"], 16 * ((s - 2) // 2))
                    act.copy(max_t[0:2 * H, s % 2, :], P1[0:2 * H, 0:P].bitcast(BF16)).then_inc(sem["max_t"], 1)
                if a is not None:
                    first_part(1, a)
                if z is not None:
                    keep_mod(1, z, P1)

                def keep_v():
                    act.wait_ge(sem["v_ps1"], base["v_ps1"] + a + 1)
                    if a == 0:
                        act.wait_ge(sem["v_ones"], 1)
                    at_least(act, sem["pv1"], 12 * cnt(a - 4))
                    act.copy(V[:, a % 4, :, 0:9 * H].rearrange("p k (h e) -> p k h e", e=9)[:, :, :, 0:HD],
                             P1[:, 0:T].rearrange("p (k h d) -> p k h d", k=KT, d=HD)).then_inc(sem["v1"], 1)

                for g in range(12):
                    if w is not None:
                        act.wait_ge(sem["scores_exp"], 12 * w + g + 1)
                        at_least(act, sem["pv1"], 12 * w + g - 3)
                        act.activation(probs[:, g % 4, :], half_bank(g), ACT.Exp, scale=float(HD) ** -0.5)\
                           .then_inc(sem["exped"], 1)
                    if g == 0 and a is not None:
                        keep_v()
                    if g == 1 and a is not None:
                        second_part(1, a)
                    if g in (7,) and w is not None:
                        act.wait_ge(sem["pv1"], 12 * w + 6)
                        at_least(act, sem[f"y_out1_{w % 2}"], 64 * (w // 2), base[f"y_out1_{w % 2}"])
                        act.copy(y_pad[:, w % 2, 0:512], Y0[:, :]).then_inc(sem["y_pad1"], 1)
                    if g == 9 and y is not None:
                        keep_h2(1, y)
                if w is not None:
                    act.wait_ge(sem["pv1"], 12 * w + 12)
                    act.copy(y_pad[:, w % 2, 512:1024], P2[:, :]).then_inc(sem["y_pad1"], 1)
                if s == -1:
                    mix1(0, 0)
                    mix1(0, 1)
                elif s + 2 < NB:
                    mix1(0, s + 2)
                if 0 <= s - 4 < NB:
                    make_diag(1, s - 4)

            gap_exp_of(1)
            expert_tiles(1)
            for b in range(NB):
                mix1(1, b)

        @block.gpsimd
        def _(gp):
            def inverse_root(l, which, b):
                gp.wait_ge(sem[f"var{l}_{which}"], base[f"var{l}_{which}"] + b + 1)
                gp.tensor_tensor(rstd[:, which, :], var_eps[:, which, :], half_neg[:, :], ALU.pow)\
                  .then_inc(sem[f"rstd{l}_{which}"], 1)

            def modulate_rows(l, b):
                gp.wait_ge(sem[f"xh{l}_1"], base[f"xh{l}_1"] + 2 * (b + 1))
                gp.wait_ge(sem[f"mod_bc{l}"], base[f"mod_bc{l}"] + b + 1)
                wide = lambda k: mod_bc[:, b % 4, k * C:(k + 1) * C].unsqueeze(1).broadcast_to((P, KT, C))
                at_least(gp, sem[f"h_stored{l}_{b % 2}"], 16 * (b // 2), base[f"h_stored{l}_{b % 2}"])
                at_least(gp, sem[f"h2_ps{l}"], cnt(b - 2), base[f"h2_ps{l}"])
                gp.tensor_tensor(h_tmp[:, :, :], xh[:, 1, b % 2], wide(2), ALU.mult).then_inc(sem[f"h_mul{l}"], 1)
                gp.wait_ge(sem[f"h_mul{l}"], base[f"h_mul{l}"] + b + 1)
                gp.tensor_tensor(h_tok[:, b % 2], h_tmp[:, :, :], wide(1), ALU.add).then_inc(sem[f"h_tok{l}"], 2)

            def scale_w_out(l, b):
                if b == 0 and l == 0:
                    gp.wait_ge(sem["late_in"], 16 * 5)
                if b == 0 and l == 1:
                    gp.wait_ge(sem["w1_in"], 48)
                gp.wait_ge(sem[f"mod_bc{l}"], base[f"mod_bc{l}"] + b + 1)
                at_least(gp, sem[f"out_ps{l}"], cnt(b - 2), base[f"out_ps{l}"])
                gp.tensor_tensor(w_out[:, b % 2, :], w_proj[:, :], mod_bc[:, b % 4, 0:C], ALU.mult).then_inc(sem[f"w_out{l}"], 1)

            def rest0(b):
                gp.wait_ge(sem["part1_0"], b + 1)
                gp.tensor_tensor(rest[:, b % 2, :], qk[:, b % 3, :], parts[:, b % 2, 0, :], ALU.subtract).then_inc(sem["rest1_0"], 1)

            def third_part(l, b):
                gp.wait_ge(sem[f"part2_{l}"], base[f"part2_{l}"] + b + 1)
                gp.tensor_tensor(parts[:, b % 2, 2, :], rest[:, b % 2, :], parts[:, b % 2, 1, :], ALU.subtract)\
                  .then_inc(sem[f"part3_{l}"], 1)

            gp.wait_ge(sem["half_neg"], 1)
            inverse_root(0, 0, 0)
            for r in range(STACKS - 1):
                gp.memset(stack_k[:, r, :].bitcast(F32), 0.0).then_inc(sem["pool_rows"], 1)
            gp.memset(ones_b[:, :], 1.0).then_inc(sem["bf16_consts"], 1)
            gp.wait_ge(sem["consts_in"], 16)
            for dst, name in ((before_b, "before"), (iota_b, "iota"), (ident_b, "ident")):
                gp.tensor_copy(dst[:, :], const(name)).then_inc(sem["bf16_consts"], 1)
            gp.memset(neg_mask[:, :], 0.0).then_inc(sem["neg_mask"], 1)
            gp.wait_ge(sem["neg_mask"], 1)
            gp.affine_select(out=neg_mask[:, :], in_=neg_mask[:, :], compare_op=ALU.is_ge, fill=-1e30, base=0,
                             pattern=[[-1, P]], channel_multiplier=1).then_inc(sem["neg_mask"], 1)

            for s in STEPS[0]:
                b = stages(0, s)
                a, m, z, y, n = b["front"], b["scores"], b["back"], b["route"], b["next"]
                if y is not None:
                    modulate_rows(0, y)
                if a is not None:
                    gp.wait_ge(sem["rot_a"], a + 1)
                    gp.wait_ge(sem["rot_b"], a + 1)
                    at_least(gp, sem["y_state_ps"], cnt(a - 3))
                    gp.tensor_tensor(qk[:, a % 3, :], rot[:, 0], rot[:, 1], ALU.add).then_inc(sem["qk0"], 1)
                if z is not None:
                    gp.wait_ge(sem["gn_var"], z + 1)
                    gp.tensor_tensor(gn_rstd[:, :], gn_ve[:, 1:2], half_neg[:, 0:1], ALU.pow).then_inc(sem["gn_rstd"], 1)
                if a is not None:
                    gp.wait_ge(sem["qk0"], a + 1)
                    rest0(a)
                if z is not None:
                    scale_w_out(0, z)
                    gp.wait_ge(sem["y_n"], z + 1)
                    gp.wait_ge(sem["gated0"], z + 1)
                    at_least(gp, sem["out_ps0"], cnt(z - 2))
                    gp.tensor_tensor(o_t[:, z % 2, :], y_n[:, :], sgate[:, z % 6, :], ALU.mult).then_inc(sem["o_t0"], 1)
                if a is not None:
                    gp.wait_ge(sem["rest1_0"], a + 1)
                    third_part(0, a)
                if z is not None:
                    inverse_root(0, 1, z)
                if n is not None and n > 0:
                    inverse_root(0, 0, n)

            def expert_tiles(l):
                def gather(n):
                    at_least(gp, sem[f"x_t_e_ps{l}"], n - RING + 1, base[f"x_t_e_ps{l}"])
                    gp.indirect_dma_start(out=x_rows[:, n % RING, :], out_offset=None, in_=h_d[l],
                                          in_offset=bass.IndirectOffsetOnAxis(ap=src_row[:, n:n + 1], axis=0))\
                      .then_inc(sem[f"gathered{n % RING}_{l}"], 16)

                def scatter(n):
                    gp.wait_ge(sem[f"y_rows{l}"], base[f"y_rows{l}"] + n + 1)
                    gp.indirect_dma_start(out=ye_d[l], out_offset=bass.IndirectOffsetOnAxis(ap=dst_row[:, n:n + 1], axis=0),
                                          in_=y_rows[:, n % RING, :], in_offset=None)\
                      .then_inc(sem[f"scattered{n % RING}_{l}"], 16)

                gp.wait_ge(sem[f"src_row{l}"], base[f"src_row{l}"] + 1)
                for r in range(2):
                    gp.wait_ge(sem[f"h_stored{l}_{r}"], base[f"h_stored{l}_{r}"] + 16 * (NB // 2))
                for n in range(RING):
                    gather(n)
                gp.wait_ge(sem[f"dst_row{l}"], base[f"dst_row{l}"] + 1)
                for n in range(TILES):
                    if n >= 1 and n + RING - 1 < TILES:
                        gather(n + RING - 1)
                    scatter(n)

            def mix3(l, b):
                gp.wait_ge(sem[f"mixed{l}"], base[f"mixed{l}"] + 2 * (b + 1))
                at_least(gp, sem[f"mixed_x{l}"], b, base[f"mixed_x{l}"])
                gp.tensor_tensor(y_mix3[:, :, :], y_mix2[:, :, :], gb_bc[:, b, :].unsqueeze(1).broadcast_to((P, KT, C)),
                                 ALU.mult).then_inc(sem[f"mix3_{l}"], 1)

            expert_tiles(0)
            gp.memset(V[:, :, :, :], 1.0).then_inc(sem["v_ones"], 1)

            for s in STEPS[1]:
                b = stages(1, s)
                a, w, z, y, n = b["front"], b["probs"], b["back"], b["route"], b["next"]
                if y is not None:
                    modulate_rows(1, y)
                if s == 1:
                    gp.memset(stack_q[:, STACKS - 1, :].bitcast(F32), 0.0).then_inc(sem["pool_rows"], 1)
                    gp.memset(stack_k[:, STACKS - 1, :].bitcast(F32), 0.0).then_inc(sem["pool_rows"], 1)
                    gp.wait_ge(sem["pool_rows"], STACKS + 1)
                    gp.memset(stack_k[MAX_ROW:MAX_ROW + 2, STACKS - 1, :], 1.0).then_inc(sem["pool_rows"], 1)
                    gp.wait_ge(sem["pool_rows"], STACKS + 2)
                for g in range(12):
                    if w is not None:
                        gp.wait_ge(sem["exped"], 12 * w + g + 1)
                        _, s0, t0, cols = exp_cells(g)[0]
                        cells = probs[:, g % 4, :].rearrange("p (n t) -> p n t", t=cols)[:, :, 0:P]
                        gp.affine_select(out=cells, in_=cells, compare_op=ALU.is_ge, fill=0.0, base=0,
                                         pattern=[[0, 512 // cols], [1, P]], channel_multiplier=-1)\
                          .then_inc(sem["probs_causal"], 1)
                    if g == 2 and z is not None:
                        scale_w_out(1, z)
                        gp.wait_ge(sem[f"den_in{z % 2}"], 16 * (z // 2 + 1))
                        gp.wait_ge(sem[f"y_in1_{z % 2}"], base[f"y_in1_{z % 2}"] + 32 * (z // 2 + 1))
                        at_least(gp, sem["out_ps1"], cnt(z - 2), base["out_ps1"])
                        gp.tensor_tensor(o_t[:, z % 2, :], y_t[:, z % 3, :], den_bc[:, z % 2, :], ALU.mult).then_inc(sem["o_t1"], 1)
                    if g == 4 and a is not None:
                        third_part(1, a)
                    if g == 9 and z is not None:
                        inverse_root(1, 1, z)
                if s == -1:
                    mix3(0, 0)
                    inverse_root(1, 0, 0)
                    mix3(0, 1)
                if n is not None and n > 0:
                    if n + 1 < NB:
                        mix3(0, n + 1)
                    inverse_root(1, 0, n)

            expert_tiles(1)
            for b in range(NB):
                mix3(1, b)


def kernel(**inputs):
    import concourse.bacc as bacc
    from concourse.bass_utils import run_bass_kernel_spmd

    a = {k: np.asarray(v) for k, v in inputs.items()}
    pair_swap = np.arange(C) ^ 1
    w_qkv = a["L0_attn_w_qkv"]
    q_w, k_w, v_w = w_qkv[0:C], w_qkv[C:2 * C], w_qkv[2 * C:]
    order, swapped = D_MAJOR, pair_swap[D_MAJOR]
    consts, rotary = shape_constants()
    arrays = {
        "x": a["L0_attn_x"],
        "consts": consts, "rotary": rotary,
        "c_t0": a["L0_c"].T, "c_t1": a["L1_c"].T,
        "wmod0": a["L0_wmod"], "wmod1": a["L1_wmod"],
        "w_qk0": np.concatenate([q_w[order].T, k_w[order].T], 1),
        "w_qks": np.concatenate([q_w[swapped].T, k_w[swapped].T], 1),
        "w_v0": v_w.T,
        "w_gate": a["L0_attn_w_gated"][order].T,
        "w_proj0": a["L0_attn_w_proj"].T[order],
        "gn": np.stack([a["L0_attn_gn_weight"][order], a["L0_attn_gn_bias"][order]], 1),
        "router_w0": a["L0_ffn_Wg"],
        "w1": a["L0_ffn_W1"], "b1": a["L0_ffn_b1"].reshape(E, FK, P).transpose(2, 0, 1), "w2": a["L0_ffn_W2"], "b2": a["L0_ffn_b2"],
        "w_qk1": np.concatenate([a["L1_attn_Wq"][order].T, a["L1_attn_Wk"][order].T], 1),
        "w_v1": a["L1_attn_Wv"].T,
        "w_proj1": a["L1_attn_Wo"].T[order],
        "router_w1": a["L1_ffn_router_w"].T, "router_b": a["L1_ffn_router_b"],
        "gate_w": a["L1_ffn_gate_w"].transpose(0, 2, 1),
        "up_w": a["L1_ffn_up_w"].transpose(0, 2, 1),
        "down_w": a["L1_ffn_down_w"].transpose(0, 2, 1),
    }
    arrays = {k: np.ascontiguousarray(v) for k, v in arrays.items()}
    nc = bacc.Bacc("TRN2", target_bir_lowering=False, num_devices=1)
    ins = {k: nc.dram_tensor(f"in_{k}", v.shape, mybir.dt.from_np(v.dtype), kind="ExternalInput").ap()
           for k, v in arrays.items()}
    out = nc.dram_tensor("out_x", (NB, T, C), F32, kind="ExternalOutput").ap()
    adaln_layers(nc, ins, out)
    r = run_bass_kernel_spmd(nc, [{f"in_{k}": v for k, v in arrays.items()}], core_ids=[0])
    return r.results[0]["out_x"]
```

```python
from contextlib import ExitStack

import numpy as np

import concourse.bass as bass
from concourse import mybir

F32 = mybir.dt.float32
BF16 = mybir.dt.bfloat16
I32 = mybir.dt.int32
U32 = mybir.dt.uint32
ALU = mybir.AluOpType
ACT = mybir.ActivationFunctionType
AX_X = mybir.AxisListType.X

P = 128
NB, T, C = 8, 256, 128
H, HD = 16, 8
E, F = 8, 512
TOK = NB * T
NT = TOK // P
KT = T // P
FK = F // P
CHOICES = 2
TILES = (CHOICES * TOK + E * (P - 1)) // P
RING = 4
PEEL = TILES % RING + RING
TURNS = (TILES - PEEL) // RING - 1
EPS = 1e-5
FLOOR = 0.25
BIG = 3.0e38
PARTS = 3
MAX_ROW = 96
LAST_LOADS = 4
LANES = 4
STACKS = 4
TWO_ONES = float(np.array([0x3F803F80], np.uint32).view(np.float32)[0])

CONST_COLS = [("ident", P), ("causal", P), ("same_head", P),
              ("head_avg", P), ("before", P), ("iota", P), ("expert_id", P), ("restart", P),
              ("steps128", 16), ("trash", TILES), ("tile_id", 32), ("pid1", 1)]
CONST_AT, _o = {}, 0
for _n, _w in CONST_COLS:
    CONST_AT[_n] = (_o, _o + _w)
    _o += _w
CONST_N = _o
D_MAJOR = np.arange(C).reshape(H, HD).T.reshape(-1)


def shape_constants():
    out = np.zeros((P, CONST_N), np.float64)
    rotary = np.zeros((2, P, 2 * T), np.float64)

    def put(name, value):
        a, b = CONST_AT[name]
        out[:, a:b] = value

    p = np.arange(P)
    d, h = p // H, p % H
    half = np.arange(0, HD, 2)
    inv_freq = 1.0 / 10000.0 ** (half / HD)
    t = np.arange(T)
    angle = t[None, :] * inv_freq[d // 2][:, None]
    scale = ((half + 0.4 * HD) / (1.4 * HD))[d // 2][:, None] ** ((t - T // 2) / 512.0)[None, :]
    gamma = (1.0 - 2.0 ** (-5.0 - h))[:, None]
    q_side = scale * gamma ** (t - P)[None, :] * HD ** -0.5
    k_side = gamma ** (P - t)[None, :] / scale
    sign = np.where(d % 2 == 0, -1.0, 1.0)[:, None]
    rotary[0] = np.concatenate([np.cos(angle) * q_side, np.cos(angle) * k_side], 1)
    rotary[1] = np.concatenate([sign * np.sin(angle) * q_side, sign * np.sin(angle) * k_side], 1)
    put("ident", np.eye(P))
    put("causal", p[:, None] <= p[None, :])
    put("same_head", h[:, None] == h[None, :])
    put("head_avg", (h[:, None] == h[None, :]) / HD)
    put("before", p[:, None] < p[None, :])
    put("iota", p[None, :])
    put("expert_id", (p // NT)[None, :])
    put("restart", (p % NT != 0)[None, :])
    put("steps128", (P * np.arange(16))[None, :])
    put("trash", CHOICES * TOK + 1 + P * np.arange(TILES)[None, :] + p[:, None])
    put("tile_id", np.arange(2 * NT)[None, :])
    put("pid1", (p + 1)[:, None])
    return out.astype(np.float32), rotary.astype(np.float32)


LAYER0_TOTAL = {
    **dict.fromkeys(("x_t_ps", "h_t", "v_ps", "x_mid", "out_ps", "w_out", "o_t", "h_mul",
                     "h2_ps", "h2_t", "logits_ps", "logits", "qk_ps", "part1_", "rest1_", "part2_", "part3_", "var", "rstd",
                     "mix3_", "mixed_x", "v_"), NB),
    **dict.fromkeys(("stats", "mv", "xh", "h_tok", "y_pad", "mix1_", "mixed"), 2 * NB),
    **dict.fromkeys(("x_t", "x_t_e_ps", "hidden_ps", "act_hid", "hid_t", "y_ps", "y_rows"), TILES),
    "w_now": 2 * TILES, "w2_now": 2 * TILES,
    **{f"{way}{r}": 16 * ((TILES - r + RING - 1) // RING) for way in ("gathered", "scattered") for r in range(RING)},
    **dict.fromkeys(("ranks_ps", "counts_ps", "total_b", "picked_b", "tiles_before_b", "src_row", "dst_row", "tile_exp",
                     "gap_exp", "weights"), 1),
    "gap": 4,
    "pv_": 4 * NB, "slot_ps": CHOICES * NT, "hot_lane": CHOICES * NT, "hot_vals": 2, "gb_bc": 16,
    **{f"mod_bc{r}": 16 * NB // 4 for r in range(4)},
    "h_stored": 16 * NB // 2, "parts_out": 16 * NB // 2, "stacked": 96 * NB // 2, "pair_in": 32 * NB // 2,
    "y_out": 64 * NB // 2, "y_in": 16 * NB // 2,
}


def exists(n):
    return not isinstance(n, int) or 0 <= n < TILES


def all_tiles(eng, step):
    for n in range(PEEL):
        step(n, n % RING, n // RING)
    with eng.Fori(0, TURNS) as i:
        for u in range(PEEL, PEEL + RING):
            step(i * RING + u, u % RING, i + u // RING)
    for n in range(TILES - RING, TILES):
        step(n, n % RING, n // RING)


def split_layer(name):
    for at in (-1, -3):
        for base in (name[:at], name[:at - 1]):
            if base in LAYER0_TOTAL and name[at] in "01":
                return base, int(name[at]), name[at:][1:]
    return name, 0, ""


class Named(dict):

    def __init__(self, make):
        super().__init__()
        self.make = make

    def __missing__(self, name):
        self[name] = self.make(name)
        return self[name]


def at_least(eng, sem, count, base=0):
    if not isinstance(count, int) or count > 0:
        eng.wait_ge(sem, count + base)


def cnt(b):
    return max(0, min(b + 1, NB))


def adaln_layers(nc, ins, out):
    ctx = ExitStack()
    with ctx:
        def sb(name, shape, dt=F32):
            return ctx.enter_context(nc.sbuf_tensor(name, [P] + shape, dt))

        def dram(name, shape, dt=F32):
            return nc.dram_tensor(name, shape, dt, kind="Internal").ap()

        handle = Named(lambda name: ctx.enter_context(nc.semaphore(name)))
        sem = Named(lambda name: handle["%s%s" % split_layer(name)[::2]])
        base = Named(lambda name: LAYER0_TOTAL[split_layer(name)[0]] * split_layer(name)[1]
                     if split_layer(name)[0] in LAYER0_TOTAL else 0)

        X = sb("X", [NT, C])
        consts = sb("consts", [CONST_N])
        c_t = sb("c_t", [2, NB])
        sc_t = sb("sc_t", [2, NB])
        mod_pad = sb("mod_pad", [P])
        mod_t = mod_pad[:, 0:2 * 6 * NB].rearrange("p (l k b) -> p l k b", l=2, k=6)
        mod_rows = sb("mod_rows", [C])
        ones = sb("ones", [P])
        ones_b = sb("ones_b", [P], BF16)
        before_b = sb("before_b", [P], BF16)
        iota_b = sb("iota_b", [P], BF16)
        ident_b = sb("ident_b", [P], BF16)
        tile_id_b = sb("tile_id_b", [CHOICES * NT], BF16)
        half_neg = sb("half_neg", [2])
        w_qk = sb("w_qk", [2 * C])
        w_v = sb("w_v", [C])
        w_proj = sb("w_proj", [C])
        gn = sb("gn", [2])
        router_w = sb("router_w", [2, E])
        router_b = sb("router_b", [E])
        W1 = sb("W1", [E, F])
        W_up = sb("W_up", [E, F])
        B1 = sb("B1", [E, FK])
        b_now = sb("b_now", [RING, FK])
        W2 = sb("W2", [E, FK, C])

        stats = sb("stats", [2, KT, 6])
        mv = sb("mv", [2, KT, 2])
        var_eps = sb("var_eps", [2, KT])
        rstd = sb("rstd", [2, KT])
        xh = sb("xh", [2, 2, KT, C])
        h_t = sb("h_t", [2, T])
        h_tok = sb("h_tok", [2, KT, C])
        h2_t = sb("h2_t", [T])
        rot = sb("rot", [2, 2 * T])
        qk = sb("qk", [3, 2 * T])
        rest = sb("rest", [2, 2 * T])
        parts = sb("parts", [2, PARTS, 2 * T], BF16)
        stack_q = sb("stack_q", [STACKS, H * T], BF16)
        stack_k = sb("stack_k", [STACKS, H * T], BF16)
        V = sb("V", [5, KT, H * 9 + 24])
        probs = sb("probs", [4, 512])
        y_pad = sb("y_pad", [2, 4 * T])
        y_t = sb("y_t", [3, T])
        gn_stats = sb("gn_stats", [6])
        gn_mv = sb("gn_mv", [2])
        gn_avg = sb("gn_avg", [2])
        gn_ve = sb("gn_ve", [2])
        gn_rstd = sb("gn_rstd", [1])
        gn_ab = sb("gn_ab", [2])
        y_n = sb("y_n", [T])
        o_t = sb("o_t", [2, T])
        mod_bc = sb("mod_bc", [4, 3 * C])
        gb_bc = sb("gb_bc", [NB, C])
        w_out = sb("w_out", [2, C])
        row_max = sb("row_max", [KT, H])
        max_parts = sb("max_parts", [2, KT, 2 * H], BF16)
        den = sb("den", [2, 2 * H])
        den_inv = sb("den_inv", [2, 2 * H])

        logits = sb("logits", [E, NT])
        r_max = sb("r_max", [NT])
        r_min = sb("r_min", [NT])
        r_max2 = sb("r_max2", [NT])
        gap = sb("gap", [NT])
        gap_exp = sb("gap_exp", [NT])
        gap_den = sb("gap_den", [NT])
        weight = sb("weight", [CHOICES, NT])
        picked_b = sb("picked_b", [E, NT], BF16)
        tiles_before_b = sb("tiles_before_b", [E, NT], BF16)
        total_b = sb("total_b", [E], BF16)
        over = sb("over", [E, 16])
        n_tiles = sb("n_tiles", [E])
        tile_end = sb("tile_end", [E])
        tile_start = sb("tile_start", [E])
        slot = sb("slot", [CHOICES * NT])
        slot_i = sb("slot_i", [CHOICES * NT], I32)
        tile_i = sb("tile_i", [CHOICES * NT], I32)
        lane_i = sb("lane_i", [CHOICES * NT], I32)
        slot_tile = sb("slot_tile", [CHOICES * NT], BF16)
        slot_lane = sb("slot_lane", [CHOICES * NT], BF16)
        tile_exp_f = sb("tile_exp_f", [TILES])
        tile_exp = sb("tile_exp", [TILES], I32)
        ident_lo = sb("ident_lo", [TILES])
        ident_all = sb("ident_all", [TILES])
        empty = sb("empty", [TILES])
        empty_at = sb("empty_at", [TILES])
        wrap = sb("wrap", [TILES])
        src_f = sb("src_f", [TILES])
        src_row = sb("src_row", [TILES], U32)
        dst_row = sb("dst_row", [TILES], U32)

        h_tmp = sb("h_tmp", [KT, C])
        gate_tmp = sb("gate_tmp", [3, 2 * 2, NB])
        neg_mask = sb("neg_mask", [P], BF16)

        def guests(host, host_dt, layout):
            axes = "abcd"[:len(host.shape) - 1]
            flat = host[(slice(None),) * len(host.shape)]
            if len(axes) > 1:
                flat = flat.rearrange(f"p {' '.join(axes)} -> p ({' '.join(axes)})")
            if host_dt == BF16:
                flat = flat.bitcast(F32)
            views, at = [], 0
            for shape, dt in layout:
                words = int(np.prod(shape)) // (2 if dt == BF16 else 1)
                v = flat[:, at:at + words]
                at += words
                v = v.bitcast(dt) if dt != F32 else v
                if len(shape) > 1:
                    names = [f"n{i}" for i in range(len(shape))]
                    v = v.rearrange(f"p ({' '.join(names)}) -> p {' '.join(names)}", **dict(zip(names, shape)))
                views.append(v)
            return views

        (mod_w,) = guests(stack_q[:, STACKS - 1, :], BF16, [([2, 6 * C], F32)])
        sgate, y_state = guests(stack_q[:, STACKS - 1, :], BF16, [([6, T], F32), ([3, P], F32)])
        (w_now,) = guests(stack_q[:, STACKS - 1, :], BF16, [([2, 2, F], F32)])
        hid_t, hid_g = guests(stack_k[:, STACKS - 1, :], BF16, [([2, F], F32)] * 2)
        rotary, w_qks, w_gate, state, k_tok = guests(
            stack_k[:, STACKS - 1, :], BF16, [([2, 2 * T], F32), ([2 * C], F32), ([C], F32), ([C], F32), ([C], F32)])
        y_mix, y_mix2, y_mix3, den_bc, max_t = guests(
            qk, F32, [([KT, C], F32)] * 3 + [([2, T], F32), ([2, T], BF16)])
        w2_now, b2_now = guests(qk, F32, [([2, FK, C], F32), ([2, C], F32)])
        (y_pair,) = guests(rot, F32, [([2, CHOICES, KT, C], F32)])
        (last_pair,) = guests(stack_q[:, 0:2, :], BF16, [([CHOICES, NT, C], F32)])
        last_mix1, last_mix2, last_mix3 = guests(stack_k[:, 0:3, :], BF16, [([NT, C], F32)] * 3)
        (hot_vals,) = guests(parts, BF16, [([CHOICES * NT, 2, TILES], BF16)])
        (hot_lane,) = guests(rot, F32, [([4 * LANES, P], BF16)])
        hot_tile, ended = guests(rest, F32, [([CHOICES * NT, TILES], BF16), ([TILES, E], F32)])
        x_rows, y_rows, x_t, r_eq, r_idx, second, picked, upto = guests(
            probs, F32, [([RING, C], F32), ([RING, C], F32), ([2, P], F32)] + [([E, NT], F32)] * 5)
        B2, pick, place, place_c = guests(y_pad, F32, [([E, C], F32), ([CHOICES, E, NT], F32)] + [([E, NT], F32)] * 2)

        bank = [ctx.enter_context(nc.psum_tensor(f"bank{i}", [P, 512], F32)) for i in range(4)]
        pair = [ctx.enter_context(nc.psum_tensor(f"pair{i}", [P, 1024], F32)) for i in range(2)]
        P0, P1, P2, Y0 = bank
        HIDDEN = P1[:, :], P2[:, :]
        UP = Y0[:, :], pair[0][:, 0:512]
        Y_ROWS = pair[0][:, 512:512 + C], pair[1][:, 0:C]

        parts_d = dram("parts_d", [2, 2, PARTS, 2, HD, H * T], BF16)
        y_d = dram("y_d", [2, 2, HD + 1, H, T])
        den_d = dram("den_d", [2, H, T])
        max_d = dram("max_d", [2, 2 * H, T], BF16)
        mod_d = dram("mod_d", [P, C])
        h_d = [dram(f"h_d{l}", [TOK, C]) for l in range(2)]
        ye_d = [dram(f"ye_d{l}", [CHOICES * TOK + TILES * P, C]) for l in range(2)]

        def const(name):
            a, b = CONST_AT[name]
            return consts[:, a:b]

        block = ctx.enter_context(nc.Block())

        def exp_cells(g):
            gp, i6 = g // 6, g % 6
            if i6 < 4:
                return [(8 * gp + 2 * i6 + n, 0, 0, T) for n in range(2)]
            return [(8 * gp + 4 * (i6 - 4) + n, P, P, P) for n in range(4)]

        def half_bank(g):
            return pair[1][:, (g % 2) * 512:(g % 2 + 1) * 512]

        LAG = {0: dict(scores=2, back=4, route=5, last=6), 1: dict(scores=2, max_rows=3, probs=4, dens=5, back=6, route=7, last=7)}

        def stages(l, s):
            got = {"front": s, "next": s + 1} | {k: s - v for k, v in LAG[l].items()}
            got["logits"] = s - LAG[l]["route"] - 1
            return {k: (b if 0 <= b < NB else None) for k, b in got.items()}

        STEPS = {l: range(-1, NB + LAG[l]["last"]) for l in range(2)}

        @block.sync
        def _(sp):
            xv = ins["x"].rearrange("b (k p) c -> p (b k) c", p=P)
            sp.dma_start(X[:, 0:KT, :], xv[:, 0:KT, :]).then_inc(sem["x_in0"], 16)
            for l in range(2):
                sp.dma_start(mod_w[:, l, :], ins[f"wmod{l}"]).then_inc(sem["mod_in"], 16)
            sp.dma_start(consts[:, :], ins["consts"]).then_inc(sem["consts_in"], 16)
            sp.dma_start(w_qk[:, :], ins["w_qk0"]).then_inc(sem["attn_in"], 16)
            sp.dma_start(w_qks[:, :], ins["w_qks"]).then_inc(sem["attn_in"], 16)
            sp.dma_start(w_v[:, :], ins["w_v0"]).then_inc(sem["attn_in"], 16)
            sp.dma_start(w_gate[:, :], ins["w_gate"]).then_inc(sem["attn_in"], 16)
            sp.dma_start(rotary[:, :, :], ins["rotary"].rearrange("a p t -> p a t")).then_inc(sem["rotary_in"], 16)
            sp.dma_start(X[:, KT:NT, :], xv[:, KT:NT, :]).then_inc(sem["x_in1"], 16)
            sp.dma_start(w_proj[:, :], ins["w_proj0"]).then_inc(sem["late_in"], 16)
            sp.dma_start(gn[:, :], ins["gn"]).then_inc(sem["late_in"], 16)
            sp.dma_start(router_w[:, 0, :], ins["router_w0"]).then_inc(sem["late_in"], 16)
            sp.dma_start(router_w[:, 1, :], ins["router_w1"]).then_inc(sem["late_in"], 16)
            sp.dma_start(router_b[:, :], ins["router_b"].rearrange("(a e) -> a e", a=1).broadcast_to((P, E)))\
              .then_inc(sem["late_in"], 16)
            def store_h(l, b):
                sp.wait_ge(sem[f"h_tok{l}"], base[f"h_tok{l}"] + 2 * (b + 1))
                sp.dma_start(h_d[l][b * T:(b + 1) * T, :].rearrange("(k p) c -> p k c", p=P), h_tok[:, b % 2])\
                  .then_inc(sem[f"h_stored{l}_{b % 2}"], 16)

            def store_parts(l, b):
                sp.wait_ge(sem[f"part3_{l}"], base[f"part3_{l}"] + b + 1)
                d = parts_d[l, b % 2]
                at_least(sp, sem[f"stacked{l}_{b % 2}"], 96 * (b // 2), base[f"stacked{l}_{b % 2}"])
                sp.dma_start(d.rearrange("a s d (h t) -> (d h) (a s) t", t=T),
                             parts[:, b % 2, :, :].rearrange("p a (s t) -> p (a s) t", s=2))\
                  .then_inc(sem[f"parts_out{l}_{b % 2}"], 16)

            def load_stacks(l, b):
                d = parts_d[l, b % 2]
                sp.wait_ge(sem[f"parts_out{l}_{b % 2}"], base[f"parts_out{l}_{b % 2}"] + 16 * (b // 2 + 1))
                if l == 0 and b < STACKS - 1:
                    sp.wait_ge(sem[f"stack_q_set"], b + 1)
                    sp.wait_ge(sem[f"stack_k_set"], b + 1)
                if l == 1 and b == STACKS - 1:
                    sp.wait_ge(sem["stack_q_set"], STACKS)
                    sp.wait_ge(sem["stack_k_set"], STACKS)
                if l == 0:
                    at_least(sp, sem["scores0"], 4 * cnt(b - 3))
                else:
                    at_least(sp, sem["scores_exp"], 12 * cnt(b - STACKS))
                r = b % (3 if l == 0 else STACKS)
                row = 0
                for k_part, n in ((0, 3), (1, 2), (2, 1)):
                    sp.dma_start(stack_q[row:row + n * HD, r, :], d[0:n, 0].rearrange("n d f -> d n f"))\
                      .then_inc(sem[f"stacked{l}_{b % 2}"], 16)
                    k_src = d[k_part, 1]
                    if n > 1:
                        k_src = k_src.unsqueeze(1).broadcast_to((HD, n, H * T))
                    sp.dma_start(stack_k[row:row + n * HD, r, :], k_src)\
                      .then_inc(sem[f"stacked{l}_{b % 2}"], 16)
                    row += n * HD

            def unpad_y(l, b):
                sp.wait_ge(sem[f"y_pad{l}"], base[f"y_pad{l}"] + 2 * (b + 1))
                rows = HD + (l == 1)
                if l == 0:
                    at_least(sp, sem[f"y_in0_{b % 2}"], 16 * (b // 2))
                else:
                    at_least(sp, sem[f"y_in1_{b % 2}"], 32 * (b // 2), base[f"y_in1_{b % 2}"])
                for j in range(4):
                    dst = y_d[l, b % 2, 0:rows].rearrange("d (g j) t -> j d g t", j=4)[j]
                    src = y_pad[32 * j:32 * j + rows, b % 2, :]
                    sp.dma_start(dst, src.rearrange("d (g t) -> d g t", g=4)).then_inc(sem[f"y_out{l}_{b % 2}"], 16)

            def load_y(l, b):
                sp.wait_ge(sem[f"y_out{l}_{b % 2}"], base[f"y_out{l}_{b % 2}"] + 64 * (b // 2 + 1))
                at_least(sp, sem[f"o_t{l}"], cnt(b - 3), base[f"o_t{l}"])
                sp.dma_start(y_t[:, b % 3, :], y_d[l, b % 2, 0:HD].rearrange("d h t -> (d h) t"))\
                  .then_inc(sem[f"y_in{l}_{b % 2}"], 16)
                if l == 1:
                    at_least(sp, sem["den_inv"], cnt(b - 2))
                    sp.dma_start(den[:, b % 2, :], y_d[l, b % 2, HD].rearrange("h (a t) -> (h a) t", t=2 * H))\
                      .then_inc(sem[f"y_in1_{b % 2}"], 16)

            def spread_den(b):
                sp.wait_ge(sem["den_inv"], b + 1)
                at_least(sp, sem[f"den_in{b % 2}"], 16 * (b // 2))
                sp.dma_start(den_d[b % 2].rearrange("h (a t) -> (h a) t", t=2 * H), den_inv[:, b % 2, :])\
                  .then_inc(sem[f"den_out{b % 2}"], 16)
                sp.wait_ge(sem[f"den_out{b % 2}"], 16 * (b // 2 + 1))
                at_least(sp, sem["o_t1"], cnt(b - 2), base["o_t1"])
                sp.dma_start(den_bc[:, b % 2, :], den_d[b % 2:b % 2 + 1].broadcast_to((HD, H, T)))\
                  .then_inc(sem[f"den_in{b % 2}"], 16)

            def stack_max(b):
                sp.wait_ge(sem["max_t"], b + 1)
                at_least(sp, sem[f"max_in{b % 2}"], 16 * (b // 2))
                sp.dma_start(max_d[b % 2], max_t[0:2 * H, b % 2, :]).then_inc(sem[f"max_out{b % 2}"], 16)
                sp.wait_ge(sem[f"max_out{b % 2}"], 16 * (b // 2 + 1))
                sp.dma_start(stack_q[MAX_ROW:MAX_ROW + 2, b % STACKS, :], max_d[b % 2].rearrange("(r h) t -> r (h t)", r=2))\
                  .then_inc(sem[f"max_in{b % 2}"], 16)

            def load_pair(l, b):
                if b == 0:
                    for r in range(RING):
                        sp.wait_ge(sem[f"scattered{r}_{l}"],
                                   base[f"scattered{r}_{l}"] + LAYER0_TOTAL[f"scattered{r}"])
                at_least(sp, sem[f"mixed{l}"], 2 * cnt(b - 2), base[f"mixed{l}"])
                src = ye_d[l][0:CHOICES * TOK, :].rearrange("(a b k p) c -> b p a k c", a=CHOICES, k=KT, p=P)[b]
                for a in range(CHOICES):
                    sp.dma_start(y_pair[:, b % 2, a], src[:, a]).then_inc(sem[f"pair_in{l}_{b % 2}"], 16)

            def mod_of(l, kinds, b):
                rows = mod_d[0:2 * 6 * NB, :].rearrange("(l k b) c -> l k b c", l=2, k=6)
                return rows[l:l + 1, kinds, b, :]

            def load_mod(l, b):
                at_least(sp, sem[f"h_tok{l}"], 2 * cnt(b - 4), base[f"h_tok{l}"])
                if b == 0:
                    sp.wait_ge(sem["mod_stored"], 16)
                    if l == 1:
                        sp.wait_ge(sem["h_tok0"], 2 * NB)
                sp.dma_start(mod_bc[:, b % 4, :].rearrange("p (k c) -> p k c", k=3),
                             mod_of(l, slice(2, 5), b).broadcast_to((P, 3, C))).then_inc(sem[f"mod_bc{b % 4}_{l}"], 16)

            def load_gb(l):
                if l == 1:
                    sp.wait_ge(sem["mix3_0"], NB)
                sp.dma_start(gb_bc[:, :, :], mod_of(l, 5, slice(0, NB)).broadcast_to((P, NB, C))).then_inc(sem[f"gb_bc{l}"], 16)

            sp.wait_ge(sem["mod_rows"], 1)
            sp.dma_start(mod_d, mod_rows[:, :]).then_inc(sem["mod_stored"], 16)

            for s in STEPS[0]:
                b = stages(0, s)
                if b["scores"] is not None:
                    load_mod(0, b["scores"])
                    if b["scores"] == 0:
                        load_gb(0)
                if 0 <= s - 1 < NB:
                    load_stacks(0, s - 1)
                if 0 <= s - 3 < NB:
                    load_y(0, s - 3)
                if b["front"] is not None:
                    store_parts(0, b["front"])
                if b["route"] is not None:
                    store_h(0, b["route"])
                if b["scores"] is not None:
                    unpad_y(0, b["scores"])

            sp.wait_ge(sem["v_ps0"], NB)
            sp.dma_start(w_qk[:, :], ins["w_qk1"]).then_inc(sem["w1_in"], 16)
            sp.dma_start(w_v[:, :], ins["w_v1"]).then_inc(sem["w1_in"], 16)
            sp.wait_ge(sem["w_out0"], NB)
            sp.dma_start(w_proj[:, :], ins["w_proj1"]).then_inc(sem["w1_in"], 16)

            for s in STEPS[1]:
                b = stages(1, s)
                if s == -1:
                    load_pair(0, 0)
                    load_pair(0, 1)
                elif s + 2 < NB:
                    load_pair(0, s + 2)
                if b["probs"] is not None:
                    load_mod(1, b["probs"])
                if 0 <= s - 1 < NB:
                    load_stacks(1, s - 1)
                if 0 <= s - 5 < NB:
                    load_y(1, s - 5)
                if b["max_rows"] is not None:
                    stack_max(b["max_rows"])
                if b["front"] is not None:
                    store_parts(1, b["front"])
                if b["dens"] is not None:
                    spread_den(b["dens"])
                if b["route"] is not None:
                    store_h(1, b["route"])
                if b["probs"] is not None:
                    unpad_y(1, b["probs"])
            load_gb(1)

            ov = out.rearrange("b (k p) c -> p b k c", p=P)
            for r in range(RING):
                sp.wait_ge(sem[f"scattered{r}_1"], base[f"scattered{r}_1"] + LAYER0_TOTAL[f"scattered{r}"])
            n = NT // LAST_LOADS
            src = ye_d[1][0:CHOICES * TOK, :].rearrange("(a h i p) c -> h p a i c", a=CHOICES, h=LAST_LOADS, p=P)
            for h in range(LAST_LOADS):
                for a in range(CHOICES):
                    sp.dma_start(last_pair[:, a, h * n:(h + 1) * n, :], src[h, :, a]).then_inc(sem[f"last_in{h}"], 16)
            for b in range(NB):
                sp.wait_ge(sem["mixed_x1"], base["mixed_x1"] + b + 1)
                sp.dma_start(ov[:, b], X[:, b * KT:(b + 1) * KT, :]).then_inc(sem["stored"], 16)
            sp.wait_ge(sem["stored"], 16 * NB)

        @block.tensor
        def _(pe):
            def transpose_x(l, b):
                pe.wait_ge(sem[f"xh{l}_0"], base[f"xh{l}_0"] + 2 * (b + 1))
                if b == 0 and l == 0:
                    pe.wait_ge(sem["consts_in"], 16)
                for k in range(KT):
                    i = pe.transpose(P0[:, k * P:(k + 1) * P], xh[:, 0, b % 2, k], const("ident"))
                i.then_inc(sem[f"x_t_ps{l}"], 1)

            def project_qk(l, b):
                pe.wait_ge(sem[f"h_t{l}"], base[f"h_t{l}"] + b + 1)
                if b == 0:
                    pe.wait_ge(sem["w1_in" if l else "attn_in"], 16 * (3 if l else 4))
                for side in range(2):
                    i = pe.matmul(P0[:, side * T:(side + 1) * T], w_qk[:, side * C:(side + 1) * C], h_t[:, b % 2],
                                  start=True, stop=True)
                i.then_inc(sem[f"qk_ps{l}"], 1)

            def project_qks(b):
                at_least(pe, sem["gn_avg"], cnt(b - 4))
                for side in range(2):
                    i = pe.matmul(P1[:, side * T:(side + 1) * T], w_qks[:, side * C:(side + 1) * C], h_t[:, b % 2],
                                  start=True, stop=True)
                i.then_inc(sem["qks_ps"], 1)

            def project_v(l, b, ps):
                for k in range(KT):
                    i = pe.matmul(ps[:, k * P:(k + 1) * P], h_t[:, b % 2, k * P:(k + 1) * P], w_v[:, :],
                                  start=True, stop=True)
                if l == 0:
                    i = pe.matmul(ps[:, T:2 * T], w_gate[:, :], h_t[:, b % 2], start=True, stop=True)
                i.then_inc(sem[f"v_ps{l}"], 1)

            def retention_scores(b, g):
                if g == 0:
                    pe.wait_ge(sem[f"stacked0_{b % 2}"], 96 * (b // 2 + 1))
                at_least(pe, sem["masked"], 4 * b + g - 1)
                r, ch = b % 3, g // 2
                for n in range(8):
                    at = (8 * (g % 2) + n) * T + ch * P
                    i = pe.matmul(pair[g % 2][:, n * P:(n + 1) * P], stack_k[:, r, at:at + P], stack_q[:, r, at:at + P],
                                  start=True, stop=True)
                i.then_inc(sem["scores0"], 1)

            def retention_pv(b, g):
                pe.wait_ge(sem["masked"], 4 * b + g + 1)
                ch = g // 2
                if g == 0:
                    pe.wait_ge(sem["v_0"], b + 1)
                if g % 2 == 0:
                    at_least(pe, sem["y_pad0"], 2 * b + ch)
                for n in range(8):
                    h = 8 * (g % 2) + n
                    j, gg = h % 4, h // 4
                    i = pe.matmul(Y0[32 * j:32 * j + 32, gg * P:(gg + 1) * P], V[:, b % 5, ch, h * HD:h * HD + 32],
                                  probs[:, 2 * (g % 2) + n // 4, (n % 4) * P:(n % 4 + 1) * P], start=True, stop=True)
                i.then_inc(sem["pv_0"], 1)

            def keys_to_tokens(b):
                at_least(pe, sem["logits0"], cnt(b + 2 - 6))
                at_least(pe, sem["x_mid0"], cnt(b + 2 - 5))
                pe.wait_ge(sem["qk0"], b + 1)
                pe.transpose(P1[:, 0:P], qk[:, b % 3, T:T + P], const("ident")).then_inc(sem["k_tok_ps"], 1)

            def key_value_state(b):
                pe.wait_ge(sem["k_tok"], b + 1)
                at_least(pe, sem["rot_a"], cnt(b + 2))
                v = V[:, b % 5, 0, 0:C].rearrange("p (h d) -> p d h", d=HD)
                pe.matmul(P0[:, 0:C], k_tok[:, :], v, start=True, stop=True).then_inc(sem["state_ps"], 1)

            def state_to_y(b):
                pe.wait_ge(sem["state"], b + 1)
                at_least(pe, sem["gated0"], cnt(b + 2))
                pe.matmul(P2[:, 0:P], state[:, :], qk[:, b % 3, P:T], start=True, stop=True).then_inc(sem["y_state_ps"], 1)

            def average_heads(b):
                pe.wait_ge(sem["gn_sq"], b + 1)
                at_least(pe, sem["k_tok"], cnt(b + 2))
                pe.matmul(P1[:, 0:2], const("head_avg"), gn_mv[:, :], start=True, stop=True).then_inc(sem["gn_avg_ps"], 1)

            def project_out(l, b):
                pe.wait_ge(sem[f"o_t{l}"], base[f"o_t{l}"] + b + 1)
                pe.wait_ge(sem[f"w_out{l}"], base[f"w_out{l}"] + b + 1)
                for k in range(KT):
                    i = pe.matmul(P1[:, k * P:(k + 1) * P], o_t[:, b % 2, k * P:(k + 1) * P], w_out[:, b % 2, :],
                                  start=True, stop=True)
                i.then_inc(sem[f"out_ps{l}"], 1)

            def transpose_h2(l, b):
                pe.wait_ge(sem[f"h_tok{l}"], base[f"h_tok{l}"] + 2 * (b + 1))
                for k in range(KT):
                    i = pe.transpose(P0[:, k * P:(k + 1) * P], h_tok[:, b % 2, k], const("ident"))
                i.then_inc(sem[f"h2_ps{l}"], 1)

            def route_logits(l, b):
                pe.wait_ge(sem[f"h2_t{l}"], base[f"h2_t{l}"] + b + 1)
                if b == 0 and l == 0:
                    pe.wait_ge(sem["late_in"], 16 * 5)
                for k in range(KT):
                    i = pe.matmul(P1[:, k * E:(k + 1) * E], h2_t[:, k * P:(k + 1) * P], router_w[:, l, :],
                                  start=True, stop=True)
                i.then_inc(sem[f"logits_ps{l}"], 1)

            pe.wait_ge(sem["mod_in"], 32)
            pe.wait_ge(sem["silu_c"], 1)
            for l in range(2):
                for k in range(6):
                    i = pe.matmul(P2[:, (6 * l + k) * NB:(6 * l + k + 1) * NB], mod_w[:, l, k * C:(k + 1) * C],
                                  sc_t[:, l, :], start=True, stop=True)
            i.then_inc(sem["mod_t_ps"], 1)

            for s in STEPS[0]:
                b = stages(0, s)
                a, m, z, y = b["front"], b["scores"], b["back"], b["route"]
                if m is not None:
                    retention_scores(m, 0)
                    retention_scores(m, 1)
                if a is not None:
                    at_least(pe, sem["h2_t0"], cnt(s - 6))
                    transpose_x(0, a)
                if m is not None:
                    keys_to_tokens(m)
                if z is not None:
                    at_least(pe, sem["logits0"], cnt(s - 6))
                    average_heads(z)
                if s == 0:
                    pe.wait_ge(sem["mod_t"], 8)
                    pe.transpose(P1[:, 0:P], mod_pad[:, :], const("ident")).then_inc(sem["mod_rows_ps"], 1)
                if a is not None:
                    project_qk(0, a)
                    if s == 0:
                        pe.wait_ge(sem["mod_rows"], 1)
                    if a >= 2:
                        pe.wait_ge(sem["k_tok"], cnt(m))
                    project_qks(a)
                if m is not None:
                    retention_pv(m, 0)
                    retention_scores(m, 2)
                if a is not None:
                    at_least(pe, sem["y_state"], cnt(s - 3))
                    if a == 0:
                        pe.wait_ge(sem["mod_t"], 8)
                    else:
                        at_least(pe, sem["gated0"], cnt(a - 1))
                    project_v(0, a, P2)
                if m is not None:
                    retention_pv(m, 1)
                    retention_scores(m, 3)
                if m is not None:
                    at_least(pe, sem["h2_t0"], cnt(s - 6))
                    key_value_state(m)
                if z is not None:
                    at_least(pe, sem["rot_b"], cnt(s))
                    at_least(pe, sem["k_tok"], cnt(s - 2))
                    project_out(0, z)
                if m is not None:
                    retention_pv(m, 2)
                    state_to_y(m)
                    retention_pv(m, 3)
                if y is not None:
                    at_least(pe, sem["state"], cnt(s - 2))
                    at_least(pe, sem["h2_t0"], cnt(s - 6))
                    transpose_h2(0, y)
                    at_least(pe, sem["x_mid0"], cnt(s - 4))
                    at_least(pe, sem["logits0"], cnt(s - 6))
                    route_logits(0, y)

            def routing(l):
                pe.wait_ge(sem[f"picked_b{l}"], base[f"picked_b{l}"] + 1)
                pe.wait_ge(sem[f"tiles_before_b{l}"], base[f"tiles_before_b{l}"] + 1)
                if l == 0:
                    pe.wait_ge(sem["bf16_consts"], 5)
                flat = lambda t: t[:, :, :].rearrange("p e i -> p (e i)")
                pe.matmul(P0[:, 0:P], before_b[:, :], flat(picked_b), start=True, stop=False)
                pe.matmul(P0[:, 0:P], ones_b[:, :], flat(tiles_before_b), start=False, stop=True)\
                  .then_inc(sem[f"ranks_ps{l}"], 1)
                pe.wait_ge(sem[f"total_b{l}"], base[f"total_b{l}"] + 1)
                pe.matmul(P1[:, 0:E], ones_b[:, :], total_b[:, :], start=True, stop=True).then_inc(sem[f"counts_ps{l}"], 1)
                pe.wait_ge(sem[f"hot_vals{l}"], base[f"hot_vals{l}"] + 2)
                for n in range(CHOICES * NT):
                    pe.wait_ge(sem[f"hot_lane{l}"], base[f"hot_lane{l}"] + n + 1)
                    pe.matmul(P2[:, 0:2 * TILES], hot_lane[:, n % (4 * LANES), :], hot_vals[:, n].rearrange("p a j -> p (a j)"),
                              start=(n == 0), stop=(n == CHOICES * NT - 1)).then_inc(sem[f"slot_ps{l}"], 1)

            def expert_tiles(l):
                def transpose_rows(n, r, uses):
                    pe.wait_ge(sem[f"gathered{r}_{l}"], base[f"gathered{r}_{l}"] + 16 * (uses + 1))
                    pe.transpose(P0[:, 0:P], x_rows[:, r, :], const("ident")).then_inc(sem[f"x_t_e_ps{l}"], 1)

                def first(n, r):
                    pe.wait_ge(sem[f"x_t{l}"], base[f"x_t{l}"] + n + 1)
                    pe.wait_ge(sem[f"w_now{l}"], base[f"w_now{l}"] + 2 * n + 2)
                    if l == 0:
                        at_least(pe, sem["act_hid0"], n - 1)
                    at_least(pe, sem[f"hid_t{l}"], n - 1, base[f"hid_t{l}"])
                    for which, (banks, done) in enumerate(((HIDDEN, f"hidden_ps{l}"), (UP, "up_ps"))[:l + 1]):
                        for k in range(FK):
                            at = banks if l == 1 or k < FK // 2 else UP
                            i = pe.matmul(at[r % 2][:, k * P:(k + 1) * P], w_now[:, r % 2, which, k * P:(k + 1) * P],
                                          x_t[:, r % 2, :], start=True, stop=True)
                        i.then_inc(sem[done], 1)

                def second(n, r):
                    at_least(pe, sem[f"y_rows{l}"], n - 1, base[f"y_rows{l}"])
                    pe.wait_ge(sem[f"w2_now{l}"], base[f"w2_now{l}"] + (n + 1) * (2 - l))
                    if l == 0:
                        pe.wait_ge(sem["act_hid0"], n + 1)
                    pe.wait_ge(sem[f"hid_t{l}"], base[f"hid_t{l}"] + n + 1)
                    for k in range(FK):
                        i = pe.matmul(Y_ROWS[r % 2], hid_t[:, r % 2, k * P:(k + 1) * P], w2_now[:, r % 2, k, :],
                                      start=(k == 0), stop=(k == FK - 1))
                    i.then_inc(sem[f"y_ps{l}"], 1)

                def step(n, r, uses):
                    first(n, r)
                    if exists(n + 1):
                        transpose_rows(n + 1, (r + 1) % RING, uses + (r + 1) // RING)
                    if exists(n - 1):
                        second(n - 1, (r - 1) % RING)

                transpose_rows(0, 0, 0)
                all_tiles(pe, step)
                second(TILES - 1, (TILES - 1) % RING)

            routing(0)
            expert_tiles(0)

            half = [[pair[i][:, k * 512:(k + 1) * 512] for k in range(2)] for i in range(2)]

            def max_scores(b, g):
                ps = half[0][g % 2]
                if g == 0:
                    pe.wait_ge(sem[f"stacked1_{b % 2}"], base[f"stacked1_{b % 2}"] + 96 * (b // 2 + 1))
                at_least(pe, sem["maxed"], 12 * b + g - 1)
                r = b % STACKS
                if g < 4:
                    cells = [(4 * g + n, 0, P) for n in range(4)]
                else:
                    cells = [(2 * (g - 4) + n, P, T) for n in range(2)]
                for n, (h, t0, keys) in enumerate(cells):
                    i = pe.matmul(ps[:, n * keys:(n + 1) * keys], stack_q[0:MAX_ROW, r, h * T + t0:h * T + t0 + P],
                                  stack_k[0:MAX_ROW, r, h * T:h * T + keys], start=(n == 0), stop=False,
                                  skip_group_check=True)
                diag_blocks = [n * keys + keys - P for n in range(len(cells))]
                for n, at in enumerate(diag_blocks):
                    i = pe.matmul(ps[:, at:at + P], ident_b[:, :], neg_mask[:, :], start=False, stop=(n == len(cells) - 1),
                                  skip_group_check=True)
                i.then_inc(sem["scores_max"], 1)

            def exp_scores(b, g):
                gp, i6 = g // 6, g % 6
                ps = half[1][g % 2]
                if g == 0:
                    pe.wait_ge(sem[f"max_in{b % 2}"], 16 * (b // 2 + 1))
                at_least(pe, sem["exped"], 12 * b + g - 1)
                r = b % STACKS
                for n, (h, s0, t0, cols) in enumerate(exp_cells(g)):
                    i = pe.matmul(ps[:, n * cols:(n + 1) * cols], stack_k[:, r, h * T + s0:h * T + s0 + P],
                                  stack_q[:, r, h * T + t0:h * T + t0 + cols], start=True, stop=True)
                i.then_inc(sem["scores_exp"], 1)

            def softmax_pv(b, g):
                gp, i6 = g // 6, g % 6
                ps = (Y0, P2)[gp]
                pe.wait_ge(sem["probs_causal"], 12 * b + g + 1)
                if i6 == 0:
                    at_least(pe, sem["y_pad1"], 2 * b + gp - 1, base["y_pad1"])
                if g == 0:
                    pe.wait_ge(sem["v_1"], base["v_1"] + b + 1)
                for n, (h, s0, t0, cols) in enumerate(exp_cells(g)):
                    j, gg = h % 4, (h // 4) % 2
                    i = pe.matmul(ps[32 * j:32 * j + 32, gg * T + t0:gg * T + t0 + cols],
                                  V[:, b % 5, s0 // P, h * 9:h * 9 + 32], probs[:, g % 4, n * cols:(n + 1) * cols],
                                  start=(i6 < 2 and gg == 0), stop=(i6 >= 4), skip_group_check=True)
                i.then_inc(sem["pv_1"], 1)

            def max_to_rows(b):
                pe.wait_ge(sem["max_parts"], 2 * (b + 1))
                for k in range(KT):
                    i = pe.transpose(P1[0:2 * H, k * 64:(k + 1) * 64].bitcast(BF16), max_parts[:, b % 2, k], ident_b[:, :])
                i.then_inc(sem["max_t_ps"], 1)

            for s in STEPS[1]:
                b = stages(1, s)
                a, m, w, z, y = b["front"], b["scores"], b["probs"], b["back"], b["route"]
                mx = b["max_rows"]
                if w is not None:
                    exp_scores(w, 0)
                if m is not None:
                    max_scores(m, 0)
                for g in range(13):
                    if w is not None and g + 1 < 12:
                        exp_scores(w, g + 1)
                    if m is not None and g + 1 < 12:
                        max_scores(m, g + 1)
                    if w is not None and g >= 1:
                        softmax_pv(w, g - 1)
                    if g == 0 and a is not None:
                        at_least(pe, sem["h2_t1"], cnt(s - 8), base["h2_t1"])
                        at_least(pe, sem["part1_1"], cnt(s - 1), base["part1_1"])
                        at_least(pe, sem["rest1_1"], cnt(s - 1), base["rest1_1"])
                        transpose_x(1, a)
                    if g == 2 and a is not None:
                        project_qk(1, a)
                    if g == 7 and y is not None:
                        at_least(pe, sem["part1_1"], cnt(s), base["part1_1"])
                        at_least(pe, sem["rest1_1"], cnt(s), base["rest1_1"])
                        at_least(pe, sem["h2_t1"], cnt(s - 8), base["h2_t1"])
                        transpose_h2(1, y)
                    if g == 0 and mx is not None:
                        at_least(pe, sem["v_1"], cnt(s - 1), base["v_1"])
                        at_least(pe, sem["x_mid1"], cnt(s - 7), base["x_mid1"])
                        at_least(pe, sem["logits1"], cnt(s - 8), base["logits1"])
                        max_to_rows(mx)
                    if g == 3 and a is not None:
                        at_least(pe, sem["max_t"], cnt(s - 3))
                        at_least(pe, sem["x_mid1"], cnt(s - 7), base["x_mid1"])
                        at_least(pe, sem["logits1"], cnt(s - 8), base["logits1"])
                        project_v(1, a, P1)
                    if g == 6 and z is not None:
                        at_least(pe, sem["v_1"], cnt(s), base["v_1"])
                        at_least(pe, sem["max_t"], cnt(s - 3))
                        at_least(pe, sem["logits1"], cnt(s - 8), base["logits1"])
                        project_out(1, z)
                    if g == 9 and y is not None:
                        at_least(pe, sem["x_mid1"], cnt(s - 6), base["x_mid1"])
                        at_least(pe, sem["max_t"], cnt(s - 3))
                        at_least(pe, sem["v_1"], cnt(s), base["v_1"])
                        route_logits(1, y)

            routing(1)
            expert_tiles(1)

        @block.vector
        def _(ve):
            def norm_stats(l, which, b):
                tag = f"{l}_{which}"
                for k in range(KT):
                    ve.bn_stats(stats[:, which, k], X[:, b * KT + k, :]).then_inc(sem[f"stats{tag}"], 1)
                ve.wait_ge(sem[f"stats{tag}"], base[f"stats{tag}"] + 2 * (b + 1))
                for k in range(KT):
                    ve.bn_aggr(mv[:, which, k], stats[:, which, k]).then_inc(sem[f"mv{tag}"], 1)
                ve.wait_ge(sem[f"mv{tag}"], base[f"mv{tag}"] + 2 * (b + 1))
                ve.tensor_scalar(var_eps[:, which, :], mv[:, which, :, 1], EPS, None, ALU.add).then_inc(sem[f"var{tag}"], 1)

            def norm_apply(l, which, b):
                tag = f"{l}_{which}"
                ve.wait_ge(sem[f"rstd{tag}"], base[f"rstd{tag}"] + b + 1)
                if which == 0:
                    at_least(ve, sem[f"x_t_ps{l}"], cnt(b - 2), base[f"x_t_ps{l}"])
                else:
                    at_least(ve, sem[f"h_mul{l}"], cnt(b - 2), base[f"h_mul{l}"])
                for k in range(KT):
                    ve.tensor_scalar(xh[:, which, b % 2, k], X[:, b * KT + k, :], mv[:, which, k, 0:1], rstd[:, which, k:k + 1],
                                     ALU.subtract, ALU.mult).then_inc(sem[f"xh{tag}"], 1)

            def read_logits(l, b):
                ve.wait_ge(sem[f"logits_ps{l}"], base[f"logits_ps{l}"] + b + 1)
                dst = logits[:, :, b * KT:(b + 1) * KT].rearrange("p e k -> p k e")
                src = P1[:, 0:KT * E].rearrange("p (k e) -> p k e", e=E)
                if l == 0:
                    ve.tensor_copy(dst, src).then_inc(sem[f"logits{l}"], 1)
                else:
                    ve.tensor_tensor(dst, src, router_b[:, :].unsqueeze(1).broadcast_to((P, KT, E)), ALU.add)\
                      .then_inc(sem[f"logits{l}"], 1)

            def add_to_x(l, b):
                ve.wait_ge(sem[f"out_ps{l}"], base[f"out_ps{l}"] + b + 1)
                xs = X[:, b * KT:(b + 1) * KT, :]
                ve.tensor_tensor(xs, P1[:, 0:T].rearrange("p (k c) -> p k c", k=KT), xs, ALU.add)\
                  .then_inc(sem[f"x_mid{l}"], 1)

            def mask_scores(b, g):
                ve.wait_ge(sem["scores0"], 4 * b + g + 1)
                at_least(ve, sem["pv_0"], 4 * b + g - 1)
                if b == 0 and g == 0:
                    ve.wait_ge(sem["consts_in"], 16)
                ve.tensor_tensor(probs[:, 2 * (g % 2):2 * (g % 2) + 2, :].rearrange("p a (n t) -> p (a n) t", t=P),
                                 pair[g % 2][:, :].rearrange("p (n t) -> p n t", t=P),
                                 const("causal").unsqueeze(1).broadcast_to((P, 8, P)), ALU.mult).then_inc(sem["masked"], 1)

            def group_stats(b):
                ve.wait_ge(sem[f"y_in0_{b % 2}"], 16 * (b // 2 + 1))
                ve.wait_ge(sem["y_state"], b + 1)
                y = y_t[:, b % 3, :]
                ve.tensor_tensor(y[:, P:T], y[:, P:T], y_state[:, b % 3, :], ALU.add).then_inc(sem["y_sum"], 1)
                ve.wait_ge(sem["y_sum"], b + 1)
                ve.bn_stats(gn_stats[:, :], y).then_inc(sem["gn_stats"], 1)
                ve.wait_ge(sem["gn_stats"], 2 * b + 1)
                at_least(ve, sem["gn_avg_ps"], b)
                ve.bn_aggr(gn_mv[:, :], gn_stats[:, :]).then_inc(sem["gn_stats"], 1)
                ve.wait_ge(sem["gn_stats"], 2 * b + 2)
                ve.scalar_tensor_tensor(out=gn_mv[:, 1:2], in0=gn_mv[:, 0:1], scalar=gn_mv[:, 0:1], in1=gn_mv[:, 1:2],
                                        op0=ALU.mult, op1=ALU.add).then_inc(sem["gn_sq"], 1)

            def group_var(b):
                ve.wait_ge(sem["gn_avg"], b + 1)
                ve.scalar_tensor_tensor(out=gn_ve[:, 0:1], in0=gn_avg[:, 0:1], scalar=gn_avg[:, 0:1], in1=gn_avg[:, 1:2],
                                        op0=ALU.mult, op1=ALU.subtract).then_inc(sem["gn_neg"], 1)
                ve.wait_ge(sem["gn_neg"], b + 1)
                ve.tensor_scalar(gn_ve[:, 1:2], gn_ve[:, 0:1], -1.0, EPS, ALU.mult, ALU.add).then_inc(sem["gn_var"], 1)

            def group_apply(b):
                ve.wait_ge(sem["gn_rstd"], b + 1)
                if b == 0:
                    ve.wait_ge(sem["late_in"], 16 * 5)
                ve.tensor_tensor(gn_ab[:, 0:1], gn_rstd[:, :], gn[:, 0:1], ALU.mult).then_inc(sem["gn_a"], 1)
                ve.wait_ge(sem["gn_a"], b + 1)
                ve.scalar_tensor_tensor(out=gn_ab[:, 1:2], in0=gn_avg[:, 0:1], scalar=gn_ab[:, 0:1], in1=gn[:, 1:2],
                                        op0=ALU.mult, op1=ALU.subtract).then_inc(sem["gn_b"], 1)
                ve.wait_ge(sem["gn_b"], b + 1)
                at_least(ve, sem["o_t0"], b)
                ve.tensor_scalar(y_n[:, :], y_t[:, b % 3, :], gn_ab[:, 0:1], gn_ab[:, 1:2], ALU.mult, ALU.subtract)\
                  .then_inc(sem["y_n"], 1)

            def rotate(b):
                ve.wait_ge(sem["qk_ps0"], b + 1)
                at_least(ve, sem["qk0"], b)
                if b == 0:
                    ve.wait_ge(sem["rotary_in"], 16)
                ve.tensor_tensor(rot[:, 0], P0[:, :], rotary[:, 0], ALU.mult).then_inc(sem["rot_a"], 1)
                ve.wait_ge(sem["qks_ps"], b + 1)
                ve.tensor_tensor(rot[:, 1], P1[:, :], rotary[:, 1], ALU.mult).then_inc(sem["rot_b"], 1)

            def mask_state(b):
                ve.wait_ge(sem["state_ps"], b + 1)
                at_least(ve, sem["y_state_ps"], b)
                ve.tensor_tensor(state[:, :], P0[:, 0:C], const("same_head"), ALU.mult).then_inc(sem["state"], 1)

            ve.memset(ones[:, :], 1.0).then_inc(sem["first_memsets"], 1)
            ve.memset(mod_pad[:, :], 0.0).then_inc(sem["first_memsets"], 1)
            ve.wait_ge(sem["first_memsets"], 2)
            ve.memset(half_neg[:, :], -0.5).then_inc(sem["first_memsets"], 1)
            ve.memset(stack_q[:, 0, :].bitcast(F32), 0.0).then_inc(sem["stack_q_set"], 1)
            ve.wait_ge(sem["x_in0"], 16)
            norm_stats(0, 0, 0)
            norm_apply(0, 0, 0)
            ve.wait_ge(sem["mod_t_ps"], 1)
            kinds = lambda t: t.rearrange("p l (n k) b -> p l n k b", k=3)
            raw = kinds(P2[:, 0:2 * 6 * NB].rearrange("p (l k b) -> p l k b", l=2, k=6))
            ready = kinds(mod_t)
            ve.tensor_copy(ready[:, :, :, 0], raw[:, :, :, 0]).then_inc(sem["mod_t"], 1)
            ve.tensor_scalar(ready[:, :, :, 1], raw[:, :, :, 1], 1.0, None, ALU.add).then_inc(sem["mod_t"], 1)
            low, up, pos = (gate_tmp[:, i].rearrange("p (l n) b -> p l n b", l=2) for i in range(3))
            ve.tensor_scalar(low, raw[:, :, :, 2], -FLOOR, None, ALU.min).then_inc(sem["mod_t"], 1)
            ve.tensor_scalar(up, raw[:, :, :, 2], FLOOR, None, ALU.max).then_inc(sem["mod_t"], 1)
            ve.wait_ge(sem["mod_t"], 4)
            ve.tensor_tensor(up, up, low, ALU.subtract).then_inc(sem["mod_t"], 1)
            ve.tensor_scalar(pos, raw[:, :, :, 2], 0.0, None, ALU.is_ge).then_inc(sem["mod_t"], 1)
            ve.wait_ge(sem["mod_t"], 6)
            ve.tensor_tensor(pos, pos, up, ALU.mult).then_inc(sem["mod_t"], 1)
            ve.wait_ge(sem["mod_t"], 7)
            ve.tensor_tensor(ready[:, :, :, 2], pos, low, ALU.add).then_inc(sem["mod_t"], 1)
            ve.memset(V[:, :, :, :], 0.0).then_inc(sem["v_clear"], 1)
            ve.wait_ge(sem["v_clear"], 1)

            for s in STEPS[0]:
                b = stages(0, s)
                a, m, z, y = b["front"], b["scores"], b["back"], b["route"]
                if b["logits"] is not None:
                    read_logits(0, b["logits"])
                if z is not None:
                    group_stats(z)
                if m is not None:
                    mask_scores(m, 0)
                if y is not None:
                    norm_apply(0, 1, y)
                if m is not None:
                    mask_scores(m, 1)
                if z is not None:
                    group_var(z)
                if a is not None:
                    rotate(a)
                if z is not None:
                    group_apply(z)
                n = b["next"]
                if n is not None and n > 0:
                    if n == 1:
                        ve.wait_ge(sem["x_in1"], 16)
                    norm_stats(0, 0, n)
                if m is not None:
                    mask_scores(m, 2)
                    mask_state(m)
                if n is not None and n > 0:
                    norm_apply(0, 0, n)
                if m is not None:
                    mask_scores(m, 3)
                if z is not None:
                    add_to_x(0, z)
                    ve.wait_ge(sem["x_mid0"], z + 1)
                    norm_stats(0, 1, z)

            routing_steps = [0]

            def routing(l):
                steps = routing_steps

                def done(i):
                    i.then_inc(sem["routing"], 1)
                    steps[0] += 1
                    ve.wait_ge(sem["routing"], steps[0])

                by_tile = lambda t: t.rearrange("p e i -> p i e")
                over_e = lambda t: t.unsqueeze(1).broadcast_to((P, E, NT))
                L = logits[:, :, :]
                ve.wait_ge(sem[f"logits{l}"], base[f"logits{l}"] + NB)
                if l == 0:
                    ve.wait_ge(sem["bf16_consts"], 5)
                ids = const("expert_id").rearrange("p (e i) -> p e i", e=E)
                for choice, (src, top) in enumerate(((L, r_max), (second[:, :, :], r_max2))):
                    if choice == 1:
                        done(ve.scalar_tensor_tensor(out=second[:, :, :], in0=pick[:, 0], scalar=-BIG, in1=L,
                                                     op0=ALU.mult, op1=ALU.add))
                    done(ve.tensor_reduce(top[:, :], by_tile(src), AX_X, ALU.max))
                    done(ve.tensor_tensor(r_eq[:, :, :], src, over_e(top[:, :]), ALU.is_equal))
                    done(ve.scalar_tensor_tensor(out=r_idx[:, :, :], in0=r_eq[:, :, :], scalar=-64.0, in1=ids,
                                                 op0=ALU.mult, op1=ALU.add))
                    done(ve.tensor_reduce(r_min[:, :], by_tile(r_idx[:, :, :]), AX_X, ALU.min))
                    done(ve.tensor_tensor(pick[:, choice], r_idx[:, :, :], over_e(r_min[:, :]), ALU.is_equal))
                ve.tensor_tensor(gap[:, :], r_max2[:, :], r_max[:, :], ALU.subtract).then_inc(sem[f"gap{l}"], 1)
                done(ve.tensor_tensor(picked[:, :, :], pick[:, 0], pick[:, 1], ALU.add))
                ve.tensor_copy(picked_b[:, :, :], picked[:, :, :]).then_inc(sem[f"picked_b{l}"], 1)
                flat = lambda t: t[:, :, :].rearrange("p e i -> p (e i)")
                done(ve.tensor_tensor_scan(flat(upto), const("restart"), flat(picked), 0.0, ALU.mult, ALU.add))
                ve.tensor_tensor(tiles_before_b[:, :, :], upto[:, :, :], picked[:, :, :], ALU.subtract)\
                  .then_inc(sem[f"tiles_before_b{l}"], 1)
                ve.tensor_copy(total_b[:, :], upto[:, :, NT - 1]).then_inc(sem[f"total_b{l}"], 1)
                ve.wait_ge(sem[f"counts_ps{l}"], base[f"counts_ps{l}"] + 1)
                done(ve.tensor_tensor(over[:, :, :], P1[:, 0:E].unsqueeze(2).broadcast_to((P, E, 16)),
                                      const("steps128").unsqueeze(1).broadcast_to((P, E, 16)), ALU.is_gt))
                done(ve.tensor_reduce(n_tiles[:, :], over[:, :, :], AX_X, ALU.add))
                done(ve.tensor_tensor_scan(tile_end[:, :], ones[:, 0:E], n_tiles[:, :], 0.0, ALU.mult, ALU.add))
                done(ve.tensor_tensor(tile_start[:, :], tile_end[:, :], n_tiles[:, :], ALU.subtract))
                ve.wait_ge(sem[f"ranks_ps{l}"], base[f"ranks_ps{l}"] + 1)
                done(ve.scalar_tensor_tensor(out=place[:, :, :], in0=tile_start[:, :].unsqueeze(2).broadcast_to((P, E, NT)),
                                             scalar=float(P), in1=P0[:, 0:P].rearrange("p (e i) -> p e i", e=E),
                                             op0=ALU.mult, op1=ALU.add))
                for choice in range(CHOICES):
                    done(ve.tensor_tensor(place_c[:, :, :], pick[:, choice], place[:, :, :], ALU.mult))
                    done(ve.tensor_reduce(slot[:, choice * NT:(choice + 1) * NT], by_tile(place_c[:, :, :]), AX_X, ALU.add))
                done(ve.tensor_copy(slot_i[:, :], slot[:, :]))
                ve.tensor_scalar(tile_i[:, :], slot_i[:, :], 7, None, ALU.logical_shift_right).then_inc(sem[f"gap{l}"], 1)
                done(ve.tensor_scalar(lane_i[:, :], slot_i[:, :], P - 1, None, ALU.bitwise_and))
                ve.wait_ge(sem[f"gap{l}"], base[f"gap{l}"] + 2)
                ve.tensor_copy(slot_tile[:, :], tile_i[:, :]).then_inc(sem[f"gap{l}"], 1)
                done(ve.tensor_copy(slot_lane[:, :], lane_i[:, :]))
                ve.wait_ge(sem[f"gap{l}"], base[f"gap{l}"] + 3)
                i = (ve.tensor_tensor(hot_tile[:, :, :], slot_tile[:, :].unsqueeze(2).broadcast_to((P, CHOICES * NT, TILES)),
                                      iota_b[:, 0:TILES].unsqueeze(1).broadcast_to((P, CHOICES * NT, TILES)),
                                      ALU.is_equal))
                i.then_inc(sem[f"gap{l}"], 1)
                ve.wait_ge(sem[f"gap{l}"], base[f"gap{l}"] + 4)
                ve.tensor_scalar(hot_vals[:, :, 0, :], hot_tile[:, :, :], const("pid1"), None, ALU.mult)\
                  .then_inc(sem[f"hot_vals{l}"], 1)
                for n in range(0, CHOICES * NT, LANES):
                    at_least(ve, sem[f"slot_ps{l}"], n - 3 * LANES, base[f"slot_ps{l}"])
                    ve.tensor_tensor(hot_lane[:, n % (4 * LANES):n % (4 * LANES) + LANES, :],
                                     iota_b[:, :].unsqueeze(1).broadcast_to((P, LANES, P)),
                                     slot_lane[:, n:n + LANES].unsqueeze(2).broadcast_to((P, LANES, P)), ALU.is_equal)\
                      .then_inc(sem[f"hot_lane{l}"], LANES)
                done(ve.tensor_tensor(ended[:, :, :], tile_end[:, :].unsqueeze(1).broadcast_to((P, TILES, E)),
                                      const("iota")[:, 0:TILES].unsqueeze(2).broadcast_to((P, TILES, E)), ALU.is_le))
                done(ve.tensor_reduce(tile_exp_f[:, :], ended[:, :, :], AX_X, ALU.add))
                ve.tensor_scalar(tile_exp[:, :], tile_exp_f[:, :], float(E - 1), None, ALU.min).then_inc(sem[f"tile_exp{l}"], 1)
                ve.wait_ge(sem[f"slot_ps{l}"], base[f"slot_ps{l}"] + CHOICES * NT)
                done(ve.tensor_copy(ident_lo[:, :], P2[:, 0:TILES]))
                done(ve.scalar_tensor_tensor(out=ident_all[:, :], in0=P2[:, TILES:2 * TILES], scalar=float(P), in1=ident_lo[:, :],
                                             op0=ALU.mult, op1=ALU.add))
                done(ve.tensor_scalar(wrap[:, :], ident_all[:, :], TOK + 0.5, -float(TOK), ALU.is_gt, ALU.mult))
                done(ve.scalar_tensor_tensor(out=src_f[:, :], in0=wrap[:, :], scalar=-1.0, in1=ident_all[:, :],
                                             op0=ALU.add, op1=ALU.add))
                ve.tensor_scalar(src_row[:, :], src_f[:, :], 0.0, None, ALU.max).then_inc(sem[f"src_row{l}"], 1)
                done(ve.tensor_scalar(empty[:, :], ident_all[:, :], 0.5, None, ALU.is_lt))
                done(ve.tensor_tensor(empty_at[:, :], empty[:, :], const("trash"), ALU.mult))
                ve.scalar_tensor_tensor(out=dst_row[:, :], in0=empty_at[:, :], scalar=-1.0, in1=ident_all[:, :],
                                        op0=ALU.add, op1=ALU.add).then_inc(sem[f"dst_row{l}"], 1)
                ve.wait_ge(sem[f"gap_exp{l}"], base[f"gap_exp{l}"] + 1)
                done(ve.tensor_scalar(gap_den[:, :], gap_exp[:, :], 1.0, None, ALU.add))
                done(ve.reciprocal(weight[:, 0, :], gap_den[:, :]))
                ve.tensor_tensor(weight[:, 1, :], gap_exp[:, :], weight[:, 0, :], ALU.mult).then_inc(sem[f"weights{l}"], 1)

            def expert_tiles(l):
                def copy_second(n, r):
                    e = ve.value_load(tile_exp[0:1, bass.ds(n, 1)], min_val=0, max_val=E - 1)
                    ve.tensor_copy(w2_now[:, r % 2], W2[:, bass.ds(e, 1), :, :].rearrange("p e k c -> p (e k) c"))\
                      .then_inc(sem[f"w2_now{l}"], 1)
                    if l == 0:
                        ve.tensor_copy(b2_now[:, r % 2, :], B2[:, bass.ds(e, 1), :]).then_inc(sem["w2_now0"], 1)

                def keep_rows(n, r, uses):
                    if l == 0:
                        ve.wait_ge(sem["w2_now0"], 2 * n + 2)
                    at_least(ve, sem[f"scattered{r}_{l}"], 16 * uses, base[f"scattered{r}_{l}"])
                    ve.wait_ge(sem[f"y_ps{l}"], base[f"y_ps{l}"] + n + 1)
                    if l == 0:
                        ve.tensor_tensor(y_rows[:, r, :], Y_ROWS[r % 2], b2_now[:, r % 2, :], ALU.add).then_inc(sem["y_rows0"], 1)
                    else:
                        ve.tensor_copy(y_rows[:, r, :], Y_ROWS[r % 2]).then_inc(sem["y_rows1"], 1)

                def step(n, r, uses):
                    at_least(ve, sem[f"y_ps{l}"], n - 1, base[f"y_ps{l}"])
                    if l == 0:
                        ve.wait_ge(sem["w_now0"], 2 * n + 2)
                        ve.wait_ge(sem["hidden_ps0"], n + 1)
                        for k in range(FK // 2):
                            i = ve.tensor_scalar(hid_t[:, r % 2, k * P:(k + 1) * P], HIDDEN[r % 2][:, k * P:(k + 1) * P],
                                                 b_now[:, r, k:k + 1], 0.0, ALU.add, ALU.max)
                        i.then_inc(sem["hid_t0"], 1)
                    else:
                        ve.wait_ge(sem["act_hid1"], base["act_hid1"] + n + 1)
                        ve.wait_ge(sem["up_ps"], n + 1)
                        ve.tensor_tensor(hid_t[:, r % 2, :], UP[r % 2], hid_g[:, r % 2, :], ALU.mult).then_inc(sem["hid_t1"], 1)
                    if exists(n - 1):
                        keep_rows(n - 1, (r - 1) % RING, uses - (r == 0))
                    if l == 0:
                        at_least(ve, sem["y_rows0"], n)
                    if exists(n + 1):
                        copy_second(n + 1, r + 1)

                ve.wait_ge(sem[f"tile_exp{l}"], base[f"tile_exp{l}"] + 1)
                ve.wait_ge(sem[f"experts{l}_in"], 16 * (2 * E + 2 * (l == 0)))
                copy_second(0, 0)
                all_tiles(ve, step)
                keep_rows(TILES - 1, (TILES - 1) % RING, (TILES - 1) // RING)

            def mix(l, b):
                for k in range(KT):
                    ve.wait_ge(sem[f"mix1_{l}"], base[f"mix1_{l}"] + 2 * b + k + 1)
                    at_least(ve, sem[f"mix3_{l}"], b, base[f"mix3_{l}"])
                    ve.scalar_tensor_tensor(out=y_mix2[:, k, :], in0=y_pair[:, b % 2, 1, k],
                                            scalar=weight[:, 1, b * KT + k:b * KT + k + 1], in1=y_mix[:, k, :],
                                            op0=ALU.mult, op1=ALU.add).then_inc(sem[f"mixed{l}"], 1)

            def mix_into_x(l, b):
                ve.wait_ge(sem[f"mix3_{l}"], base[f"mix3_{l}"] + b + 1)
                xs = X[:, b * KT:(b + 1) * KT, :]
                ve.tensor_tensor(xs, xs, y_mix3[:, :, :], ALU.add).then_inc(sem[f"mixed_x{l}"], 1)

            routing(0)
            expert_tiles(0)

            def max_of(b, g):
                ve.wait_ge(sem["scores_max"], 12 * b + g + 1)
                if g == 0:
                    at_least(ve, sem["max_parts"], 2 * b)
                ps = pair[0][:, (g % 2) * 512:(g % 2 + 1) * 512]
                if g < 4:
                    ve.tensor_reduce(row_max[:, 0, 4 * g:4 * g + 4], ps.rearrange("p (h s) -> p h s", h=4), AX_X, ALU.max)\
                      .then_inc(sem["maxed"], 1)
                else:
                    ve.tensor_reduce(row_max[:, 1, 2 * (g - 4):2 * (g - 4) + 2], ps.rearrange("p (h s) -> p h s", h=2), AX_X,
                                     ALU.max).then_inc(sem["maxed"], 1)

            def split_max(b):
                ve.wait_ge(sem["maxed"], 12 * (b + 1))
                at_least(ve, sem["max_t_ps"], cnt(b - 2))
                hi, lo = max_parts[:, b % 2, :, 0:H], max_parts[:, b % 2, :, H:2 * H]
                ve.tensor_scalar(hi, row_max[:, :, :], -1.0, None, ALU.mult).then_inc(sem["max_hi"], 1)
                ve.wait_ge(sem["max_hi"], b + 1)
                ve.scalar_tensor_tensor(out=lo, in0=row_max[:, :, :], scalar=-1.0, in1=hi, op0=ALU.mult, op1=ALU.subtract)\
                  .then_inc(sem["max_parts"], 2)

            def rest_of_qk(b):
                ve.wait_ge(sem["part1_1"], base["part1_1"] + b + 1)
                at_least(ve, sem["part3_1"], cnt(b - 2), base["part3_1"])
                ve.tensor_tensor(rest[:, b % 2, :], P0[:, :], parts[:, b % 2, 0, :], ALU.subtract).then_inc(sem["rest1_1"], 1)

            for s in STEPS[1]:
                b = stages(1, s)
                a, m, v, z, y, n = b["front"], b["scores"], b["dens"], b["back"], b["route"], b["next"]
                if s == -1:
                    mix(0, 0)
                    mix_into_x(0, 0)
                    ve.wait_ge(sem["mixed_x0"], 1)
                    norm_stats(1, 0, 0)
                    mix(0, 1)
                    norm_apply(1, 0, 0)
                    mix_into_x(0, 1)
                for g in range(12):
                    if m is not None:
                        max_of(m, g)
                    if g == 0 and n is not None and n > 0:
                        ve.wait_ge(sem["mixed_x0"], n + 1)
                        norm_stats(1, 0, n)
                    if g == 1 and y is not None:
                        norm_apply(1, 1, y)
                    if g == 3 and a is not None:
                        rest_of_qk(a)
                    if g == 4 and n is not None and n > 0:
                        norm_apply(1, 0, n)
                    if g == 9 and v is not None:
                        ve.wait_ge(sem[f"y_in1_{v % 2}"], base[f"y_in1_{v % 2}"] + 32 * (v // 2 + 1))
                        at_least(ve, sem[f"den_out{v % 2}"], 16 * (v // 2))
                        ve.reciprocal(den_inv[:, v % 2, :], den[:, v % 2, :]).then_inc(sem["den_inv"], 1)
                    if g == 6 and 0 <= s and s + 2 < NB:
                        mix(0, s + 2)
                    if g == 8 and z is not None:
                        add_to_x(1, z)
                        ve.wait_ge(sem["x_mid1"], base["x_mid1"] + z + 1)
                        norm_stats(1, 1, z)
                    if g == 9 and 0 <= s and s + 2 < NB:
                        mix_into_x(0, s + 2)
                    if g == 11 and y is not None:
                        read_logits(1, y)
                if m is not None:
                    split_max(m)

            routing(1)
            expert_tiles(1)
            for b in range(NB + 2):
                if b < NB:
                    for k in range(KT):
                        i = b * KT + k
                        ve.wait_ge(sem["mix1_1"], base["mix1_1"] + i + 1)
                        ve.scalar_tensor_tensor(out=last_mix2[:, i, :], in0=last_pair[:, 1, i, :], scalar=weight[:, 1, i:i + 1],
                                                in1=last_mix1[:, i, :], op0=ALU.mult, op1=ALU.add).then_inc(sem["mixed1"], 1)
                if b >= 2:
                    xs = slice((b - 2) * KT, (b - 1) * KT)
                    ve.wait_ge(sem["mix3_1"], base["mix3_1"] + b - 1)
                    ve.tensor_tensor(X[:, xs, :], X[:, xs, :], last_mix3[:, xs, :], ALU.add).then_inc(sem["mixed_x1"], 1)

        @block.scalar
        def _(act):
            def modulate(l, b):
                act.wait_ge(sem[f"x_t_ps{l}"], base[f"x_t_ps{l}"] + b + 1)
                at_least(act, sem[f"v_ps{l}"], cnt(b - 2), base[f"v_ps{l}"])
                if b == 0 and l == 0:
                    act.wait_ge(sem["mod_t"], 8)
                act.activation(h_t[:, b % 2], P0[:, 0:T], ACT.Identity, bias=mod_t[:, l, 0, b:b + 1],
                               scale=mod_t[:, l, 1, b:b + 1]).then_inc(sem[f"h_t{l}"], 1)

            def keep_y(b, ch):
                act.copy(y_pad[:, b % 2, :].rearrange("p (g c t) -> p c g t", g=4, c=KT)[:, ch],
                         Y0[:, :].rearrange("p (g t) -> p g t", g=4)).then_inc(sem["y_pad0"], 1)

            def first_part(l, b):
                at_least(act, sem[f"parts_out{l}_{b % 2}"], 16 * (b // 2), base[f"parts_out{l}_{b % 2}"])
                if l == 0:
                    act.wait_ge(sem["qk0"], b + 1)
                    act.copy(parts[:, b % 2, 0, :], qk[:, b % 3, :]).then_inc(sem["part1_0"], 1)
                else:
                    act.wait_ge(sem["qk_ps1"], base["qk_ps1"] + b + 1)
                    act.copy(parts[:, b % 2, 0, :], P0[:, :]).then_inc(sem["part1_1"], 1)

            def second_part(l, b):
                act.wait_ge(sem[f"rest1_{l}"], base[f"rest1_{l}"] + b + 1)
                act.copy(parts[:, b % 2, 1, :], rest[:, b % 2, :]).then_inc(sem[f"part2_{l}"], 1)

            def keep_h2(l, b):
                act.wait_ge(sem[f"h2_ps{l}"], base[f"h2_ps{l}"] + b + 1)
                at_least(act, sem[f"logits_ps{l}"], b, base[f"logits_ps{l}"])
                act.copy(h2_t[:, :], P0[:, 0:T]).then_inc(sem[f"h2_t{l}"], 1)

            for l in range(2):
                act.dma_start(c_t[:, l, :], ins[f"c_t{l}"]).then_inc(sem["c_in"], 16)
            act.wait_ge(sem["c_in"], 32)
            act.activation(sc_t[:, :, :], c_t[:, :, :], ACT.Silu).then_inc(sem["silu_c"], 1)

            act.dma_start(B1[:, :, :], ins["b1"]).then_inc(sem["experts0_in"], 16)

            def load_expert(l, e):
                first, second_w = (("w1", "w2"), ("gate_w", "down_w"))[l]
                act.dma_start(W1[:, e, :], ins[first][e]).then_inc(sem[f"experts{l}_in"], 16)
                act.dma_start(W2[:, e, :, :], ins[second_w][e].rearrange("(k p) c -> p k c", p=P))\
                   .then_inc(sem[f"experts{l}_in"], 16)
                if l == 0:
                    act.dma_start(W_up[:, e, :], ins["up_w"][e]).then_inc(sem["up_in"], 16)

            for s in STEPS[0]:
                b = stages(0, s)
                a, m, z, y = b["front"], b["scores"], b["back"], b["route"]
                if a is not None:
                    modulate(0, a)
                if s == 0:
                    act.wait_ge(sem["mod_rows_ps"], 1)
                    act.copy(mod_rows[:, :], P1[:, 0:P]).then_inc(sem["mod_rows"], 1)
                if m is not None:
                    act.wait_ge(sem["k_tok_ps"], m + 1)
                    at_least(act, sem["state_ps"], m)
                    act.copy(k_tok[:, :], P1[:, 0:P]).then_inc(sem["k_tok"], 1)
                if z is not None:
                    act.wait_ge(sem["gn_avg_ps"], z + 1)
                    at_least(act, sem["gn_b"], z)
                    act.copy(gn_avg[:, :], P1[:, 0:2]).then_inc(sem["gn_avg"], 1)
                if a is not None:
                    first_part(0, a)
                    act.wait_ge(sem["v_ps0"], a + 1)
                    if a == 0:
                        act.wait_ge(sem["v_clear"], 1)
                    at_least(act, sem["pv_0"], 4 * cnt(a - 5))
                    act.copy(V[:, a % 5, :, 0:C], P2[:, 0:T].rearrange("p (k c) -> p k c", k=KT)).then_inc(sem["v_0"], 1)
                    at_least(act, sem["o_t0"], cnt(a - 6))
                    act.activation(sgate[:, a % 6, :], P2[:, T:2 * T], ACT.Silu).then_inc(sem["gated0"], 1)
                if m is not None:
                    act.wait_ge(sem["pv_0"], 4 * m + 2)
                    at_least(act, sem[f"y_out0_{m % 2}"], 64 * (m // 2))
                    keep_y(m, 0)
                    act.wait_ge(sem["y_state_ps"], m + 1)
                    at_least(act, sem["y_sum"], cnt(m - 3))
                    act.copy(y_state[:, m % 3, :], P2[:, 0:P]).then_inc(sem["y_state"], 1)
                if a is not None:
                    second_part(0, a)
                if m is not None:
                    act.wait_ge(sem["pv_0"], 4 * m + 4)
                    keep_y(m, 1)
                if y is not None:
                    keep_h2(0, y)
                if a is not None:
                    load_expert(0, a)

            def expert_tiles(l):
                def keep_x_t(n, r):
                    act.wait_ge(sem[f"x_t_e_ps{l}"], base[f"x_t_e_ps{l}"] + n + 1)
                    act.copy(x_t[:, r % 2, :], P0[:, 0:P]).then_inc(sem[f"x_t{l}"], 1)

                def copy_first(n, r, e):
                    if l == 0:
                        act.copy(b_now[:, r, :], B1[:, bass.ds(e, 1), :].rearrange("p e k -> p (e k)")).then_inc(sem["w_now0"], 1)
                        act.copy(w_now[:, r % 2, 0, :], W1[:, bass.ds(e, 1), :].rearrange("p e f -> p (e f)"))\
                           .then_inc(sem["w_now0"], 1)
                    else:
                        act.copy(w_now[:, r % 2, 0, :], W1[:, bass.ds(e, 1), :].rearrange("p e f -> p (e f)"))\
                           .then_inc(sem["w_now1"], 1)
                        act.copy(w_now[:, r % 2, 1, :], W_up[:, bass.ds(e, 1), :].rearrange("p e f -> p (e f)"))\
                           .then_inc(sem["w_now1"], 1)

                def expert_of(n):
                    return act.value_load(tile_exp[0:1, bass.ds(n, 1)], min_val=0, max_val=E - 1)

                def step(n, r, uses):
                    e = expert_of(n + 2) if exists(n + 2) else None
                    if l == 0:
                        act.wait_ge(sem["w_now0"], 2 * n + 2)
                        act.wait_ge(sem["hidden_ps0"], n + 1)
                        at_least(act, sem["y_ps0"], n - 1)
                        for k in range(FK // 2, FK):
                            i = act.activation(hid_t[:, r % 2, k * P:(k + 1) * P], UP[r % 2][:, k * P:(k + 1) * P],
                                               ACT.Relu, bias=b_now[:, r, k:k + 1])
                        i.then_inc(sem["act_hid0"], 1)
                    else:
                        at_least(act, sem["hid_t1"], n - 1, base["hid_t1"])
                        act.wait_ge(sem["hidden_ps1"], base["hidden_ps1"] + n + 1)
                        act.activation(hid_g[:, r % 2, :], HIDDEN[r % 2], ACT.Silu).then_inc(sem["act_hid1"], 1)
                    if exists(n + 1):
                        keep_x_t(n + 1, r + 1)
                    if exists(n + 2):
                        copy_first(n + 2, (r + 2) % RING, e)

                act.wait_ge(sem[f"tile_exp{l}"], base[f"tile_exp{l}"] + 1)
                act.wait_ge(sem[f"experts{l}_in"], 16 * (2 * E + 2 * (l == 0)))
                if l == 1:
                    act.wait_ge(sem["up_in"], 16 * E)
                for n in range(2):
                    copy_first(n, n, expert_of(n))
                    if n == 0:
                        keep_x_t(0, 0)
                all_tiles(act, step)

            def gap_exp_of(l):
                act.wait_ge(sem[f"gap{l}"], base[f"gap{l}"] + 1)
                act.activation(gap_exp[:, :], gap[:, :], ACT.Exp).then_inc(sem[f"gap_exp{l}"], 1)

            def mix1(l, b):
                act.wait_ge(sem[f"pair_in{l}_{b % 2}"], base[f"pair_in{l}_{b % 2}"] + 32 * (b // 2 + 1))
                act.wait_ge(sem[f"weights{l}"], base[f"weights{l}"] + 1)
                for k in range(KT):
                    at_least(act, sem[f"mixed{l}"], 2 * (b - 1) + k + 1, base[f"mixed{l}"])
                    act.activation(y_mix[:, k, :], y_pair[:, b % 2, 0, k], ACT.Copy, scale=weight[:, 0, b * KT + k:b * KT + k + 1])\
                       .then_inc(sem[f"mix1_{l}"], 1)

            for r in range(2):
                act.wait_ge(sem[f"y_out0_{r}"], 64 * (NB // 2))
            b2 = ins["b2"].rearrange("(a e) c -> a (e c)", a=1)
            act.dma_start(B2[:, :, :].rearrange("p e c -> p (e c)"), b2.broadcast_to((P, E * C))).then_inc(sem["experts0_in"], 16)
            gap_exp_of(0)
            expert_tiles(0)
            act.wait_ge(sem["y_ps0"], TILES)
            act.wait_ge(sem["w_now0"], 2 * TILES)
            act.wait_ge(sem["w2_now0"], 2 * TILES)

            for s in STEPS[1]:
                b = stages(1, s)
                a, w, y, mx = b["front"], b["probs"], b["route"], b["max_rows"]

                def keep_v():
                    act.wait_ge(sem["v_ps1"], base["v_ps1"] + a + 1)
                    if a == 0:
                        act.wait_ge(sem["v_ones"], 1)
                    at_least(act, sem["pv_1"], 12 * cnt(a - 5), base["pv_1"])
                    act.copy(V[:, a % 5, :, 0:9 * H].rearrange("p k (h e) -> p k h e", e=9)[:, :, :, 0:HD],
                             P1[:, 0:T].rearrange("p (k h d) -> p k h d", k=KT, d=HD)).then_inc(sem["v_1"], 1)

                if s == -1:
                    mix1(0, 0)
                    mix1(0, 1)
                if 0 <= s - 1 < E:
                    load_expert(1, s - 1)
                for g in range(12):
                    if w is not None:
                        act.wait_ge(sem["scores_exp"], 12 * w + g + 1)
                        at_least(act, sem["pv_1"], 12 * w + g - 3, base["pv_1"])
                        act.activation(probs[:, g % 4, :], half_bank(g), ACT.Exp, scale=float(HD) ** -0.5)\
                           .then_inc(sem["exped"], 1)
                    if g == 0 and a is not None:
                        modulate(1, a)
                    if g == 1 and mx is not None:
                        act.wait_ge(sem["max_t_ps"], mx + 1)
                        at_least(act, sem[f"max_out{mx % 2}"], 16 * (mx // 2))
                        act.copy(max_t[0:2 * H, mx % 2, :], P1[0:2 * H, 0:P].bitcast(BF16)).then_inc(sem["max_t"], 1)
                    if g == 2 and a is not None:
                        first_part(1, a)
                    if g == 3 and a is not None:
                        keep_v()
                    if g == 4 and a is not None:
                        second_part(1, a)
                    if g == 5 and 0 <= s and s + 2 < NB:
                        mix1(0, s + 2)
                    if g == 8 and w is not None:
                        act.wait_ge(sem["pv_1"], base["pv_1"] + 12 * w + 6)
                        at_least(act, sem[f"y_out1_{w % 2}"], 64 * (w // 2), base[f"y_out1_{w % 2}"])
                        act.copy(y_pad[:, w % 2, 0:512], Y0[:, :]).then_inc(sem["y_pad1"], 1)
                    if g == 9 and y is not None:
                        keep_h2(1, y)
                if w is not None:
                    act.wait_ge(sem["pv_1"], base["pv_1"] + 12 * w + 12)
                    act.copy(y_pad[:, w % 2, 512:1024], P2[:, :]).then_inc(sem["y_pad1"], 1)

            gap_exp_of(1)
            expert_tiles(1)
            act.wait_ge(sem["weights1"], base["weights1"] + 1)
            for i in range(NT):
                if i % (NT // LAST_LOADS) == 0:
                    act.wait_ge(sem[f"last_in{i // (NT // LAST_LOADS)}"], 32)
                act.activation(last_mix1[:, i, :], last_pair[:, 0, i, :], ACT.Copy, scale=weight[:, 0, i:i + 1])\
                   .then_inc(sem["mix1_1"], 1)

        @block.gpsimd
        def _(gp):
            def inverse_root(l, which, b):
                gp.wait_ge(sem[f"var{l}_{which}"], base[f"var{l}_{which}"] + b + 1)
                gp.tensor_tensor(rstd[:, which, :], var_eps[:, which, :], half_neg[:, :], ALU.pow)\
                  .then_inc(sem[f"rstd{l}_{which}"], 1)

            def modulate_rows(l, b):
                gp.wait_ge(sem[f"xh{l}_1"], base[f"xh{l}_1"] + 2 * (b + 1))
                gp.wait_ge(sem[f"mod_bc{b % 4}_{l}"], base[f"mod_bc{b % 4}_{l}"] + 16 * (b // 4 + 1))
                wide = lambda k: mod_bc[:, b % 4, k * C:(k + 1) * C].unsqueeze(1).broadcast_to((P, KT, C))
                at_least(gp, sem[f"h_stored{l}_{b % 2}"], 16 * (b // 2), base[f"h_stored{l}_{b % 2}"])
                at_least(gp, sem[f"h2_ps{l}"], cnt(b - 2), base[f"h2_ps{l}"])
                gp.tensor_tensor(h_tmp[:, :, :], xh[:, 1, b % 2], wide(2), ALU.mult).then_inc(sem[f"h_mul{l}"], 1)
                gp.wait_ge(sem[f"h_mul{l}"], base[f"h_mul{l}"] + b + 1)
                gp.tensor_tensor(h_tok[:, b % 2], h_tmp[:, :, :], wide(1), ALU.add).then_inc(sem[f"h_tok{l}"], 2)

            def scale_w_out(l, b):
                if b == 0 and l == 0:
                    gp.wait_ge(sem["late_in"], 16 * 5)
                if b == 0 and l == 1:
                    gp.wait_ge(sem["w1_in"], 48)
                gp.wait_ge(sem[f"mod_bc{b % 4}_{l}"], base[f"mod_bc{b % 4}_{l}"] + 16 * (b // 4 + 1))
                at_least(gp, sem[f"out_ps{l}"], cnt(b - 2), base[f"out_ps{l}"])
                gp.tensor_tensor(w_out[:, b % 2, :], w_proj[:, :], mod_bc[:, b % 4, 0:C], ALU.mult).then_inc(sem[f"w_out{l}"], 1)

            def rest0(b):
                gp.wait_ge(sem["part1_0"], b + 1)
                gp.tensor_tensor(rest[:, b % 2, :], qk[:, b % 3, :], parts[:, b % 2, 0, :], ALU.subtract).then_inc(sem["rest1_0"], 1)

            def third_part(l, b):
                gp.wait_ge(sem[f"part2_{l}"], base[f"part2_{l}"] + b + 1)
                gp.tensor_tensor(parts[:, b % 2, 2, :], rest[:, b % 2, :], parts[:, b % 2, 1, :], ALU.subtract)\
                  .then_inc(sem[f"part3_{l}"], 1)

            gp.wait_ge(sem["first_memsets"], 3)
            inverse_root(0, 0, 0)
            gp.memset(stack_k[:, 0, :].bitcast(F32), TWO_ONES).then_inc(sem["stack_k_set"], 1)
            gp.memset(ones_b[:, :], 1.0).then_inc(sem["bf16_consts"], 1)
            gp.wait_ge(sem["consts_in"], 16)
            for dst, name in ((before_b, "before"), (iota_b, "iota"), (ident_b, "ident"), (tile_id_b, "tile_id")):
                gp.tensor_copy(dst[:, :], const(name)).then_inc(sem["bf16_consts"], 1)
            gp.memset(neg_mask[:, :], 0.0).then_inc(sem["neg_mask"], 1)
            gp.wait_ge(sem["neg_mask"], 1)
            gp.affine_select(out=neg_mask[:, :], in_=neg_mask[:, :], compare_op=ALU.is_ge, fill=-1e30, base=0,
                             pattern=[[-1, P]], channel_multiplier=1).then_inc(sem["neg_mask"], 1)

            def set_stack(r):
                gp.memset(stack_k[:, r, :].bitcast(F32), TWO_ONES).then_inc(sem["stack_k_set"], 1)
                gp.memset(stack_q[:, r, :].bitcast(F32), 0.0).then_inc(sem["stack_q_set"], 1)

            for s in STEPS[0]:
                b = stages(0, s)
                a, m, z, y, n = b["front"], b["scores"], b["back"], b["route"], b["next"]
                if z is not None:
                    scale_w_out(0, z)
                    gp.wait_ge(sem["gn_var"], z + 1)
                    gp.tensor_tensor(gn_rstd[:, :], gn_ve[:, 1:2], half_neg[:, 0:1], ALU.pow).then_inc(sem["gn_rstd"], 1)
                if a is not None:
                    gp.wait_ge(sem["rot_a"], a + 1)
                    gp.wait_ge(sem["rot_b"], a + 1)
                    at_least(gp, sem["y_state_ps"], cnt(a - 3))
                    gp.tensor_tensor(qk[:, a % 3, :], rot[:, 0], rot[:, 1], ALU.add).then_inc(sem["qk0"], 1)
                if z is not None:
                    gp.wait_ge(sem["y_n"], z + 1)
                    gp.wait_ge(sem["gated0"], z + 1)
                    at_least(gp, sem["out_ps0"], cnt(z - 2))
                    gp.tensor_tensor(o_t[:, z % 2, :], y_n[:, :], sgate[:, z % 6, :], ALU.mult).then_inc(sem["o_t0"], 1)
                if n is not None and n > 0:
                    inverse_root(0, 0, n)
                if a is not None:
                    rest0(a)
                if y is not None:
                    modulate_rows(0, y)
                if a is not None:
                    gp.wait_ge(sem["rest1_0"], a + 1)
                    third_part(0, a)
                if 0 <= s < 2:
                    set_stack(s + 1)
                if z is not None:
                    inverse_root(0, 1, z)

            def expert_tiles(l):
                def gather(n):
                    at_least(gp, sem[f"x_t_e_ps{l}"], n - RING + 1, base[f"x_t_e_ps{l}"])
                    gp.indirect_dma_start(out=x_rows[:, n % RING, :], out_offset=None, in_=h_d[l],
                                          in_offset=bass.IndirectOffsetOnAxis(ap=src_row[:, n:n + 1], axis=0))\
                      .then_inc(sem[f"gathered{n % RING}_{l}"], 16)

                def scatter(n):
                    gp.wait_ge(sem[f"y_rows{l}"], base[f"y_rows{l}"] + n + 1)
                    gp.indirect_dma_start(out=ye_d[l], out_offset=bass.IndirectOffsetOnAxis(ap=dst_row[:, n:n + 1], axis=0),
                                          in_=y_rows[:, n % RING, :], in_offset=None)\
                      .then_inc(sem[f"scattered{n % RING}_{l}"], 16)

                gp.wait_ge(sem[f"gap{l}"], base[f"gap{l}"] + 4)
                gp.tensor_tensor(hot_vals[:, :, 1, :], hot_tile[:, :, :],
                                 tile_id_b[:, :].unsqueeze(2).broadcast_to((P, CHOICES * NT, TILES)), ALU.mult)\
                  .then_inc(sem[f"hot_vals{l}"], 1)
                gp.wait_ge(sem[f"src_row{l}"], base[f"src_row{l}"] + 1)
                for r in range(2):
                    gp.wait_ge(sem[f"h_stored{l}_{r}"], base[f"h_stored{l}_{r}"] + 16 * (NB // 2))
                for n in range(RING):
                    gather(n)
                gp.wait_ge(sem[f"dst_row{l}"], base[f"dst_row{l}"] + 1)
                for n in range(TILES):
                    if n + RING < TILES:
                        gather(n + RING)
                    scatter(n)

            def mix3(l, b):
                if b == 0:
                    gp.wait_ge(sem[f"gb_bc{l}"], base[f"gb_bc{l}"] + 16)
                gp.wait_ge(sem[f"mixed{l}"], base[f"mixed{l}"] + 2 * (b + 1))
                at_least(gp, sem[f"mixed_x{l}"], b, base[f"mixed_x{l}"])
                gp.tensor_tensor(y_mix3[:, :, :], y_mix2[:, :, :], gb_bc[:, b, :].unsqueeze(1).broadcast_to((P, KT, C)),
                                 ALU.mult).then_inc(sem[f"mix3_{l}"], 1)

            expert_tiles(0)
            gp.memset(V[:, :, :, :], 1.0).then_inc(sem["v_ones"], 1)

            for s in STEPS[1]:
                b = stages(1, s)
                a, w, z, y, n = b["front"], b["probs"], b["back"], b["route"], b["next"]
                if s == -1:
                    mix3(0, 0)
                    inverse_root(1, 0, 0)
                    mix3(0, 1)
                if s == 1:
                    set_stack(STACKS - 1)
                for g in range(12):
                    if w is not None:
                        gp.wait_ge(sem["exped"], 12 * w + g + 1)
                        _, s0, t0, cols = exp_cells(g)[0]
                        cells = probs[:, g % 4, :].rearrange("p (n t) -> p n t", t=cols)[:, :, 0:P]
                        gp.affine_select(out=cells, in_=cells, compare_op=ALU.is_ge, fill=0.0, base=0,
                                         pattern=[[0, 512 // cols], [1, P]], channel_multiplier=-1)\
                          .then_inc(sem["probs_causal"], 1)
                    if g == 1 and z is not None:
                        scale_w_out(1, z)
                    if g == 2 and n is not None and n > 0:
                        inverse_root(1, 0, n)
                    if g == 3 and z is not None:
                        gp.wait_ge(sem[f"den_in{z % 2}"], 16 * (z // 2 + 1))
                        gp.wait_ge(sem[f"y_in1_{z % 2}"], base[f"y_in1_{z % 2}"] + 32 * (z // 2 + 1))
                        at_least(gp, sem["out_ps1"], cnt(z - 2), base["out_ps1"])
                        gp.tensor_tensor(o_t[:, z % 2, :], y_t[:, z % 3, :], den_bc[:, z % 2, :], ALU.mult)\
                          .then_inc(sem["o_t1"], 1)
                    if g == 5 and a is not None:
                        third_part(1, a)
                    if g == 6 and y is not None:
                        modulate_rows(1, y)
                    if g == 8 and 0 <= s and s + 2 < NB:
                        mix3(0, s + 2)
                    if g == 10 and z is not None:
                        inverse_root(1, 1, z)

            expert_tiles(1)
            gp.wait_ge(sem["gb_bc1"], base["gb_bc1"] + 16)
            for b in range(NB):
                rows = slice(b * KT, (b + 1) * KT)
                gp.wait_ge(sem["mixed1"], base["mixed1"] + 2 * (b + 1))
                gp.tensor_tensor(last_mix3[:, rows, :], last_mix2[:, rows, :],
                                 gb_bc[:, b, :].unsqueeze(1).broadcast_to((P, KT, C)), ALU.mult).then_inc(sem["mix3_1"], 1)


def kernel(**inputs):
    import concourse.bacc as bacc
    from concourse.bass_utils import run_bass_kernel_spmd

    a = {k: np.asarray(v) for k, v in inputs.items()}
    pair_swap = np.arange(C) ^ 1
    w_qkv = a["L0_attn_w_qkv"]
    q_w, k_w, v_w = w_qkv[0:C], w_qkv[C:2 * C], w_qkv[2 * C:]
    order, swapped = D_MAJOR, pair_swap[D_MAJOR]
    consts, rotary = shape_constants()
    arrays = {
        "x": a["L0_attn_x"],
        "consts": consts, "rotary": rotary,
        "c_t0": a["L0_c"].T, "c_t1": a["L1_c"].T,
        "wmod0": a["L0_wmod"], "wmod1": a["L1_wmod"],
        "w_qk0": np.concatenate([q_w[order].T, k_w[order].T], 1),
        "w_qks": np.concatenate([q_w[swapped].T, k_w[swapped].T], 1),
        "w_v0": v_w.T,
        "w_gate": a["L0_attn_w_gated"][order].T,
        "w_proj0": a["L0_attn_w_proj"].T[order],
        "gn": np.stack([a["L0_attn_gn_weight"][order], a["L0_attn_gn_bias"][order]], 1),
        "router_w0": a["L0_ffn_Wg"],
        "w1": a["L0_ffn_W1"], "b1": a["L0_ffn_b1"].reshape(E, FK, P).transpose(2, 0, 1), "w2": a["L0_ffn_W2"], "b2": a["L0_ffn_b2"],
        "w_qk1": np.concatenate([a["L1_attn_Wq"][order].T, a["L1_attn_Wk"][order].T], 1),
        "w_v1": a["L1_attn_Wv"].T,
        "w_proj1": a["L1_attn_Wo"].T[order],
        "router_w1": a["L1_ffn_router_w"].T, "router_b": a["L1_ffn_router_b"],
        "gate_w": a["L1_ffn_gate_w"].transpose(0, 2, 1),
        "up_w": a["L1_ffn_up_w"].transpose(0, 2, 1),
        "down_w": a["L1_ffn_down_w"].transpose(0, 2, 1),
    }
    arrays = {k: np.ascontiguousarray(v) for k, v in arrays.items()}
    nc = bacc.Bacc("TRN2", target_bir_lowering=False, num_devices=1)
    ins = {k: nc.dram_tensor(f"in_{k}", v.shape, mybir.dt.from_np(v.dtype), kind="ExternalInput").ap()
           for k, v in arrays.items()}
    out = nc.dram_tensor("out_x", (NB, T, C), F32, kind="ExternalOutput").ap()
    adaln_layers(nc, ins, out)
    r = run_bass_kernel_spmd(nc, [{f"in_{k}": v for k, v in arrays.items()}], core_ids=[0])
    return r.results[0]["out_x"]
```
